# Optimizing a Trainium2 kernel written in Bass

```python
import numpy as np
import jax
import jax.numpy as jnp

def _softmax(x, axis=-1):
    return jax.nn.softmax(x, axis=axis)

def _gelu(x):
    return jax.nn.gelu(x, approximate=True)

def _silu(x):
    return jax.nn.silu(x)

def _sigmoid(x):
    return jax.nn.sigmoid(x)

def _layernorm(x, axis=-1, eps=1e-05):
    m = jnp.mean(x, axis=axis, keepdims=True)
    v = jnp.var(x, axis=axis, keepdims=True)
    return (x - m) / jnp.sqrt(v + eps)

def _scatter_add(tgt, idx, src, axis=0):
    return tgt.at[idx].add(src)

def _segment_sum(src, seg, n):
    return jax.ops.segment_sum(src, seg, n)
kernel_name = 'mk_prb_d1_jaxref_r4_c1e6ea'

def setup_inputs(seed: int=0):
    np.random.seed(seed)
    _w = jnp.asarray

    def _L0_attn_setup():
        import jax, jax.numpy as jnp
        import numpy as np
        B, N, H = (1, 1024, 512)
        NH, HD = (16, H // 16)
        WINDOW = 1024
        EPS = 1e-06
        THETA = 10000.0
        NEG = -1e+30

        def rmsnorm(x, w):
            var = jnp.mean(jnp.square(x.astype(jnp.float32)), axis=-1, keepdims=True)
            return (x * jax.lax.rsqrt(var + EPS)).astype(w.dtype) * w

        def rotate_half(x):
            x1, x2 = (x[..., :x.shape[-1] // 2], x[..., x.shape[-1] // 2:])
            return jnp.concatenate((-x2, x1), axis=-1)
        key = jax.random.key(seed)
        k1, k2, k3 = jax.random.split(key, 3)
        x = jax.random.normal(k1, (B, N, H), dtype=jnp.float32)
        w_qkv = jax.random.normal(k2, (H, 3 * H), dtype=jnp.float32) * (1.0 / np.sqrt(H))
        w_out = jax.random.normal(k3, (H, H), dtype=jnp.float32) * (1.0 / np.sqrt(H))
        q_gamma = jnp.ones((HD,), dtype=jnp.float32)
        k_gamma = jnp.ones((HD,), dtype=jnp.float32)
        return {'x': x, 'w_qkv': w_qkv, 'w_out': w_out, 'q_gamma': q_gamma, 'k_gamma': k_gamma}
    _L0_attn_in = _L0_attn_setup()

    def _L0_ffn_setup():
        import jax, jax.numpy as jnp
        import numpy as np
        CAPACITY = 0.125
        HEAD_DIM = 128
        N_HEADS = 16
        N_KV_HEADS = 8
        ROPE_THETA = 10000.0
        EPS = 1e-06

        def _rms_norm(x, w):
            return x * jax.lax.rsqrt(jnp.mean(x * x, axis=-1, keepdims=True) + EPS) * w

        def _rotate_half(t):
            h = t.shape[-1] // 2
            return jnp.concatenate([-t[..., h:], t[..., :h]], axis=-1)
        key = jax.random.key(seed)
        ks = jax.random.split(key, 12)
        B, T, D = (4, 1024, 512)
        I = 2048
        s = 0.02
        return {'hidden_states': jax.random.normal(ks[0], (B, T, D), jnp.float32), 'w_router': jax.random.normal(ks[1], (D,), jnp.float32) * s, 'wq': jax.random.normal(ks[2], (D, N_HEADS * HEAD_DIM), jnp.float32) * s, 'bq': jnp.zeros((N_HEADS * HEAD_DIM,), jnp.float32), 'wk': jax.random.normal(ks[3], (D, N_KV_HEADS * HEAD_DIM), jnp.float32) * s, 'bk': jnp.zeros((N_KV_HEADS * HEAD_DIM,), jnp.float32), 'wv': jax.random.normal(ks[4], (D, N_KV_HEADS * HEAD_DIM), jnp.float32) * s, 'bv': jnp.zeros((N_KV_HEADS * HEAD_DIM,), jnp.float32), 'wo': jax.random.normal(ks[5], (N_HEADS * HEAD_DIM, D), jnp.float32) * s, 'w_gate': jax.random.normal(ks[6], (D, I), jnp.float32) * s, 'w_up': jax.random.normal(ks[7], (D, I), jnp.float32) * s, 'w_down': jax.random.normal(ks[8], (I, D), jnp.float32) * s, 'ln1_w': jnp.ones((D,), jnp.float32), 'ln2_w': jnp.ones((D,), jnp.float32)}
    _L0_ffn_in = _L0_ffn_setup()
    _d = {'L0_attn_x': _L0_attn_in['x'], 'L0_attn_w_qkv': _L0_attn_in['w_qkv'], 'L0_attn_w_out': _L0_attn_in['w_out'], 'L0_attn_q_gamma': _L0_attn_in['q_gamma'], 'L0_attn_k_gamma': _L0_attn_in['k_gamma'], 'L0_ffn_w_router': _L0_ffn_in['w_router'], 'L0_ffn_wq': _L0_ffn_in['wq'], 'L0_ffn_bq': _L0_ffn_in['bq'], 'L0_ffn_wk': _L0_ffn_in['wk'], 'L0_ffn_bk': _L0_ffn_in['bk'], 'L0_ffn_wv': _L0_ffn_in['wv'], 'L0_ffn_bv': _L0_ffn_in['bv'], 'L0_ffn_wo': _L0_ffn_in['wo'], 'L0_ffn_w_gate': _L0_ffn_in['w_gate'], 'L0_ffn_w_up': _L0_ffn_in['w_up'], 'L0_ffn_w_down': _L0_ffn_in['w_down'], 'L0_ffn_ln1_w': _L0_ffn_in['ln1_w'], 'L0_ffn_ln2_w': _L0_ffn_in['ln2_w']}
    _x0 = _d['L0_attn_x']
    _d['L0_attn_x'] = jax.random.normal(jax.random.fold_in(jax.random.key(seed), 1), (4, 1024, 512), dtype=_x0.dtype)
    del _x0
    return _d

def reference(L0_attn_x, L0_attn_w_qkv, L0_attn_w_out, L0_attn_q_gamma, L0_attn_k_gamma, L0_ffn_w_router, L0_ffn_wq, L0_ffn_bq, L0_ffn_wk, L0_ffn_bk, L0_ffn_wv, L0_ffn_bv, L0_ffn_wo, L0_ffn_w_gate, L0_ffn_w_up, L0_ffn_w_down, L0_ffn_ln1_w, L0_ffn_ln2_w):

    def _L0_attn_ref(x, w_qkv, w_out, q_gamma, k_gamma):
        import jax, jax.numpy as jnp
        import numpy as np
        B, N, H = (1, 1024, 512)
        NH, HD = (16, H // 16)
        WINDOW = 1024
        EPS = 1e-06
        THETA = 10000.0
        NEG = -1e+30

        def rmsnorm(x, w):
            var = jnp.mean(jnp.square(x.astype(jnp.float32)), axis=-1, keepdims=True)
            return (x * jax.lax.rsqrt(var + EPS)).astype(w.dtype) * w

        def rotate_half(x):
            x1, x2 = (x[..., :x.shape[-1] // 2], x[..., x.shape[-1] // 2:])
            return jnp.concatenate((-x2, x1), axis=-1)
        b, n, _ = x.shape
        qkv = jnp.einsum('bnh,hm->bnm', x, w_qkv)
        q, k, v = jnp.split(qkv, 3, axis=-1)
        q = q.reshape(b, n, NH, HD).transpose(0, 2, 1, 3)
        k = k.reshape(b, n, NH, HD).transpose(0, 2, 1, 3)
        v = v.reshape(b, n, NH, HD).transpose(0, 2, 1, 3)
        q = rmsnorm(q, q_gamma)
        k = rmsnorm(k, k_gamma)
        inv_freq = 1.0 / THETA ** (jnp.arange(0, HD, 2, dtype=jnp.float32) / HD)
        t = jnp.arange(n, dtype=jnp.float32)
        freqs = t[:, None] * inv_freq[None, :]
        emb = jnp.concatenate((freqs, freqs), axis=-1)
        cos = jnp.cos(emb)[None, None, :, :]
        sin = jnp.sin(emb)[None, None, :, :]
        q = q * cos + rotate_half(q) * sin
        k = k * cos + rotate_half(k) * sin
        kv_len = k.shape[-2]
        q_idx = jnp.arange(n)[:, None] + (kv_len - n)
        k_idx = jnp.arange(kv_len)[None, :]
        mask = (q_idx >= k_idx) & (q_idx - k_idx <= WINDOW)
        scores = jnp.einsum('bhqd,bhkd->bhqk', q, k) / np.sqrt(HD)
        scores = jnp.where(mask[None, None, :, :], scores, NEG)
        attn = jax.nn.softmax(scores, axis=-1)
        out = jnp.einsum('bhqk,bhkd->bhqd', attn, v)
        out = out.transpose(0, 2, 1, 3).reshape(b, n, H)
        return jnp.einsum('bnh,hm->bnm', out, w_out)

    def _L0_ffn_ref(hidden_states, w_router, wq, bq, wk, bk, wv, bv, wo, w_gate, w_up, w_down, ln1_w, ln2_w):
        import jax, jax.numpy as jnp
        import numpy as np
        CAPACITY = 0.125
        HEAD_DIM = 128
        N_HEADS = 16
        N_KV_HEADS = 8
        ROPE_THETA = 10000.0
        EPS = 1e-06

        def _rms_norm(x, w):
            return x * jax.lax.rsqrt(jnp.mean(x * x, axis=-1, keepdims=True) + EPS) * w

        def _rotate_half(t):
            h = t.shape[-1] // 2
            return jnp.concatenate([-t[..., h:], t[..., :h]], axis=-1)
        B, T, D = hidden_states.shape
        k = max(1, int(T * CAPACITY))
        scores = jnp.einsum('btd,d->bt', hidden_states, w_router)
        _, idx = jax.lax.top_k(scores, k)
        idx = jnp.sort(idx, axis=-1)
        b = jnp.arange(B)[:, None]
        sel = hidden_states[b, idx]
        sel_scores = scores[b, idx]
        S = B * k
        x = sel.reshape(S, D)
        pos = idx.reshape(S)
        inv_freq = 1.0 / ROPE_THETA ** (jnp.arange(0, HEAD_DIM, 2, dtype=jnp.float32) / HEAD_DIM)
        ang = pos.astype(jnp.float32)[:, None] * inv_freq
        cos = jnp.concatenate([jnp.cos(ang), jnp.cos(ang)], axis=-1)[:, None, :]
        sin = jnp.concatenate([jnp.sin(ang), jnp.sin(ang)], axis=-1)[:, None, :]
        h = _rms_norm(x, ln1_w)
        q = (h @ wq + bq).reshape(S, N_HEADS, HEAD_DIM)
        kk = (h @ wk + bk).reshape(S, N_KV_HEADS, HEAD_DIM)
        v = (h @ wv + bv).reshape(S, N_KV_HEADS, HEAD_DIM)
        q = q * cos + _rotate_half(q) * sin
        kk = kk * cos + _rotate_half(kk) * sin
        rep = N_HEADS // N_KV_HEADS
        kk = jnp.repeat(kk, rep, axis=1)
        v = jnp.repeat(v, rep, axis=1)
        att = jnp.einsum('shd,thd->hst', q, kk) / np.sqrt(HEAD_DIM)
        causal = jnp.tril(jnp.ones((S, S), bool))
        att = jnp.where(causal[None], att, jnp.finfo(att.dtype).min)
        att = jax.nn.softmax(att, axis=-1)
        attn_out = jnp.einsum('hst,thd->shd', att, v).reshape(S, N_HEADS * HEAD_DIM) @ wo
        x1 = x + attn_out
        h2 = _rms_norm(x1, ln2_w)
        mlp = jax.nn.silu(h2 @ w_gate) * (h2 @ w_up) @ w_down
        processed = x1 + mlp
        gate = jax.nn.sigmoid(sel_scores).reshape(S, 1)
        gated = gate * processed + (1.0 - gate) * x
        output = hidden_states.at[b, idx].set(gated.reshape(B, k, D))
        return output
    x = L0_attn_x
    xn = _layernorm(x, axis=-1)
    x = x + _L0_attn_ref(xn, L0_attn_w_qkv, L0_attn_w_out, L0_attn_q_gamma, L0_attn_k_gamma) + _L0_ffn_ref(xn, L0_ffn_w_router, L0_ffn_wq, L0_ffn_bq, L0_ffn_wk, L0_ffn_bk, L0_ffn_wv, L0_ffn_bv, L0_ffn_wo, L0_ffn_w_gate, L0_ffn_w_up, L0_ffn_w_down, L0_ffn_ln1_w, L0_ffn_ln2_w)
    return x

_drawn_inputs = setup_inputs


def setup_inputs(seed=0):
    import zlib

    import numpy as np

    out = dict(_drawn_inputs(seed))
    spreads = {'L0_attn_q_gamma': (1.0, 0.6),
     'L0_attn_k_gamma': (1.0, 0.6),
     'L0_ffn_bq': (0.0, 0.8),
     'L0_ffn_bk': (0.0, 0.8),
     'L0_ffn_bv': (0.0, 0.674),
     'L0_ffn_ln1_w': (1.0, 0.6),
     'L0_ffn_ln2_w': (1.0, 0.6)}
    factors = {'L0_ffn_w_router': 3.109,
     'L0_ffn_wq': 8.0,
     'L0_ffn_wk': 8.0,
     'L0_ffn_wv': 7.216,
     'L0_ffn_wo': 4.197,
     'L0_ffn_w_gate': 4.464,
     'L0_ffn_w_up': 4.371,
     'L0_ffn_w_down': 4.383}
    for name, (base, spread) in spreads.items():
        noise = np.random.default_rng([zlib.crc32(name.encode()), seed]).standard_normal(out[name].shape)
        drawn = base * np.exp(spread * noise) if base else spread * noise
        out[name] = jnp.asarray(drawn.astype(out[name].dtype))
    for name, factor in factors.items():
        out[name] = (out[name] * factor).astype(out[name].dtype)
    return out
```

```python
import concourse.bass as bass
from concourse import mybir
from contextlib import ExitStack

P = 128
B, T, D = 4, 1024, 512
NT = T // P
KD = D // P
AH, AD = 16, 32
HG = P // AD
NG = AH // HG
FH, FKV, FD = 16, 8, 128
REP = FH // FKV
SEL = T // 8
S = B * SEL
ST = S // P
FI = 2048
NC = FI // P
CH = 512
LN_EPS, RMS_EPS = 1e-5, 1e-6
NP = AH // 2
STK = 3 * AD
RH = STK
SLOTS = 4
RING = 2
MASKED = -1e30

C_ID, C_ONE, C_MASK, C_TRI, C_IOTA, C_TIE = 0, 128, 256, 768, 896, 1024
TIE_W = 2 * T - P
C_W = C_TIE + TIE_W
FT_W = 4 * (FD // 2)


def build(nc, x_d, w_qkv_d, w_out_d, qg_d, kg_d, wr_d, wq_d, bq_d, wk_d, bk_d, wv_d, bv_d, wo_d,
          wg_d, wu_d, wd_d, ln1_d, ln2_d, const_d, rope_d, frope_d, out_d):
    f32, f32r, bf16 = mybir.dt.float32, mybir.dt.float32r, mybir.dt.bfloat16
    ALU, ACT, AX = mybir.AluOpType, mybir.ActivationFunctionType, mybir.AxisListType

    x_v = x_d.rearrange("b (t p) d -> b p t d", p=P)
    out_v = out_d.rearrange("b (t p) d -> b p t d", p=P)
    wqkv_v = w_qkv_d.rearrange("(k p) n -> p k n", p=P)
    wout_v = w_out_d.rearrange("(k p) n -> p k n", p=P)
    wq_v = wq_d.rearrange("(k p) (n c) -> n p k c", p=P, c=REP * FD)
    wk_v = wk_d.rearrange("(k p) (n c) -> n p k c", p=P, c=FD)
    wv_v = wv_d.rearrange("(k p) (n c) -> n p k c", p=P, c=FD)
    wo_v = wo_d.rearrange("(n r p) d -> n p r d", p=P, r=REP)
    wg_v = wg_d.rearrange("(k p) (n c) -> n p k c", p=P, c=P)
    wu_v = wu_d.rearrange("(k p) (n c) -> n p k c", p=P, c=P)
    wd_v = wd_d.rearrange("(n p) d -> n p d", p=P)

    ctx = ExitStack()
    with ctx:
        ARENA = 53200 - 8 * T
        arena = ctx.enter_context(nc.sbuf_tensor("arena", [P, ARENA], f32))
        qS = [ctx.enter_context(nc.sbuf_tensor(f"q_stack{i}", [P, 2, T], f32r)) for i in range(2)]
        kS = [ctx.enter_context(nc.sbuf_tensor(f"k_stack{i}", [P, 2, T], f32r)) for i in range(2)]
        psum = ctx.enter_context(nc.psum_tensor("psum", [P, 8, 512], f32))

        def sem(name):
            return ctx.enter_context(nc.semaphore(name))

        class Place:
            def __init__(self, at, end):
                self.at, self.end = at, end

            def f(self, *shape):
                n = 1
                for s in shape:
                    n *= s
                a = arena[:, self.at:self.at + n]
                self.at += n
                assert self.at <= self.end, (self.at, self.end)
                if len(shape) == 2:
                    a = a.rearrange("p (a b) -> p a b", b=shape[1])
                if len(shape) == 3:
                    a = a.rearrange("p (a b c) -> p a b c", b=shape[1], c=shape[2])
                return a

            def h(self, *shape):
                n = 1
                for s in shape:
                    n *= s
                a = arena[:, self.at:self.at + n // 2].bitcast(bf16)
                self.at += n // 2
                assert self.at <= self.end, (self.at, self.end)
                if len(shape) == 2:
                    a = a.rearrange("p (a b) -> p a b", b=shape[1])
                return a

        keep = Place(0, ARENA)
        ident = keep.f(P)
        ones = keep.f(P)
        mask = keep.f(CH)
        onehotT = keep.h(B, T)
        delta = keep.f(B, D)
        ln_mean = keep.f(B, NT)
        ln_rstd = keep.f(B, NT)
        half_neg = keep.f(32)
        w_qkv = keep.f(KD, 3 * D)
        cosG = keep.f(NT, 2, AD)
        sinG = keep.f(NT, 2, AD)
        w_out_at = keep.at
        w_out = keep.f(KD, D)
        rest = keep.at

        p1 = Place(w_out_at, ARENA)
        x_all = p1.f(B * NT, D)
        x_end = p1.at
        xsel = p1.f(ST, D)
        tabsel = p1.f(ST, FT_W + 1)
        rest2 = p1.at
        xn1 = p1.f(NT, D)
        tab = p1.f(NT, FT_W + 1)
        s_row = p1.f(T)
        onehot = p1.f(NT, P)
        junk1 = p1.h(2, T)
        wr_b = p1.f(D)
        cst1 = p1.f(C_W - C_TRI)
        tri = cst1[:, 0:P]
        iota1 = cst1[:, C_IOTA - C_TRI:C_IOTA - C_TRI + P]
        tie = cst1[:, C_TIE - C_TRI:]
        gam = p1.f(2, AD)
        rope_raw = p1.f(NT, 2 * AD)
        stats = p1.f(NT, 6)
        mv = p1.f(NT, 2)
        vpe = p1.f(NT)
        rstd1 = p1.f(NT)
        s_col = p1.f(NT)
        above = p1.f(NT)
        tied = p1.f(NT)
        rank = p1.f(NT)
        chosen = p1.f(NT)
        slot = p1.f(NT)

        p2 = Place(rest, x_end)
        hn = p2.f(ST, D)
        hT = p2.f(KD, S)
        x1 = p2.f(ST, D)
        mlp_at = p2.at
        prob2 = p2.f(REP * ST, S)
        probT2 = [p2.f(ST, S) for _ in range(REP)]
        mlp_end = p2.at
        p2 = Place(rest2, ARENA)
        cosT = p2.f(S)
        sinT = p2.f(S)
        bias_rows = prob2[:, 1, 0:FD]
        biasT = p2.f(FH + FKV)
        bv_b = p2.f(FKV * FD)
        ln1_b = prob2[:, 0, :]
        ln2_b = p2.f(D)
        wq_s = [p2.f(KD, REP * FD) for _ in range(2)]
        wk_s = [p2.f(KD, FD) for _ in range(2)]
        wv_s = [p2.f(KD, FD) for _ in range(2)]
        wo_s = [p2.f(REP, D) for _ in range(2)]
        raw = p2.f(2, S)
        rotd = p2.f(S)
        qT2 = p2.f(REP, S)
        kT2 = p2.f(S)
        v2 = p2.f(ST, FD)
        oT2 = p2.f(REP, S)
        ss2 = p2.f(ST)
        ms2 = p2.f(ST)
        rs2 = p2.f(ST)
        nmax2 = p2.f(REP * ST)
        den2 = p2.f(REP * ST)
        rden2 = p2.f(REP * ST)
        gate = p2.f(ST)
        egate = p2.f(ST)
        dgate = p2.f(ST)
        p2m = Place(mlp_at, mlp_end)
        wg_s = [p2m.f(KD, P) for _ in range(2)]
        wu_s = [p2m.f(KD, P) for _ in range(2)]
        wd_s = [p2m.f(D) for _ in range(2)]
        eg = p2m.f(2, S)
        sg = p2m.f(2, S)
        aT = p2m.f(2, S)
        zrow = p2m.f(D)

        p3 = Place(rest, ARENA)
        xn = p3.f(NT, D)
        xnT = p3.f(KD, T)
        probT = xnT.rearrange("p k n -> p (k n)").rearrange("p (s h n) -> p s h n", s=SLOTS, h=2)
        roped = p3.f(NT, 2 * D)
        v = p3.f(NT, D)
        oT = p3.f(NG, T)
        stack = p3.f(2, NT, 2 * STK)
        flat = stack.rearrange("p w t c -> p (w t c)")
        qk, sq, rot = (flat[:, i * 2 * D:(i + 1) * 2 * D] for i in range(3))
        xr = p3.f(RING, D)
        ohT = p3.f(T)
        top = p3.f(2, 2 * NT)
        top_rows = p3.f(P)
        ss3 = p3.f(2 * AH)
        ms3 = p3.f(2 * AH)
        rs3 = p3.f(2 * AH)
        past_top = p3.f(4)
        rden = p3.f(CH)
        mean_b = p3.f(NT)
        rstd_b = p3.f(NT)

        consts_in = sem("consts_in")
        consts1_in = sem("consts1_in")
        x_in = sem("x_in")
        late_in = sem("late_in")
        gam_ready = sem("gam_ready")
        rope_ready = sem("rope_ready")
        p1_stats = sem("p1_stats")
        p1_vpe = sem("p1_vpe")
        p1_rstd = sem("p1_rstd")
        p1_norm = sem("p1_norm")
        p1_score = sem("p1_score")
        p1_row_ps = sem("p1_row_ps")
        p1_row = sem("p1_row")
        p1_cnt = sem("p1_cnt")
        p1_rank = sem("p1_rank")
        p1_chosen = sem("p1_chosen")
        p1_pos = sem("p1_pos")
        p1_slot = sem("p1_slot")
        p1_onehot = sem("p1_onehot")
        p1_tab = sem("p1_tab")
        p1_tab_score = sem("p1_tab_score")
        p1_gather_ps = sem("p1_gather_ps")
        p1_gathered = sem("p1_gathered")
        p1_mean = sem("p1_mean")
        init_done = sem("init_done")
        f_const_in = sem("f_const_in")
        w2_in0 = sem("w2_in0")
        w2_in1 = sem("w2_in1")
        ss2_ready = sem("ss2_ready")
        ms2_ready = sem("ms2_ready")
        rs2_ready = sem("rs2_ready")
        h_ready = sem("h_ready")
        hT_ps = sem("hT_ps")
        hT_ready = sem("hT_ready")
        tabT_ps = sem("tabT_ps")
        tabT_ready = sem("tabT_ready")
        bias_ps = sem("bias_ps")
        biasT_ready = sem("biasT_ready")
        proj_ps = sem("proj_ps")
        proj_out = sem("proj_out")
        raw_used = sem("raw_used")
        rope_a = sem("rope_a")
        rope_b = sem("rope_b")
        rope_done = sem("rope_done")
        v2_ready = sem("v2_ready")
        s2_ps = sem("s2_ps")
        s2_low = sem("s2_low")
        s2_exp = sem("s2_exp")
        s2_den = sem("s2_den")
        s2_prob = sem("s2_prob")
        pT2_ps = sem("pT2_ps")
        pT2_ready = sem("pT2_ready")
        o2_ps = sem("o2_ps")
        o2_ready = sem("o2_ready")
        wo_ps = sem("wo_ps")
        x1_ready = sem("x1_ready")
        wm_in0 = sem("wm_in0")
        wm_in1 = sem("wm_in1")
        gu_ps = sem("gu_ps")
        eg_ready = sem("eg_ready")
        sg_1 = sem("sg_1")
        sg_2 = sem("sg_2")
        sg_3 = sem("sg_3")
        aT_ready = sem("aT_ready")
        wm_free = sem("wm_free")
        zero_ready = sem("zero_ready")
        mlp_ps = sem("mlp_ps")
        delta_a = sem("delta_a")
        delta_b = sem("delta_b")
        delta_done = sem("delta_done")
        gate_1 = sem("gate_1")
        gate_2 = sem("gate_2")
        gate_3 = sem("gate_3")
        xb_in = sem("xb_in")
        xn_ready = sem("xn_ready")
        xnT_ps = sem("xnT_ps")
        xnT_ready = sem("xnT_ready")
        qk_ps = sem("qk_ps")
        qk_sq = sem("qk_sq")
        qk_raw = sem("qk_raw")
        ss3_ready = sem("ss3_ready")
        ms3_ready = sem("ms3_ready")
        rs3_ready = sem("rs3_ready")
        scaled = sem("scaled")
        rotated = sem("rotated")
        cosed = sem("cosed")
        roped_ready = sem("roped_ready")
        v_ps = sem("v_ps")
        v_ready = sem("v_ready")
        hi_ready = sem("hi_ready")
        lo_ready = sem("lo_ready")
        stack_ready = sem("stack_ready")
        stackT_ps = sem("stackT_ps")
        stackT_ready = sem("stackT_ready")
        m_ps = sem("m_ps")
        m_seen = sem("m_seen")
        topT_ps = sem("topT_ps")
        toprow_ready = sem("toprow_ready")
        row_in = sem("row_in")
        sc_ps = sem("sc_ps")
        sc_exp = sem("sc_exp")
        sc_masked = sem("sc_masked")
        o_ps = sem("o_ps")
        rden_ready = sem("rden_ready")
        oT_ready = sem("oT_ready")
        kones_ready = sem("kones_ready")
        stats_b = sem("stats_b")
        xr_norm = sem("xr_norm")
        xr_ready = sem("xr_ready")
        oh_ready = sem("oh_ready")
        y_ps = sem("y_ps")
        y_ready = sem("y_ready")
        xr_in = [sem(f"xr_in{i}") for i in range(RING)]
        out_done = [sem(f"out_done{i}") for i in range(RING)]

        def wait(eng, semaphore, value):
            if not isinstance(value, int) or value > 0:
                eng.wait_ge(semaphore, value)

        passed = {e.engine: sem(f"passed_{n}") for n, e in (("sync", nc.sync), ("gpsimd", nc.gpsimd), ("vector", nc.vector))}

        def wait_apart(eng, semaphore, value):
            if isinstance(value, int):
                wait(eng, semaphore, value)
            else:
                eng.wait_ge(semaphore, value)
                eng.sem_inc(passed[eng.engine], 1)

        block = ctx.enter_context(nc.Block())

        @block.sync
        def _(sp):
            sp.dma_start(arena[:, 0:C_TRI], const_d[:, 0:C_TRI]).then_inc(consts_in, 16)
            sp.dma_start(cst1, const_d[:, C_TRI:C_W]).then_inc(consts1_in, 16)
            sp.dma_start(wr_b, wr_d.partition_broadcast(P)).then_inc(consts1_in, 16)
            with sp.Fori(0, B) as b:
                sp.dma_start(x_all[:, bass.ds(b * NT, NT), :], x_v[bass.ds(b, 1), :, :, :].rearrange("b p t d -> p (b t) d")).then_inc(x_in, 16)
                wait_apart(sp, x_in, b * 16 + 16)
            sp.dma_start(w_qkv, wqkv_v).then_inc(late_in, 16)
            sp.wait_ge(p1_gathered, 3 * B + 1)
            sp.wait_ge(rope_ready, 3)
            sp.wait_ge(p1_mean, 2 * B + 1)
            sp.dma_start(w_out, wout_v).then_inc(late_in, 16)
            sp.dma_start(bias_rows[0:FH, :], bq_d.rearrange("(h d) -> h d", d=FD)).then_inc(f_const_in, 16)
            sp.dma_start(bias_rows[FH:FH + FKV, :], bk_d.rearrange("(h d) -> h d", d=FD)).then_inc(f_const_in, 16)
            sp.dma_start(bv_b, bv_d.partition_broadcast(P)).then_inc(f_const_in, 16)
            sp.dma_start(ln1_b, ln1_d.partition_broadcast(P)).then_inc(f_const_in, 16)
            sp.dma_start(ln2_b, ln2_d.partition_broadcast(P)).then_inc(f_const_in, 16)
            def load_heads(n, u):
                for dst, src in ((wq_s, wq_v), (wk_s, wk_v), (wv_s, wv_v), (wo_s, wo_v)):
                    sp.dma_start(dst[u], src[bass.ds(n, 1), :, :, :].rearrange("n p k c -> p (n k) c")).then_inc((w2_in0, w2_in1)[u], 16)

            for u in range(2):
                load_heads(u, u)
            with sp.Fori(1, FKV // 2) as i:
                for u in range(2):
                    sp.wait_ge(wo_ps, i * (2 * ST) + (u - 1) * ST + 1)
                    load_heads(i * 2 + u, u)

            def load_mlp(n, u):
                filled = (wm_in0, wm_in1)[u]
                for dst, src in ((wg_s, wg_v), (wu_s, wu_v)):
                    sp.dma_start(dst[u], src[bass.ds(n, 1), :, :, :].rearrange("n p k c -> p (n k) c")).then_inc(filled, 16)
                sp.dma_start(wd_s[u], wd_v[bass.ds(n, 1), :, :].rearrange("n p c -> p (n c)")).then_inc(filled, 16)

            sp.wait_ge(pT2_ready, FKV * REP * ST)
            sp.wait_ge(o2_ps, FKV * REP + 1)
            for u in range(2):
                load_mlp(u, u)
            with sp.Fori(1, NC // 2) as i:
                for u in range(2):
                    sp.wait_ge(wm_free, i * 2 + u - 1 + 1)
                    load_mlp(i * 2 + u, u)
            sp.wait_ge(delta_done, ST)
            sp.dma_start(xn, x_v[0, :, :, :]).then_inc(xb_in, 16)

            def batch(b, first):
                if not first:
                    outputs(b - 1)
                sp.wait_ge(xnT_ps, b * NT + NT)
                nb = (b + 1) % B
                sp.dma_start(xn, x_v[bass.ds(nb, 1), :, :, :].rearrange("b p t d -> p (b t) d")).then_inc(xb_in, 16)
                for p in range(NP):
                    sp.wait_ge(toprow_ready, b * NP + p + 1)
                    sp.dma_start(qS[p % 2][RH:RH + 1, :, :].bitcast(f32), top_rows[0:2 * NT, :]).then_inc(row_in, 16)

            def outputs(b):
                def fetch(t):
                    sp.dma_start(xr[:, t % RING, :], x_v[bass.ds(b, 1), :, t, :].rearrange("b p d -> p (b d)")).then_inc(xr_in[t % RING], 16)

                for t in range(RING):
                    fetch(t)
                for t in range(NT):
                    sp.wait_ge(y_ready, b * NT + t + 1)
                    sp.dma_start(out_v[bass.ds(b, 1), :, t, :].rearrange("b p d -> p (b d)"), xr[:, t % RING, :]).then_inc(out_done[t % RING], 16)
                    wait_apart(sp, out_done[t % RING], b * (16 * NT // RING) + 16 * (t // RING + 1))
                    if t + RING < NT:
                        fetch(t + RING)

            batch(0, True)
            with sp.Fori(1, B) as b:
                batch(b, False)
            outputs(B - 1)
            sp.wait_ge(xb_in, 16 * (B + 1))

        @block.gpsimd
        def _(pool):
            for started in (p1_mean,):
                pool.sem_inc(started, 1)
            pool.memset(half_neg, -0.5).then_inc(init_done, 1)
            pool.dma_start(gam[:, 0, :], qg_d.partition_broadcast(P)).then_inc(gam_ready, 16)
            pool.dma_start(gam[:, 1, :], kg_d.partition_broadcast(P)).then_inc(gam_ready, 16)
            pool.dma_start(rope_raw, rope_d.rearrange("(t p) c -> p t c", p=P)).then_inc(gam_ready, 16)
            pool.dma_start(tab[:, :, 0:FT_W], frope_d.rearrange("(t p) c -> p t c", p=P)).then_inc(p1_tab, 16)
            pool.wait_ge(init_done, 1)
            with pool.Fori(0, B) as b:
                wait_apart(pool, p1_stats, b * 2 * NT + 2 * NT)
                pool.tensor_scalar(vpe, mv[:, :, 1], LN_EPS, None, ALU.add).then_inc(p1_vpe, 1)
                pool.wait_ge(p1_vpe, b + 1)
                pool.tensor_tensor(rstd1, vpe, half_neg[:, 0:NT], ALU.pow).then_inc(p1_rstd, 1)
                wait_apart(pool, p1_rstd, b + 1)
                pool.tensor_copy(ln_mean[:, bass.ds(b, 1), :].rearrange("p b t -> p (b t)"), mv[:, :, 0]).then_inc(p1_mean, 1)
                pool.tensor_copy(ln_rstd[:, bass.ds(b, 1), :].rearrange("p b t -> p (b t)"), rstd1).then_inc(p1_mean, 1)
            pool.wait_ge(gam_ready, 48)
            for w in range(2):
                g = gam[:, w, :]
                gb = g.unsqueeze(1).to_broadcast([P, NT, AD])
                scale = AD ** -0.5 if w == 0 else 1.0
                pool.tensor_tensor(cosG[:, :, w, :], rope_raw[:, :, 0:AD], gb, ALU.mult).then_inc(rope_ready, 1)
                for h in range(2):
                    o = h * (AD // 2)
                    gr = g[:, AD // 2 - o:AD - o].unsqueeze(1).to_broadcast([P, NT, AD // 2])
                    last = pool.tensor_tensor(sinG[:, :, w, o:o + AD // 2], rope_raw[:, :, AD + o:AD + o + AD // 2], gr, ALU.mult)
                last.then_inc(rope_ready, 1)
            pool.wait_ge(rope_ready, 4)
            pool.tensor_scalar(cosG[:, :, 0, :], cosG[:, :, 0, :], AD ** -0.5, None, ALU.mult)
            pool.tensor_scalar(sinG[:, :, 0, :], sinG[:, :, 0, :], AD ** -0.5, None, ALU.mult).then_inc(rope_ready, 1)
            for n in range(2):
                pool.wait_ge(ss2_ready, ST * (n + 1))
                pool.tensor_scalar(ms2, ss2, 1.0 / D, RMS_EPS, ALU.mult, ALU.add).then_inc(ms2_ready, 1)
                pool.wait_ge(ms2_ready, n + 1)
                pool.tensor_tensor(rs2, ms2, half_neg[:, 0:ST], ALU.pow).then_inc(rs2_ready, 1)
            pool.wait_ge(delta_done, ST)
            for i in range(2):
                pool.memset(kS[i][RH:RH + 1, :, :].bitcast(f32), 1.0).then_inc(kones_ready, 1)
            qk4 = qk.rearrange("p (w h d) -> p w h d", w=2, d=AD)
            rot4 = rot.rearrange("p (w h d) -> p w h d", w=2, d=AD)

            def outputs(b):
                pool.tensor_copy(ohT, onehotT[:, bass.ds(b, 1), :].rearrange("p b t -> p (b t)")).then_inc(oh_ready, 1)
                pool.tensor_copy(mean_b, ln_mean[:, bass.ds(b, 1), :].rearrange("p b t -> p (b t)")).then_inc(stats_b, 1)
                pool.tensor_copy(rstd_b, ln_rstd[:, bass.ds(b, 1), :].rearrange("p b t -> p (b t)")).then_inc(stats_b, 1)
                wait_apart(pool, stats_b, b * 2 + 2)
                for t in range(NT):
                    wait_apart(pool, xr_in[t % RING], b * (16 * NT // RING) + 16 * (t // RING + 1))
                    if t >= 2:
                        wait_apart(pool, xr_ready, b * NT + t - 1)
                    tmp = rot[:, (t % 2) * D:(t % 2 + 1) * D]
                    pool.tensor_scalar(tmp, xr[:, t % RING, :], mean_b[:, t:t + 1], rstd_b[:, t:t + 1], ALU.subtract, ALU.mult).then_inc(xr_norm, 1)
                    pool.wait_ge(xr_norm, b * NT + t + 1)
                    pool.tensor_tensor(xr[:, t % RING, :], xr[:, t % RING, :], tmp, ALU.add).then_inc(xr_ready, 1)

            def build(b, p):
                q = b * NP + p
                wait_apart(pool, stackT_ps, q * 8)
                if p == 0:
                    wait_apart(pool, roped_ready, b * NT + NT)
                for w in range(2):
                    src = roped[:, :, w * D + p * 2 * AD:w * D + (p + 1) * 2 * AD].rearrange("p t (h d) -> p t h d", h=2)
                    st = stack[:, w].rearrange("p t (h c) -> p t h c", h=2)
                    hi = st[:, :, :, 0:AD]
                    hi2 = st[:, :, :, AD:2 * AD] if w else st[:, :, :, 2 * AD:3 * AD]
                    lo = st[:, :, :, 2 * AD:3 * AD] if w else st[:, :, :, AD:2 * AD]
                    for h in range(2):
                        pool.tensor_copy(hi[:, :, h].bitcast(f32r), src[:, :, h]).then_inc(hi_ready, 1)
                    wait_apart(pool, hi_ready, q * 4 + w * 2 + 2)
                    for h in range(2):
                        pool.tensor_tensor(lo[:, :, h], src[:, :, h], hi[:, :, h], ALU.subtract).then_inc(lo_ready, 1)
                        last = pool.tensor_copy(hi2[:, :, h], hi[:, :, h])
                    last.then_inc(stack_ready, 1)

            def batch(b, first):
                if not first:
                    outputs(b - 1)
                for t in range(NT):
                    k = b * NT + t + 1
                    wait_apart(pool, ss3_ready, k)
                    pool.tensor_scalar(ms3, ss3, 1.0 / AD, RMS_EPS, ALU.mult, ALU.add).then_inc(ms3_ready, 1)
                    pool.wait_ge(ms3_ready, k)
                    pool.tensor_tensor(rs3, ms3, half_neg, ALU.pow).then_inc(rs3_ready, 1)
                    pool.wait_ge(scaled, k)
                    wait(pool, roped_ready, k - 1)
                    for w in range(2):
                        for h in range(2):
                            o = h * (AD // 2)
                            sn = sinG[:, t, w, o:o + AD // 2].unsqueeze(1).to_broadcast([P, AH, AD // 2])
                            last = pool.tensor_tensor(rot4[:, w, :, o:o + AD // 2],
                                                      qk4[:, w, :, AD // 2 - o:AD - o], sn, ALU.mult)
                    last.then_inc(rotated, 1)
                build(b, 0)
                build(b, 1)
                for p in range(NP):
                    for n, (c, j) in enumerate(STEPS):
                        if j >= 4 * c:
                            k = p * NS + n
                            wait_apart(pool, sc_exp, b * NP * NS + k + 1)
                            blk = probT[:, k % SLOTS, :, (j - 4 * c) * P:(j - 4 * c + 1) * P]
                            pool.affine_select(out=blk, in_=blk, compare_op=ALU.is_ge, fill=0.0, base=0,
                                               pattern=[[0, 2], [1, P]], channel_multiplier=-1).then_inc(sc_masked, 1)
                        if (c, j) == (0, 3) and p + 2 < NP:
                            build(b, p + 2)

            batch(0, True)
            with pool.Fori(1, B) as b:
                batch(b, False)
            outputs(B - 1)

        @block.scalar
        def _(act):
            def out_pT(n, m):
                h, t = m // ST, m % ST
                act.wait_ge(pT2_ps, n * 8 + m + 1 + 1)
                act.activation(probT2[h][:, 0:t + 1, t * P:(t + 1) * P],
                               psum[:, 4 + m % 2, 0:(t + 1) * P].rearrange("p (j n) -> p j n", n=P), ACT.Copy).then_inc(pT2_ready, 1)

            for started in (p1_gathered, proj_out):
                act.sem_inc(started, 1)
            with act.Fori(0, B) as b:
                act.wait_ge(p1_row_ps, b + 1)
                act.activation(s_row, psum[:, 0:2, :].rearrange("p a n -> p (a n)"), ACT.Copy).then_inc(p1_row, 1)
                act.wait_ge(p1_gather_ps, b * 3 + 1)
                act.activation(xsel[:, bass.ds(b, 1), :].rearrange("p b d -> p (b d)"), psum[:, 3, :], ACT.Copy).then_inc(p1_gathered, 1)
                act.wait_ge(p1_gather_ps, b * 3 + 2)
                act.activation(tabsel[:, bass.ds(b, 1), :].rearrange("p b d -> p (b d)"), psum[:, 4, 0:FT_W + 1], ACT.Copy).then_inc(p1_gathered, 1)
                act.wait_ge(p1_gather_ps, b * 3 + 3)
                act.activation(onehotT[:, bass.ds(b, 1), :].rearrange("p b t -> p (b t)"),
                               psum[:, 5:7, :].rearrange("p a n -> p (a n)"), ACT.Copy).then_inc(p1_gathered, 1)
            act.wait_ge(p1_gathered, 3 * B + 1)
            act.activation(egate, tabsel[:, :, FT_W], ACT.Exp, scale=-1.0).then_inc(gate_1, 1)

            def turn_h(n):
                for t in range(ST):
                    act.wait_ge(hT_ps, n * ST + t + 1)
                    act.activation(hT[:, :, t * P:(t + 1) * P], psum[:, t, :].rearrange("p (k n) -> p k n", k=KD), ACT.Copy).then_inc(hT_ready, 1)

            turn_h(0)
            act.wait_ge(tabT_ps, 1)
            act.activation(cosT, psum[:, 4, :], ACT.Copy).then_inc(tabT_ready, 1)
            act.activation(sinT, psum[:, 5, :], ACT.Copy).then_inc(tabT_ready, 1)
            act.wait_ge(bias_ps, 1)
            act.activation(biasT, psum[:, 6, 0:FH + FKV], ACT.Copy).then_inc(biasT_ready, 1)
            act.wait_ge(biasT_ready, 1)
            with act.Fori(0, FKV // 2) as i:
                for u in range(2):
                    n = i * 2 + u
                    for r in range(REP + 1):
                        act.wait_ge(proj_ps, n * 4 + r + 1)
                        if r == 0:
                            act.wait_ge(rope_done, n * 3 + 1)
                        if r == 2:
                            act.wait_ge(rope_done, n * 3 + 1 + 1)
                        bcol = biasT[:, bass.ds(n * REP + r, 1)] if r < REP else biasT[:, bass.ds(n + FH, 1)]
                        act.activation(raw[:, r % 2, :], psum[:, r % 2, :], ACT.Identity, bias=bcol).then_inc(proj_out, 1)
                    for m in range(REP * ST):
                        w = (m % ST + 1) * P
                        act.wait_ge(s2_low, n * 8 + m + 1)
                        act.activation(prob2[:, m, 0:w], prob2[:, m, 0:w], ACT.Exp, bias=nmax2[:, m:m + 1], scale=-1.0,
                                       accum_out=den2[:, m:m + 1]).then_inc(s2_exp, 1)
                        if m >= 2:
                            out_pT(n, m - 2)
                    out_pT(n, 6)
                    out_pT(n, 7)
            turn_h(1)
            with act.Fori(0, NC // 2) as i:
                for u in range(2):
                    act.wait_ge(gu_ps, i * 4 + 2 * u + 1)
                    act.wait_ge(sg_3, i * 2 + 1)
                    act.activation(eg[:, u, :], psum[:, 2 * u, :], ACT.Exp, scale=-1.0).then_inc(eg_ready, 1)
            act.wait_ge(delta_done, ST)

            def user(b, p, kind, arg):
                q = b * NP + p
                bank = 6 + USERS.index((kind, arg)) % 2
                if kind == "turn":
                    w, h, half = arg
                    n = TURNS.index(arg)
                    if n == 0:
                        wait(act, sc_ps, (q - 1) * NS)
                        wait(act, m_ps, q * len(PIECES))
                    act.wait_ge(stackT_ps, q * 8 + n + 1)
                    act.activation((kS if w else qS)[p % 2][0:RH, h, half * CH:(half + 1) * CH], psum[0:RH, bank, :], ACT.Copy).then_inc(stackT_ready, 1)
                if kind == "top":
                    act.wait_ge(topT_ps, q + 1)
                    wait(act, row_in, q * 16)
                    act.activation(top_rows[0:2 * NT, :].bitcast(f32r), psum[0:2 * NT, bank, 0:P], ACT.Copy, scale=-1.0).then_inc(toprow_ready, 1)

            def batch(b, first):
                wait(act, o_ps, b * NP * NS)
                for t in range(NT):
                    act.wait_ge(xnT_ps, b * NT + t + 1)
                    act.activation(xnT[:, :, t * P:(t + 1) * P], psum[:, 6 + t % 2, :].rearrange("p (k n) -> p k n", k=KD), ACT.Copy).then_inc(xnT_ready, 1)
                for t in range(NT):
                    a = 2 * (t % 2)
                    k = b * NT + t + 1
                    qkp = psum[:, a:a + 2, :].rearrange("p a n -> p (a n)")
                    act.wait_ge(qk_ps, k)
                    if t == 0:
                        wait(act, stackT_ps, b * NP * 8)
                    wait(act, ss3_ready, k - 1)
                    act.activation(sq, qkp, ACT.Square).then_inc(qk_sq, 1)
                    wait(act, rotated, k - 1)
                    wait(act, cosed, k - 1)
                    act.activation(qk, qkp, ACT.Copy).then_inc(qk_raw, 1)
                for t in range(NT):
                    act.wait_ge(v_ps, b * NT + t + 1)
                    act.activation(v[:, t, :], psum[:, 4 + t % 2, :], ACT.Copy).then_inc(v_ready, 1)
                    for u in BESIDE_V[t]:
                        user(b, 0, *u)
                for p in range(NP):
                    for n, (c, j) in enumerate(STEPS):
                        k = p * NS + n
                        lo = max(0, j - 4 * c) * P
                        act.wait_ge(sc_ps, b * NP * NS + k + 1)
                        if k >= SLOTS:
                            act.wait_ge(o_ps, b * NP * NS + k - SLOTS + 1)
                        a = 2 * (k % 2)
                        act.activation(probT[:, k % SLOTS, :, lo:CH], psum[:, a:a + 2, lo:CH], ACT.Exp).then_inc(sc_exp, 1)
                        if p + 1 < NP:
                            for u in BESIDE_STEP[n]:
                                user(b, p + 1, *u)

            batch(0, True)
            with act.Fori(1, B) as b:
                batch(b, False)

        @block.tensor
        def _(pe):
            for started in (o2_ps, pT2_ps, s2_ps, wm_free, wo_ps,):
                pe.sem_inc(started, 1)
            pe.wait_ge(consts_in, 16)
            pe.wait_ge(consts1_in, 32)
            pe.wait_ge(p1_tab, 16)
            with pe.Fori(0, B) as b:
                pe.wait_ge(p1_score, b * NT + NT)
                for t in range(NT):
                    last = pe.transpose(psum[:, t // 4, (t % 4) * P:(t % 4 + 1) * P], s_col[:, t:t + 1].to_broadcast([P, P]), ident)
                last.then_inc(p1_row_ps, 1)
                pe.wait_ge(p1_chosen, b + 1)
                pe.matmul(psum[:, 2, 0:NT], tri, chosen, start=True, stop=False)
                for k in range(1, NT):
                    last = pe.matmul(psum[:, 2, k:NT], ones, chosen[:, 0:NT - k], start=False, stop=(k == NT - 1))
                last.then_inc(p1_pos, 1)
                pe.wait_ge(p1_onehot, b + 1)
                pe.wait_ge(p1_gathered, b * 3 + 1)
                for t in range(NT):
                    last = pe.matmul(psum[:, 3, :], onehot[:, t, :], xn1[:, t, :], start=(t == 0), stop=(t == NT - 1))
                last.then_inc(p1_gather_ps, 1)
                for t in range(NT):
                    last = pe.matmul(psum[:, 4, 0:FT_W + 1], onehot[:, t, :], tab[:, t, :], start=(t == 0), stop=(t == NT - 1))
                last.then_inc(p1_gather_ps, 1)
                for t in range(NT):
                    last = pe.transpose(psum[:, 5 + t // 4, (t % 4) * P:(t % 4 + 1) * P], onehot[:, t, :], ident)
                last.then_inc(p1_gather_ps, 1)

            def turn_h(n):
                for t in range(ST):
                    pe.wait_ge(h_ready, n * ST + t + 1)
                    for k in range(KD):
                        last = pe.transpose(psum[:, t, k * P:(k + 1) * P], hn[:, t, k * P:(k + 1) * P], ident)
                    last.then_inc(hT_ps, 1)

            pe.wait_ge(p1_gathered, 3 * B + 1)
            turn_h(0)
            for w in range(2):
                for t in range(ST):
                    last = pe.transpose(psum[:, 4 + w, t * P:(t + 1) * P], tabsel[:, t, w * FD:(w + 1) * FD], ident)
            last.then_inc(tabT_ps, 1)
            pe.wait_ge(f_const_in, 80)
            pe.transpose(psum[:, 6, 0:FH + FKV], bias_rows[0:FH + FKV, :], ident[0:FH + FKV, 0:FH + FKV]).then_inc(bias_ps, 1)
            pe.wait_ge(hT_ready, ST)
            pe.wait_ge(tabT_ready, 2)
            pe.wait_ge(biasT_ready, 1)
            with pe.Fori(0, FKV // 2) as i:
                for u in range(2):
                    n = i * 2 + u
                    pe.wait_ge((w2_in0, w2_in1)[u], i * 64 + 64)
                    for r in range(REP + 1):
                        if r == 0:
                            pe.wait_ge(proj_out, n * 3 + 1)
                        if r == 1:
                            pe.wait_ge(v2_ready, n + 1)
                        if r == 2:
                            pe.wait_ge(proj_out, n * 3 + 1 + 1)
                        for k in range(KD):
                            w = wq_s[u][:, k, r * FD:(r + 1) * FD] if r < REP else wk_s[u][:, k, :]
                            last = pe.matmul(psum[:, r % 2, :], w, hT[:, k, :], start=(k == 0), stop=(k == KD - 1))
                        last.then_inc(proj_ps, 1)
                    pe.wait_ge(proj_out, n * 3 + 2 + 1)
                    for t in range(ST):
                        for k in range(KD):
                            last = pe.matmul(psum[:, 1, t * P:(t + 1) * P], hT[:, k, t * P:(t + 1) * P], wv_s[u][:, k, :],
                                             start=(k == 0), stop=(k == KD - 1))
                    last.then_inc(proj_ps, 1)
                    pe.wait_ge(rope_done, n * 3 + 3 + 1)

                    def scores(m):
                        h, t = m // ST, m % ST
                        if m >= 2:
                            pe.wait_ge(s2_low, n * 8 + m - 1)
                        pe.matmul(psum[:, 2 + m % 2, 0:(t + 1) * P], qT2[:, h, t * P:(t + 1) * P], kT2[:, 0:(t + 1) * P],
                                  start=True, stop=True).then_inc(s2_ps, 1)

                    def turn(m):
                        t = m % ST
                        pe.wait_ge(s2_prob, n * 8 + m + 1)
                        if m >= 2:
                            pe.wait_ge(pT2_ready, n * 8 + m - 1)
                        for j in range(t + 1):
                            last = pe.transpose(psum[:, 4 + m % 2, j * P:(j + 1) * P], prob2[:, m, j * P:(j + 1) * P], ident)
                        last.then_inc(pT2_ps, 1)

                    def values(h):
                        pe.wait_ge(pT2_ready, n * 8 + (h + 1) * ST)
                        if h == 0:
                            pe.wait_ge(v2_ready, n + 1 + 1)
                            pe.wait_ge(x1_ready, n * ST + 1)
                        if h == 1:
                            pe.wait_ge(o2_ready, n * REP + 1)
                        for j in range(ST):
                            last = pe.matmul(psum[:, 6, j * P:S], v2[:, j, :], probT2[h][:, j, j * P:S], start=(j == 0), stop=(j == ST - 1))
                        last.then_inc(o2_ps, 1)

                    for m in range(REP * ST):
                        scores(m)
                        if m >= 3:
                            turn(m - 3)
                    for m in range(REP * ST - 3, REP * ST):
                        turn(m)
                    values(0)
                    values(1)
                    pe.wait_ge(o2_ready, n * REP + 2)
                    for t in range(ST):
                        if t >= 2:
                            pe.wait_ge(x1_ready, n * ST + t - 1 + 1)
                        for h in range(REP):
                            last = pe.matmul(psum[:, 7 - t % 2, :], oT2[:, h, t * P:(t + 1) * P], wo_s[u][:, h, :], start=(h == 0), stop=(h == REP - 1))
                        last.then_inc(wo_ps, 1)
            turn_h(1)
            pe.wait_ge(hT_ready, 2 * ST)
            pe.wait_ge(zero_ready, 1)
            for t in range(ST):
                pe.matmul(psum[:, 4 + t, :], zrow[:, 0:P], zrow, start=True, stop=False, skip_group_check=True)
            with pe.Fori(0, NC // 2) as i:
                for u in range(2):
                    pe.wait_ge((wm_in0, wm_in1)[u], i * 48 + 48)
                    pe.wait_ge(aT_ready, i * 2 + 1)
                    for w in range(2):
                        for k in range(KD):
                            last = pe.matmul(psum[:, 2 * u + w, :], (wg_s, wu_s)[w][u][:, k, :], hT[:, k, :], start=(k == 0), stop=(k == KD - 1))
                        last.then_inc(gu_ps, 1)
                for u in range(2):
                    pe.wait_ge(aT_ready, i * 2 + u + 1 + 1)
                    for t in range(ST):
                        last = pe.matmul(psum[:, 4 + t, :], aT[:, u, t * P:(t + 1) * P], wd_s[u], start=False, stop=False, skip_group_check=True)
                    last.then_inc(wm_free, 1)
            for t in range(ST):
                last = pe.matmul(psum[:, 4 + t, :], zrow[:, 0:P], zrow, start=False, stop=True, skip_group_check=True)
            last.then_inc(mlp_ps, 1)
            pe.wait_ge(delta_done, ST)
            pe.wait_ge(late_in, 32)
            pe.wait_ge(kones_ready, 2)

            def freed(b, p, u):
                q = b * NP + p
                if u < 2 and p == 0:
                    return
                kind, arg = USERS[u - 2]
                if u < 2:
                    q = q - 1
                if kind == "turn":
                    wait(pe, stackT_ready, q * 8 + TURNS.index(arg) + 1)
                if kind == "max":
                    wait(pe, m_seen, q * len(PIECES) + PIECES.index(arg) + 1)
                if kind == "top":
                    wait(pe, toprow_ready, q + 1)

            def user(b, p, kind, arg):
                q = b * NP + p
                u = USERS.index((kind, arg))
                bank = 6 + u % 2
                freed(b, p, u)
                if kind == "turn":
                    w, h, half = arg
                    pe.wait_ge(stack_ready, q * 2 + w + 1)
                    for i in range(CH // P):
                        t = half * (CH // P) + i
                        last = pe.transpose(psum[0:RH, bank, i * P:(i + 1) * P], stack[:, w, t, h * STK:h * STK + RH], ident)
                    last.then_inc(stackT_ps, 1)
                if kind == "max":
                    t, c, h = arg
                    w = min(CH, (t + 1) * P - c * CH)
                    pe.wait_ge(stackT_ready, q * 8 + (4 if t < 4 else 8))
                    pe.matmul(psum[:, bank, 0:w], qS[p % 2][0:RH, h, t * P:(t + 1) * P], kS[p % 2][0:RH, h, c * CH:c * CH + w],
                              start=True, stop=True).then_inc(m_ps, 1)
                if kind == "top":
                    pe.wait_ge(m_seen, (q + 1) * len(PIECES))
                    pe.transpose(psum[0:2 * NT, bank, 0:P], top[:, p % 2, :], ident).then_inc(topT_ps, 1)

            def outputs(b):
                pe.wait_ge(oT_ready, b * 2 * NP + 2 * NP)
                pe.wait_ge(oh_ready, b + 1)
                for t in range(NT):
                    if t >= 2:
                        pe.wait_ge(y_ready, b * NT + t - 1)
                    bank = psum[:, 4 + t % 2, :]
                    for g in range(NG):
                        pe.matmul(bank, oT[:, g, t * P:(t + 1) * P], w_out[:, g, :], start=(g == 0), stop=False)
                    pe.matmul(bank, ohT[:, t * P:(t + 1) * P], delta[:, bass.ds(b, 1), :].rearrange("p b d -> p (b d)"), start=False, stop=True).then_inc(y_ps, 1)

            def score(b, p, n):
                c, j = STEPS[n]
                lo = max(0, j - 4 * c) * P
                k = p * NS + n
                if n == 0:
                    pe.wait_ge(row_in, (b * NP + p + 1) * 16)
                if k >= 2:
                    pe.wait_ge(sc_exp, b * NP * NS + k - 1)
                else:
                    pe.wait_ge(qk_raw, b * NT + NT)
                a = 2 * (k % 2)
                for h in range(2):
                    last = pe.matmul(psum[:, a + h, lo:CH], kS[p % 2][0:RH + 1, h, j * P:(j + 1) * P],
                                     qS[p % 2][0:RH + 1, h, c * CH + lo:(c + 1) * CH], start=True, stop=True)
                last.then_inc(sc_ps, 1)

            def value(b, p, n):
                c, j = STEPS[n]
                lo = max(0, j - 4 * c) * P
                k = p * NS + n
                if j >= 4 * c:
                    pe.wait_ge(sc_masked, b * NP * 8 + p * 8 + j + 1)
                else:
                    pe.wait_ge(sc_exp, b * NP * NS + k + 1)
                if j == 0:
                    m = b * 2 * NP + 2 * p + c
                    if p == 0:
                        pe.wait_ge(v_ready, b * NT + NT)
                    else:
                        pe.wait_ge(oT_ready, m - 1)
                bank = 4 + c % 2
                for r in range(4):
                    h = r % 2
                    w = v[:, j, (p * 2 + h) * AD:(p * 2 + h + 1) * AD] if r < 2 else ones[:, 0:AD]
                    last = pe.matmul(psum[AD * r:AD * (r + 1), bank, lo:CH], w, probT[:, k % SLOTS, h, lo:CH],
                                     start=(j == 0), stop=(j == 4 * c + 3))
                last.then_inc(o_ps, 1)

            def batch(b, first):
                for t in range(NT):
                    pe.wait_ge(xn_ready, b * NT + t + 1)
                    if t >= 2:
                        pe.wait_ge(xnT_ready, b * NT + t - 1)
                    else:
                        wait(pe, toprow_ready, b * NP)
                    for k in range(KD):
                        last = pe.transpose(psum[:, 6 + t % 2, k * P:(k + 1) * P], xn[:, t, k * P:(k + 1) * P], ident)
                    last.then_inc(xnT_ps, 1)
                if not first:
                    outputs(b - 1)
                pe.wait_ge(xnT_ready, b * NT + NT)
                for t in range(NT):
                    if t >= 2:
                        pe.wait_ge(qk_raw, b * NT + t - 1)
                    else:
                        wait(pe, sc_exp, b * NP * NS)
                    for w in range(2):
                        for k in range(KD):
                            last = pe.matmul(psum[:, 2 * (t % 2) + w, :], xnT[:, k, t * P:(t + 1) * P], w_qkv[:, k, w * D:(w + 1) * D], start=(k == 0), stop=(k == KD - 1))
                    last.then_inc(qk_ps, 1)
                for t in range(NT):
                    if t >= 2:
                        pe.wait_ge(v_ready, b * NT + t - 1)
                    else:
                        wait(pe, y_ready, b * NT)
                    for k in range(KD):
                        last = pe.matmul(psum[:, 4 + t % 2, :], xnT[:, k, t * P:(t + 1) * P], w_qkv[:, k, 2 * D:3 * D], start=(k == 0), stop=(k == KD - 1))
                    last.then_inc(v_ps, 1)
                    for u in BESIDE_V[t]:
                        user(b, 0, *u)
                for p in range(NP):
                    for n in range(NS):
                        score(b, p, n)
                        beside = BESIDE_STEP[n] if p + 1 < NP else []
                        for u in beside[:len(beside) // 2]:
                            user(b, p + 1, *u)
                        if p * NS + n >= 2:
                            value(b, *divmod(p * NS + n - 2, NS))
                        for u in beside[len(beside) // 2:]:
                            user(b, p + 1, *u)
                value(b, NP - 1, NS - 2)
                value(b, NP - 1, NS - 1)

            batch(0, True)
            with pe.Fori(1, B) as b:
                batch(b, False)
            outputs(B - 1)

        @block.vector
        def _(dve):
            for started in (rope_done, sg_3, aT_ready, v2_ready, x1_ready,):
                dve.sem_inc(started, 1)
            dve.wait_ge(consts1_in, 32)
            dve.wait_ge(p1_tab, 16)
            with dve.Fori(0, B) as b:
                dve.wait_ge(x_in, b * 16 + 16)
                for t in range(NT):
                    dve.bn_stats(stats[:, t, :], x_all[:, bass.ds(b * NT + t, 1), :].rearrange("p b d -> p (b d)")).then_inc(p1_stats, 1)
                wait_apart(dve, p1_stats, b * 2 * NT + NT)
                wait_apart(dve, p1_mean, b * 2 + 1)
                for t in range(NT):
                    dve.bn_aggr(mv[:, t, :], stats[:, t, :]).then_inc(p1_stats, 1)
                dve.wait_ge(p1_rstd, b + 1)
                dve.wait_ge(p1_gathered, b * 3 + 1)
                for t in range(NT):
                    dve.tensor_scalar(xn1[:, t, :], x_all[:, bass.ds(b * NT + t, 1), :].rearrange("p b d -> p (b d)"),
                                      mv[:, t, 0:1], rstd1[:, t:t + 1], ALU.subtract, ALU.mult).then_inc(p1_norm, 1)
                for t in range(NT):
                    dve.wait_ge(p1_norm, b * NT + t + 1)
                    if t >= 2:
                        dve.wait_ge(p1_score, b * NT + t - 1)
                    dve.tensor_tensor_reduce(s_row[:, (t % 2) * D:(t % 2 + 1) * D], xn1[:, t, :], wr_b, 1.0, 0.0, ALU.mult, ALU.add, s_col[:, t:t + 1]).then_inc(p1_score, 1)
                dve.wait_ge(p1_score, b * NT + NT)
                dve.tensor_copy(tab[:, :, FT_W], s_col).then_inc(p1_tab_score, 1)
                dve.wait_ge(p1_row, b + 1)
                for t in range(NT):
                    if t >= 1:
                        dve.wait_ge(p1_cnt, b * 2 * NT + 2 * t - 1)
                    dve.tensor_scalar(junk1[:, 0, :], s_row, s_col[:, t:t + 1], 0.0, ALU.is_gt, ALU.add, accum_out=above[:, t:t + 1]).then_inc(p1_cnt, 1)
                    o = T - P - t * P
                    if t >= 1:
                        dve.wait_ge(p1_cnt, b * 2 * NT + 2 * t)
                    dve.scalar_tensor_tensor(out=junk1[:, 1, :], in0=s_row, scalar=s_col[:, t:t + 1], in1=tie[:, o:o + T],
                                             op0=ALU.is_equal, op1=ALU.mult, accum_out=tied[:, t:t + 1]).then_inc(p1_cnt, 1)
                dve.wait_ge(p1_cnt, b * 2 * NT + 2 * NT)
                dve.tensor_tensor(rank, above, tied, ALU.add).then_inc(p1_rank, 1)
                dve.wait_ge(p1_rank, b + 1)
                dve.tensor_scalar(chosen, rank, float(SEL), None, ALU.is_lt).then_inc(p1_chosen, 1)
                dve.wait_ge(p1_pos, b + 1)
                dve.scalar_tensor_tensor(out=slot, in0=psum[:, 2, 0:NT], scalar=1.0, in1=chosen, op0=ALU.add, op1=ALU.mult).then_inc(p1_slot, 1)
                dve.wait_ge(p1_slot, b + 1)
                for t in range(NT):
                    last = dve.tensor_scalar(onehot[:, t, :], iota1, slot[:, t:t + 1], None, ALU.is_equal)
                last.then_inc(p1_onehot, 1)

            dve.wait_ge(gate_1, 1)
            dve.tensor_scalar(dgate, egate, 1.0, None, ALU.add).then_inc(gate_2, 1)
            dve.wait_ge(gate_2, 1)
            dve.reciprocal(gate, dgate).then_inc(gate_3, 1)

            def norm(src, w_b, n):
                for t in range(ST):
                    dve.tensor_tensor_reduce(hn[:, t, :], src[:, t, :], src[:, t, :], 1.0, 0.0, ALU.mult, ALU.add, ss2[:, t:t + 1]).then_inc(ss2_ready, 1)
                dve.wait_ge(rs2_ready, n + 1)
                for t in range(ST):
                    dve.scalar_tensor_tensor(out=hn[:, t, :], in0=src[:, t, :], scalar=rs2[:, t:t + 1], in1=w_b, op0=ALU.mult, op1=ALU.mult).then_inc(h_ready, 1)

            dve.wait_ge(p1_gathered, 3 * B + 1)
            dve.wait_ge(rope_ready, 5)
            dve.wait_ge(f_const_in, 80)
            norm(xsel, ln1_b, 0)
            dve.tensor_copy(x1, xsel).then_inc(delta_a, 1)
            dve.wait_ge(tabT_ready, 2)
            dve.wait_ge(delta_a, 1)
            with dve.Fori(0, FKV // 2) as i:
                for u in range(2):
                    n = i * 2 + u
                    for r in range(REP + 1):
                        dst = qT2[:, r, :] if r < REP else kT2
                        half = FD // 2
                        dve.wait_ge(proj_out, n * 3 + r + 1 + 1)
                        dve.wait_ge(rope_done, n * 3 + r + 1)
                        dve.tensor_tensor(rotd[0:half, :], raw[half:FD, r % 2, :], sinT[half:FD, :], ALU.mult).then_inc(rope_a, 1)
                        dve.tensor_tensor(rotd[half:FD, :], raw[0:half, r % 2, :], sinT[0:half, :], ALU.mult).then_inc(rope_a, 1)
                        if r == 0:
                            dve.wait_ge(s2_ps, n * 8 + 1)
                        dve.tensor_tensor(dst, raw[:, r % 2, :], cosT, ALU.mult).then_inc(rope_a, 1)
                        dve.wait_ge(rope_a, n * 9 + 3 * r + 3)
                        dve.tensor_tensor(dst, dst, rotd, ALU.add).then_inc(rope_done, 1)
                    dve.wait_ge(proj_ps, n * 4 + 4)
                    dve.wait_ge(o2_ps, n * REP + 1)
                    dve.tensor_tensor(v2, psum[:, 1, :].rearrange("p (t d) -> p t d", d=FD),
                                      bv_b[:, bass.ds(n * FD, FD)].unsqueeze(1).to_broadcast([P, ST, FD]), ALU.add).then_inc(v2_ready, 1)

                    def normalise(m):
                        w = (m % ST + 1) * P
                        dve.wait_ge(s2_exp, n * 8 + m + 1)
                        dve.reciprocal(rden2[:, m:m + 1], den2[:, m:m + 1]).then_inc(s2_den, 1)
                        dve.wait_ge(s2_den, n * 8 + m + 1)
                        dve.tensor_scalar(prob2[:, m, 0:w], prob2[:, m, 0:w], rden2[:, m:m + 1], None, ALU.mult).then_inc(s2_prob, 1)

                    for m in range(REP * ST):
                        w = (m % ST + 1) * P
                        if m == 0:
                            wait_apart(dve, pT2_ps, n * 8 + 1)
                        wait_apart(dve, s2_ps, n * 8 + m + 1 + 1)
                        dve.tensor_tensor_reduce(prob2[:, m, 0:w], psum[:, 2 + m % 2, 0:w], mask[:, CH - w:CH], -(FD ** -0.5), 3e38,
                                                 ALU.add, ALU.min, nmax2[:, m:m + 1]).then_inc(s2_low, 1)
                        if m >= 1:
                            normalise(m - 1)
                    normalise(REP * ST - 1)
                    for h in range(REP):
                        dve.wait_ge(o2_ps, n * REP + h + 1 + 1)
                        if h == 0:
                            dve.wait_ge(wo_ps, n * ST + 1)
                        dve.tensor_copy(oT2[:, h, :], psum[:, 6, :]).then_inc(o2_ready, 1)
                    for t in range(ST):
                        dve.wait_ge(wo_ps, n * ST + t + 1 + 1)
                        dve.tensor_tensor(x1[:, t, :], psum[:, 7 - t % 2, :], x1[:, t, :], ALU.add).then_inc(x1_ready, 1)
            dve.wait_ge(x1_ready, FKV * ST + 1)
            norm(x1, ln2_b, 1)
            dve.memset(zrow, 0.0).then_inc(zero_ready, 1)
            with dve.Fori(0, NC // 2) as i:
                for u in range(2):
                    n = i * 2 + u
                    dve.wait_ge(eg_ready, n + 1)
                    dve.tensor_scalar(sg[:, u, :], eg[:, u, :], 1.0, None, ALU.add).then_inc(sg_1, 1)
                    dve.wait_ge(sg_1, n + 1)
                    dve.reciprocal(eg[:, u, :], sg[:, u, :]).then_inc(sg_2, 1)
                    dve.wait_ge(sg_2, n + 1)
                    dve.tensor_tensor(sg[:, u, :], psum[:, 2 * u, :], eg[:, u, :], ALU.mult).then_inc(sg_3, 1)
                    dve.wait_ge(sg_3, n + 1 + 1)
                    dve.wait_ge(gu_ps, n * 2 + 2)
                    dve.wait_ge(wm_free, i * 2 + 1)
                    dve.tensor_tensor(aT[:, u, :], psum[:, 2 * u + 1, :], sg[:, u, :], ALU.mult).then_inc(aT_ready, 1)
            dve.wait_ge(mlp_ps, 1)
            for t in range(ST):
                dve.tensor_tensor(x1[:, t, :], psum[:, 4 + t, :], x1[:, t, :], ALU.add).then_inc(delta_a, 1)
            for t in range(ST):
                dve.wait_ge(delta_a, t + 2)
                dve.tensor_tensor(hn[:, t, :], x1[:, t, :], xsel[:, t, :], ALU.subtract).then_inc(delta_b, 1)
            for t in range(ST):
                dve.wait_ge(delta_b, t + 1)
                dve.tensor_scalar(delta[:, t, :], hn[:, t, :], gate[:, t:t + 1], None, ALU.mult).then_inc(delta_done, 1)

            qk3 = qk.rearrange("p (h d) -> p h d", d=AD)
            qk4 = qk.rearrange("p (w h d) -> p w h d", w=2, d=AD)

            def norms(b):
                nb = b % B
                dve.wait_ge(xb_in, b * 16 + 16)
                for t in range(NT):
                    dve.tensor_scalar(xn[:, t, :], xn[:, t, :], ln_mean[:, bass.ds(nb, 1), t], ln_rstd[:, bass.ds(nb, 1), t],
                                      ALU.subtract, ALU.mult).then_inc(xn_ready, 1)

            def user(b, p, kind, arg):
                if kind != "max":
                    return
                t, c, h = arg
                n = PIECES.index(arg)
                w = min(CH, (t + 1) * P - c * CH)
                q = b * NP + p
                bank = 6 + USERS.index((kind, arg)) % 2
                past = past_top[:, 2 * (t % 2) + h:2 * (t % 2) + h + 1]
                diag = c == t // 4
                wait_apart(dve, m_ps, q * len(PIECES) + n + 1)
                if n == 0:
                    wait_apart(dve, topT_ps, q - 1)
                if not diag:
                    dve.tensor_reduce(past, psum[:, bank, :], AX.X, ALU.max).then_inc(m_seen, 1)
                    return
                if c:
                    wait_apart(dve, m_seen, q * len(PIECES) + PIECES.index((t, c - 1, h)) + 1)
                dve.tensor_tensor_reduce(psum[:, bank, 0:w], psum[:, bank, 0:w], mask[:, CH - w:CH], 1.0,
                                         past if c else -3e38, ALU.add, ALU.max, top[:, p % 2, h * NT + t:h * NT + t + 1]).then_inc(m_seen, 1)

            def finish(b, p, c):
                m = b * 2 * NP + 2 * p + c
                half = 2 * AD
                dve.wait_ge(o_ps, b * NP * NS + p * NS + (4 if c == 0 else NS))
                wait(dve, oT_ready, m)
                dve.reciprocal(rden[0:half, :], psum[half:P, 4 + c, :]).then_inc(rden_ready, 1)
                dve.wait_ge(rden_ready, m + 1)
                r = (p % 2) * half
                dve.tensor_tensor(oT[r:r + half, p // 2, c * CH:(c + 1) * CH], psum[0:half, 4 + c, :], rden[0:half, :], ALU.mult).then_inc(oT_ready, 1)

            def outputs(b):
                for t in range(NT):
                    dve.wait_ge(y_ps, b * NT + t + 1)
                    dve.wait_ge(xr_ready, b * NT + t + 1)
                    dve.tensor_tensor(xr[:, t % RING, :], psum[:, 4 + t % 2, :], xr[:, t % RING, :], ALU.add).then_inc(y_ready, 1)

            def batch(b, first):
                if not first:
                    outputs(b - 1)
                for t in range(NT):
                    k = b * NT + t + 1
                    dve.wait_ge(qk_sq, k)
                    wait(dve, ms3_ready, k - 1)
                    dve.tensor_reduce(ss3, sq.rearrange("p (h d) -> p h d", d=AD), AX.X, ALU.add).then_inc(ss3_ready, 1)
                    dve.wait_ge(qk_raw, k)
                    dve.wait_ge(rs3_ready, k)
                    dve.tensor_tensor(qk3, qk3, rs3.unsqueeze(2).to_broadcast([P, 2 * AH, AD]), ALU.mult).then_inc(scaled, 1)
                    dve.wait_ge(scaled, k)
                    if t == 0:
                        wait(dve, stack_ready, b * NP * 2)
                    tile = roped[:, t, :].rearrange("p (w h d) -> p w h d", w=2, d=AD)
                    for w in range(2):
                        last = dve.tensor_tensor(tile[:, w], qk4[:, w], cosG[:, t, w, :].unsqueeze(1).to_broadcast([P, AH, AD]), ALU.mult)
                    last.then_inc(cosed, 1)
                    dve.wait_ge(rotated, k)
                    dve.wait_ge(cosed, k)
                    dve.tensor_tensor(roped[:, t, :], roped[:, t, :], rot, ALU.add).then_inc(roped_ready, 1)
                for t in range(NT):
                    for u in BESIDE_V[t]:
                        user(b, 0, *u)
                for p in range(NP):
                    for n in range(NS):
                        if p + 1 < NP:
                            for u in BESIDE_STEP[n]:
                                user(b, p + 1, *u)
                        if n == 1 and p > 0:
                            finish(b, p - 1, 1)
                        if n == 5:
                            finish(b, p, 0)
                    if p == NP - 2:
                        norms(b + 1)
                finish(b, NP - 1, 1)

            norms(0)
            batch(0, True)
            with dve.Fori(1, B) as b:
                batch(b, False)
            outputs(B - 1)



STEPS = [(c, j) for c in range(T // CH) for j in range((c + 1) * CH // P)]
NS = len(STEPS)
TURNS = [(w, h, half) for half in range(2) for h in range(2) for w in range(2)]
PIECES = [(t, c, h) for t in range(NT) for c in range(t // 4 + 1) for h in range(2)]
_T, _M = [("turn", a) for a in TURNS], [("max", a) for a in PIECES]
USERS = _T[:4] + _M[:2] + _T[4:6] + _M[2:4] + _T[6:] + _M[4:] + [("top", None)]


def dealt(counts):
    out, at = [], 0
    for n in counts:
        out.append(USERS[at:at + n])
        at += n
    assert at == len(USERS)
    return out


BESIDE_V = dealt([5, 5, 5, 5, 4, 4, 4, 1])
BESIDE_STEP = dealt([2, 3, 4, 4, 4, 4, 4, 4, 3, 1, 0, 0])

_INS = ["L0_attn_x", "L0_attn_w_qkv", "L0_attn_w_out", "L0_attn_q_gamma", "L0_attn_k_gamma", "L0_ffn_w_router",
        "L0_ffn_wq", "L0_ffn_bq", "L0_ffn_wk", "L0_ffn_bk", "L0_ffn_wv", "L0_ffn_bv", "L0_ffn_wo",
        "L0_ffn_w_gate", "L0_ffn_w_up", "L0_ffn_w_down", "L0_ffn_ln1_w", "L0_ffn_ln2_w"]


def shape_constants():
    import numpy as np
    p = np.arange(P)[:, None]
    const = np.zeros((P, C_W), np.float32)
    const[:, C_ID:C_ID + P] = np.eye(P)
    const[:, C_ONE:C_ONE + P] = 1
    const[:, C_MASK + CH - P:C_MASK + CH] = np.where(np.arange(P)[None] <= p, 0, MASKED)
    const[:, C_TRI:C_TRI + P] = p < np.arange(P)[None]
    const[:, C_IOTA:C_IOTA + P] = np.arange(P)[None] + 1
    const[:, C_TIE:] = np.arange(TIE_W)[None] < T - P + p

    def angles(width):
        e = np.arange(0, width, 2, dtype=np.float32) / np.float32(width)
        inv = (np.float32(1) / np.power(np.float32(10000.0), e)).astype(np.float32)
        a = np.arange(T, dtype=np.float32)[:, None] * inv[None]
        return np.cos(a).astype(np.float32), np.sin(a).astype(np.float32)

    c, sn = angles(AD)
    rope = np.concatenate([c, c, -sn, sn], 1)
    c, sn = angles(FD)
    frope = np.concatenate([c, c, sn, -sn], 1)
    return {"const": const, "rope": rope, "frope": frope}


def kernel(**inputs):
    import numpy as _np
    import concourse.bacc as _bacc
    from concourse import mybir as _mybir
    from concourse.bass_utils import run_bass_kernel_spmd as _run

    nc = _bacc.Bacc("TRN2", target_bir_lowering=False, num_devices=1)
    arrays, args = {}, []
    given = {n: _np.ascontiguousarray(inputs[n]) for n in _INS}
    given.update(shape_constants())
    for name, a in given.items():
        arrays[f"in_{name}"] = a
        args.append(nc.dram_tensor(f"in_{name}", a.shape, _mybir.dt.from_np(a.dtype), kind="ExternalInput").ap())
    args.append(nc.dram_tensor("out_y", (B, T, D), _mybir.dt.float32, kind="ExternalOutput").ap())
    build(nc, *args)
    r = _run(nc, [arrays], core_ids=[0])
    return r.results[0]["out_y"]
```

```python
import concourse.bass as bass
from concourse import mybir
from contextlib import ExitStack

P = 128
B, T, D = 4, 1024, 512
NT = T // P
KD = D // P
AH, AD = 16, 32
HG = P // AD
NG = AH // HG
FH, FKV, FD = 16, 8, 128
REP = FH // FKV
SEL = T // 8
S = B * SEL
ST = S // P
FI = 2048
NC = FI // P
CH = 512
LN_EPS, RMS_EPS = 1e-5, 1e-6
NP = AH // 2
STK = 3 * AD
RH = STK
SLOTS = 4
MASKED = -1e30

C_ID, C_ONE, C_MASK, C_TRI, C_IOTA, C_TIE = 0, 128, 256, 768, 896, 1024
C_W = C_TIE + P
FT_W = 4 * (FD // 2)


def build(nc, x_d, w_qkv_d, w_out_d, qg_d, kg_d, wr_d, wq_d, bq_d, wk_d, bk_d, wv_d, bv_d, wo_d,
          wg_d, wu_d, wd_d, ln1_d, ln2_d, const_d, rope_d, frope_d, out_d):
    f32, f32r, bf16 = mybir.dt.float32, mybir.dt.float32r, mybir.dt.bfloat16
    ALU, ACT, AX = mybir.AluOpType, mybir.ActivationFunctionType, mybir.AxisListType

    x_v = x_d.rearrange("b (t p) d -> b p t d", p=P)
    out_v = out_d.rearrange("b (t p) d -> b p t d", p=P)
    wqkv_v = w_qkv_d.rearrange("(k p) n -> p k n", p=P)
    wout_v = w_out_d.rearrange("(k p) n -> p k n", p=P)
    wq_v = wq_d.rearrange("(k p) (n c) -> n p k c", p=P, c=REP * FD)
    wk_v = wk_d.rearrange("(k p) (n c) -> n p k c", p=P, c=FD)
    wv_v = wv_d.rearrange("(k p) (n c) -> n p k c", p=P, c=FD)
    wo_v = wo_d.rearrange("(n r p) d -> n p r d", p=P, r=REP)
    wg_v = wg_d.rearrange("(k p) (n c) -> n p k c", p=P, c=P)
    wu_v = wu_d.rearrange("(k p) (n c) -> n p k c", p=P, c=P)
    wd_v = wd_d.rearrange("(n p) d -> n p d", p=P)

    ctx = ExitStack()
    with ctx:
        ARENA = 53200 - 8 * T - 4 * NT * STK - P
        arena = ctx.enter_context(nc.sbuf_tensor("arena", [P, ARENA], f32))
        qS = [ctx.enter_context(nc.sbuf_tensor(f"q_stack{i}", [P, 2, T], f32r)) for i in range(2)]
        kS = [ctx.enter_context(nc.sbuf_tensor(f"k_stack{i}", [P, 2, T], f32r)) for i in range(2)]
        stack = ctx.enter_context(nc.sbuf_tensor("stack", [P, 2, NT, 2 * STK], f32r))
        ident_r = ctx.enter_context(nc.sbuf_tensor("ident_r", [P, P], f32r))
        psum = ctx.enter_context(nc.psum_tensor("psum", [P, 8, 512], f32))

        def sem(name):
            return ctx.enter_context(nc.semaphore(name))

        class Place:
            def __init__(self, at, end):
                self.at, self.end = at, end

            def f(self, *shape):
                n = 1
                for s in shape:
                    n *= s
                a = arena[:, self.at:self.at + n]
                self.at += n
                assert self.at <= self.end, (self.at, self.end)
                if len(shape) == 2:
                    a = a.rearrange("p (a b) -> p a b", b=shape[1])
                if len(shape) == 3:
                    a = a.rearrange("p (a b c) -> p a b c", b=shape[1], c=shape[2])
                return a

            def h(self, *shape):
                n = 1
                for s in shape:
                    n *= s
                a = arena[:, self.at:self.at + n // 2].bitcast(bf16)
                self.at += n // 2
                assert self.at <= self.end, (self.at, self.end)
                if len(shape) == 2:
                    a = a.rearrange("p (a b) -> p a b", b=shape[1])
                return a

        keep = Place(0, ARENA)
        ident = keep.f(P)
        ones = keep.f(P)
        mask = keep.f(CH)
        onehotT = keep.h(B, T)
        delta = keep.f(B, D)
        ln_mean = keep.f(B, NT)
        ln_rstd = keep.f(B, NT)
        half_neg = keep.f(32)
        cosG = keep.f(NT, 2, AD)
        sinG = keep.f(NT, 2, AD)
        w_qkv_at = keep.at
        w_qkv = keep.f(KD, 3 * D)
        w_out_at = keep.at
        w_out = keep.f(KD, D)
        rest = keep.at

        p1 = Place(w_out_at, ARENA)
        x_all = p1.f(B * NT, D)
        x_end = p1.at
        xsel = p1.f(ST, D)
        tabsel = p1.f(ST, FT_W + 1)
        rest2 = p1.at
        tab = p1.f(NT, FT_W + 1)
        s_row = p1.f(T)
        onehot = p1.f(NT, P)
        junk1 = p1.h(2, T)
        wr_b = p1.f(D)
        cst1 = p1.f(C_W - C_TRI)
        tri = cst1[:, 0:P]
        iota1 = cst1[:, C_IOTA - C_TRI:C_IOTA - C_TRI + P]
        tie = cst1[:, C_TIE - C_TRI:]
        gam = p1.f(2, AD)
        rope_raw = p1.f(NT, 2 * AD)
        stats = p1.f(NT, 6)
        mv = p1.f(NT, 2)
        vpe = p1.f(NT)
        rstd1 = p1.f(NT)
        s_col = p1.f(NT)
        above = p1.f(NT)
        earlier = p1.f(NT)
        tied = p1.f(NT)
        rank = p1.f(NT)
        chosen = p1.f(NT)
        slot = p1.f(NT)

        p2 = Place(rest, x_end)
        hn = p2.f(ST, D)
        hT = p2.f(KD, S)
        x1 = p2.f(ST, D)
        mlp_at = p2.at
        prob2 = p2.f(REP * ST, S)
        probT2 = [p2.f(ST, S) for _ in range(REP)]
        mlp_end = p2.at
        p2 = Place(rest2, ARENA)
        cosT = p2.f(S)
        sinT = p2.f(S)
        bias_rows = prob2[:, 1, 0:FD]
        biasT = p2.f(FH + FKV)
        bv_b = p2.f(FKV * FD)
        ln1_b = prob2[:, 0, :]
        ln2_b = p2.f(D)
        p2w = Place(w_qkv_at, w_out_at)
        wq_s = [p2w.f(KD, REP * FD) for _ in range(2)]
        wk_s = [p2w.f(KD, FD) for _ in range(2)]
        wv_s = [p2w.f(KD, FD) for _ in range(2)]
        wo_s = [p2w.f(REP, D) for _ in range(2)]
        raw = p2.f(2, S)
        rotd = p2.f(S)
        qT2 = p2.f(REP, S)
        kT2 = p2.f(S)
        v2 = p2.f(ST, FD)
        oT2 = p2.f(REP, S)
        ss2 = p2.f(ST)
        ms2 = p2.f(ST)
        rs2 = p2.f(ST)
        nmax2 = p2.f(REP * ST)
        den2 = p2.f(REP * ST)
        rden2 = p2.f(REP * ST)
        gate = p2.f(ST)
        egate = p2.f(ST)
        dgate = p2.f(ST)
        p2m = Place(mlp_at, mlp_end)
        wg_s = [p2m.f(KD, P) for _ in range(2)]
        wu_s = [p2m.f(KD, P) for _ in range(2)]
        wd_s = [p2m.f(D) for _ in range(2)]
        eg = p2m.f(2, S)
        sg = p2m.f(2, S)
        aT = p2m.f(2, S)
        zrow = p2m.f(D)

        p3 = Place(rest, ARENA)
        xn = p3.f(NT, D)
        xnT = p3.f(KD, T)
        probT = xnT.rearrange("p k n -> p (k n)").rearrange("p (s h n) -> p s h n", s=SLOTS, h=2)
        roped = p3.f(NT, 2 * D)
        v = p3.f(NT, D)
        oT = p3.f(NG, T)
        xr = xnT.rearrange("p k n -> p (k n)").rearrange("p (t d) -> p t d", d=D)
        qk = p3.f(2 * D)
        ohT = p3.f(T)
        rot = ohT
        top = p3.f(2, 2 * NT)
        top_rows = p3.f(2, P)
        ss3 = p3.f(2 * AH)
        ms3 = p3.f(2 * AH)
        rs3 = p3.f(2, 2 * AH)
        past_top = p3.f(4)
        rden = p3.f(CH)
        rden_t = p3.f(CH // 32)
        out_scale = p3.f(NT)
        out_shift = p3.f(NT)
        assert p3.at <= ARENA

        consts_in = sem("consts_in")
        consts1_in = sem("consts1_in")
        x_in = sem("x_in")
        late_in = sem("late_in")
        gam_ready = sem("gam_ready")
        rope_ready = sem("rope_ready")
        p1_stats = sem("p1_stats")
        p1_vpe = sem("p1_vpe")
        p1_rstd = sem("p1_rstd")
        p1_norm = sem("p1_norm")
        p1_score = sem("p1_score")
        p1_row_ps = sem("p1_row_ps")
        p1_row = sem("p1_row")
        p1_cnt = sem("p1_cnt")
        p1_rank = sem("p1_rank")
        p1_chosen = sem("p1_chosen")
        p1_pos = sem("p1_pos")
        p1_slot = sem("p1_slot")
        p1_onehot = sem("p1_onehot")
        p1_tab = sem("p1_tab")
        p1_tab_score = sem("p1_tab_score")
        p1_gather_ps = sem("p1_gather_ps")
        p1_gathered = sem("p1_gathered")
        p1_mean = sem("p1_mean")
        init_done = sem("init_done")
        f_const_in = sem("f_const_in")
        w2_in0 = sem("w2_in0")
        w2_in1 = sem("w2_in1")
        ss2_ready = sem("ss2_ready")
        ms2_ready = sem("ms2_ready")
        rs2_ready = sem("rs2_ready")
        h_ready = sem("h_ready")
        hT_ps = sem("hT_ps")
        hT_ready = sem("hT_ready")
        tabT_ps = sem("tabT_ps")
        tabT_ready = sem("tabT_ready")
        bias_ps = sem("bias_ps")
        biasT_ready = sem("biasT_ready")
        proj_ps = sem("proj_ps")
        proj_out = sem("proj_out")
        raw_used = sem("raw_used")
        rope_a = sem("rope_a")
        rope_b = sem("rope_b")
        rope_done = sem("rope_done")
        v2_ready = sem("v2_ready")
        s2_ps = sem("s2_ps")
        s2_low = sem("s2_low")
        s2_exp = sem("s2_exp")
        s2_den = sem("s2_den")
        s2_prob = sem("s2_prob")
        pT2_ps = sem("pT2_ps")
        pT2_ready = sem("pT2_ready")
        o2_ps = sem("o2_ps")
        o2_ready = sem("o2_ready")
        wo_ps = sem("wo_ps")
        x1_ready = sem("x1_ready")
        wm_in0 = sem("wm_in0")
        wm_in1 = sem("wm_in1")
        gu_ps = sem("gu_ps")
        eg_ready = sem("eg_ready")
        sg_1 = sem("sg_1")
        sg_2 = sem("sg_2")
        sg_3 = sem("sg_3")
        aT_ready = sem("aT_ready")
        wm_free = sem("wm_free")
        zero_ready = sem("zero_ready")
        mlp_ps = sem("mlp_ps")
        delta_a = sem("delta_a")
        delta_b = sem("delta_b")
        delta_done = sem("delta_done")
        gate_1 = sem("gate_1")
        gate_2 = sem("gate_2")
        gate_3 = sem("gate_3")
        xb_in = sem("xb_in")
        xn_ready = sem("xn_ready")
        xnT_ps = sem("xnT_ps")
        xnT_ready = sem("xnT_ready")
        qk_ps = sem("qk_ps")
        qk_sq = sem("qk_sq")
        ss3_ready = sem("ss3_ready")
        ms3_ready = sem("ms3_ready")
        rs3_ready = sem("rs3_ready")
        scaled = sem("scaled")
        rotated = sem("rotated")
        cosed = sem("cosed")
        roped_ready = sem("roped_ready")
        v_ps = sem("v_ps")
        v_ready = sem("v_ready")
        hi_ready = [sem("q_hi_ready"), sem("k_hi_ready")]
        lo_ready = [sem("q_lo_ready"), sem("k_lo_ready")]
        ident_ready = sem("ident_ready")
        stackT_ps = sem("stackT_ps")
        stackT_ready = sem("stackT_ready")
        m_ps = sem("m_ps")
        m_seen = sem("m_seen")
        topT_ps = sem("topT_ps")
        toprow_ready = sem("toprow_ready")
        row_in = [sem(f"row_in{half}") for half in range(2)]
        sc_ps = sem("sc_ps")
        sc_exp = sem("sc_exp")
        sc_masked = sem("sc_masked")
        o_ps = sem("o_ps")
        den_turned = sem("den_turned")
        rden_ready = sem("rden_ready")
        rden_turned = sem("rden_turned")
        oT_ready = sem("oT_ready")
        kones_ready = sem("kones_ready")
        shift_ready = sem("shift_ready")
        scale_ready = sem("scale_ready")
        hi2_ready = sem("hi2_ready")
        xr_ready = sem("xr_ready")
        oh_ready = sem("oh_ready")
        y_ps = sem("y_ps")
        y_ready = sem("y_ready")
        xr_in = [sem(f"xr_in{i}") for i in range(SLOTS)]
        out_done = [sem(f"out_done{i}") for i in range(SLOTS)]

        def wait(eng, semaphore, value):
            if not isinstance(value, int) or value > 0:
                eng.wait_ge(semaphore, value)

        passed = {e.engine: sem(f"passed_{n}") for n, e in (("sync", nc.sync), ("gpsimd", nc.gpsimd), ("vector", nc.vector))}

        def wait_apart(eng, semaphore, value):
            if isinstance(value, int):
                wait(eng, semaphore, value)
            else:
                eng.wait_ge(semaphore, value)
                eng.sem_inc(passed[eng.engine], 1)

        block = ctx.enter_context(nc.Block())

        @block.sync
        def _(sp):
            sp.dma_start(arena[:, 0:C_TRI], const_d[:, 0:C_TRI]).then_inc(consts_in, 16)
            sp.dma_start(cst1, const_d[:, C_TRI:C_W]).then_inc(consts1_in, 16)
            sp.dma_start(wr_b, wr_d.partition_broadcast(P)).then_inc(consts1_in, 16)
            with sp.Fori(0, B) as b:
                sp.dma_start(x_all[:, bass.ds(b * NT, NT), :], x_v[bass.ds(b, 1), :, :, :].rearrange("b p t d -> p (b t) d")).then_inc(x_in, 16)
                wait_apart(sp, x_in, b * 16 + 16)
            sp.wait_ge(p1_gathered, 3 * B + 1)
            sp.wait_ge(rope_ready, 3)
            sp.wait_ge(p1_mean, 2 * B + 1)
            sp.dma_start(w_out, wout_v).then_inc(late_in, 16)
            sp.dma_start(bias_rows[0:FH, :], bq_d.rearrange("(h d) -> h d", d=FD)).then_inc(f_const_in, 16)
            sp.dma_start(bias_rows[FH:FH + FKV, :], bk_d.rearrange("(h d) -> h d", d=FD)).then_inc(f_const_in, 16)
            sp.dma_start(bv_b, bv_d.partition_broadcast(P)).then_inc(f_const_in, 16)
            sp.dma_start(ln1_b, ln1_d.partition_broadcast(P)).then_inc(f_const_in, 16)
            sp.dma_start(ln2_b, ln2_d.partition_broadcast(P)).then_inc(f_const_in, 16)
            def load_heads(n, u):
                for dst, src in ((wq_s, wq_v), (wk_s, wk_v), (wv_s, wv_v), (wo_s, wo_v)):
                    sp.dma_start(dst[u], src[bass.ds(n, 1), :, :, :].rearrange("n p k c -> p (n k) c")).then_inc((w2_in0, w2_in1)[u], 16)

            for u in range(2):
                load_heads(u, u)
            with sp.Fori(1, FKV // 2) as i:
                for u in range(2):
                    sp.wait_ge(wo_ps, i * (2 * ST) + (u - 1) * ST + 1)
                    load_heads(i * 2 + u, u)

            def load_mlp(n, u):
                filled = (wm_in0, wm_in1)[u]
                for dst, src in ((wg_s, wg_v), (wu_s, wu_v)):
                    sp.dma_start(dst[u], src[bass.ds(n, 1), :, :, :].rearrange("n p k c -> p (n k) c")).then_inc(filled, 16)
                sp.dma_start(wd_s[u], wd_v[bass.ds(n, 1), :, :].rearrange("n p c -> p (n c)")).then_inc(filled, 16)

            sp.wait_ge(pT2_ready, FKV * REP * ST)
            sp.wait_ge(o2_ps, FKV * REP + 1)
            for u in range(2):
                load_mlp(u, u)
            sp.wait_ge(wo_ps, FKV * ST + 1)
            sp.dma_start(w_qkv, wqkv_v).then_inc(late_in, 16)
            with sp.Fori(1, NC // 2) as i:
                for u in range(2):
                    sp.wait_ge(wm_free, i * 2 + u - 1 + 1)
                    load_mlp(i * 2 + u, u)
            sp.wait_ge(delta_done, ST)
            sp.dma_start(xn, x_v[0, :, :, :]).then_inc(xb_in, 16)

            def batch(b, first):
                sp.wait_ge(xnT_ps, b * NT + NT)
                nb = (b + 1) % B
                sp.dma_start(xn, x_v[bass.ds(nb, 1), :, :, :].rearrange("b p t d -> p (b t) d")).then_inc(xb_in, 16)
                if not first:
                    sp.wait_ge(v_ps, b * NT + NT)
                    outputs(b - 1)
                for p in range(NP):
                    for half in range(2):
                        sp.wait_ge(toprow_ready, (b * NP + p) * 2 + half + 1)
                        sp.dma_start(qS[p % 2][RH:RH + 1, half, :].bitcast(f32), top_rows[0:NT, half, :]).then_inc(row_in[half], 16)

            def outputs(b):
                for i in range(SLOTS):
                    sp.dma_start(xr[:, 2 * i:2 * i + 2, :], x_v[bass.ds(b, 1), :, 2 * i:2 * i + 2, :].rearrange("b p t d -> p (b t) d")).then_inc(xr_in[i], 16)
                for i in range(SLOTS):
                    sp.wait_ge(y_ready, b * NT + 2 * i + 2)
                    sp.dma_start(out_v[bass.ds(b, 1), :, 2 * i:2 * i + 2, :].rearrange("b p t d -> p (b t) d"), xr[:, 2 * i:2 * i + 2, :]).then_inc(out_done[i], 16)

            batch(0, True)
            with sp.Fori(1, B) as b:
                batch(b, False)
            sp.wait_ge(o_ps, B * NP * NS)
            outputs(B - 1)
            sp.wait_ge(xb_in, 16 * (B + 1))
            for i in range(SLOTS):
                sp.wait_ge(out_done[i], B * 16)

        @block.gpsimd
        def _(pool):
            for started in (p1_mean,):
                pool.sem_inc(started, 1)
            pool.memset(half_neg, -0.5).then_inc(init_done, 1)
            pool.dma_start(gam[:, 0, :], qg_d.partition_broadcast(P)).then_inc(gam_ready, 16)
            pool.dma_start(gam[:, 1, :], kg_d.partition_broadcast(P)).then_inc(gam_ready, 16)
            pool.dma_start(rope_raw, rope_d.rearrange("(t p) c -> p t c", p=P)).then_inc(gam_ready, 16)
            pool.dma_start(tab[:, :, 0:FT_W], frope_d.rearrange("(t p) c -> p t c", p=P)).then_inc(p1_tab, 16)
            pool.wait_ge(init_done, 1)
            with pool.Fori(0, B) as b:
                wait_apart(pool, p1_stats, b * 2 * NT + 2 * NT)
                pool.tensor_scalar(vpe, mv[:, :, 1], LN_EPS, None, ALU.add).then_inc(p1_vpe, 1)
                pool.wait_ge(p1_vpe, b + 1)
                pool.tensor_tensor(rstd1, vpe, half_neg[:, 0:NT], ALU.pow).then_inc(p1_rstd, 1)
                wait_apart(pool, p1_rstd, b + 1)
                pool.tensor_copy(ln_mean[:, bass.ds(b, 1), :].rearrange("p b t -> p (b t)"), mv[:, :, 0]).then_inc(p1_mean, 1)
                pool.tensor_copy(ln_rstd[:, bass.ds(b, 1), :].rearrange("p b t -> p (b t)"), rstd1).then_inc(p1_mean, 1)
            pool.wait_ge(gam_ready, 48)
            for w in range(2):
                g = gam[:, w, :]
                gb = g.unsqueeze(1).to_broadcast([P, NT, AD])
                scale = AD ** -0.5 if w == 0 else 1.0
                pool.tensor_tensor(cosG[:, :, w, :], rope_raw[:, :, 0:AD], gb, ALU.mult).then_inc(rope_ready, 1)
                for h in range(2):
                    o = h * (AD // 2)
                    gr = g[:, AD // 2 - o:AD - o].unsqueeze(1).to_broadcast([P, NT, AD // 2])
                    last = pool.tensor_tensor(sinG[:, :, w, o:o + AD // 2], rope_raw[:, :, AD + o:AD + o + AD // 2], gr, ALU.mult)
                last.then_inc(rope_ready, 1)
            pool.wait_ge(rope_ready, 4)
            pool.tensor_scalar(cosG[:, :, 0, :], cosG[:, :, 0, :], AD ** -0.5, None, ALU.mult)
            pool.tensor_scalar(sinG[:, :, 0, :], sinG[:, :, 0, :], AD ** -0.5, None, ALU.mult).then_inc(rope_ready, 1)
            for n in range(2):
                pool.wait_ge(ss2_ready, ST * (n + 1))
                pool.tensor_scalar(ms2, ss2, 1.0 / D, RMS_EPS, ALU.mult, ALU.add).then_inc(ms2_ready, 1)
                pool.wait_ge(ms2_ready, n + 1)
                pool.tensor_tensor(rs2, ms2, half_neg[:, 0:ST], ALU.pow).then_inc(rs2_ready, 1)
            pool.wait_ge(delta_done, ST)
            for i in range(2):
                pool.memset(kS[i][RH:RH + 1, :, :].bitcast(f32), 1.0).then_inc(kones_ready, 1)
            qk4 = qk.rearrange("p (w h d) -> p w h d", w=2, d=AD)
            rot4 = rot.rearrange("p (w h d) -> p w h d", w=2, d=AD)

            def outputs(b):
                mean = ln_mean[:, bass.ds(b, 1), :].rearrange("p b t -> p (b t)")
                rstd = ln_rstd[:, bass.ds(b, 1), :].rearrange("p b t -> p (b t)")
                pool.tensor_tensor(out_shift, mean, rstd, ALU.mult).then_inc(shift_ready, 1)
                pool.tensor_copy(out_scale, rstd).then_inc(scale_ready, 1)
                wait_apart(pool, scale_ready, b * 2 + 1)
                wait_apart(pool, shift_ready, b * 2 + 1)
                pool.tensor_scalar(out_scale, out_scale, 1.0, None, ALU.add).then_inc(scale_ready, 1)
                pool.tensor_scalar(out_shift, out_shift, -1.0, None, ALU.mult).then_inc(shift_ready, 1)

            def build(b, p):
                q = b * NP + p
                wait_apart(pool, stackT_ps, q * 8)
                if p == 0:
                    wait_apart(pool, roped_ready, b * NT + NT)
                for w in range(1 if p == 0 else 2):
                    src = roped[:, :, w * D + p * 2 * AD:w * D + (p + 1) * 2 * AD].rearrange("p t (h d) -> p t h d", h=2)
                    st = stack[:, w].rearrange("p t (h c) -> p t h c", h=2)
                    lo = 2 * AD if w else AD
                    for h in range(2):
                        pool.tensor_copy(st[:, :, h, 0:AD], src[:, :, h]).then_inc(hi_ready[w], 1)
                    wait_apart(pool, hi_ready[w], q * 2 + 2)
                    for h in range(2):
                        last = pool.tensor_tensor(st[:, :, h, lo:lo + AD], src[:, :, h], st[:, :, h, 0:AD].bitcast(f32), ALU.subtract)
                    last.then_inc(lo_ready[w], 1)

            def batch(b, first):
                if not first:
                    outputs(b - 1)
                def inverse_rms(t):
                    k = b * NT + t + 1
                    wait_apart(pool, ss3_ready, k)
                    if t >= 1:
                        wait_apart(pool, rs3_ready, k - 1)
                    if t >= 2:
                        wait_apart(pool, scaled, k - 2)
                    pool.tensor_scalar(ms3, ss3, 1.0 / AD, RMS_EPS, ALU.mult, ALU.add).then_inc(ms3_ready, 1)
                    pool.wait_ge(ms3_ready, k)
                    pool.tensor_tensor(rs3[:, t % 2, :], ms3, half_neg, ALU.pow).then_inc(rs3_ready, 1)

                inverse_rms(0)
                for t in range(NT):
                    k = b * NT + t + 1
                    if t + 1 < NT:
                        inverse_rms(t + 1)
                    pool.wait_ge(scaled, k)
                    wait(pool, roped_ready, k - 1)
                    for h in range(2):
                        o = h * (AD // 2)
                        sn = sinG[:, t, 0, o:o + AD // 2].unsqueeze(1).to_broadcast([P, AH, AD // 2])
                        last = pool.tensor_tensor(rot4[:, 0, :, o:o + AD // 2], qk4[:, 0, :, AD // 2 - o:AD - o], sn, ALU.mult)
                    last.then_inc(rotated, 1)
                build(b, 0)
                build(b, 1)
                for p in range(NP):
                    for n, (c, j) in enumerate(STEPS):
                        if j >= 4 * c:
                            k = p * NS + n
                            wait_apart(pool, sc_exp, 2 * (b * NP * NS + k + 1))
                            blk = probT[:, k % SLOTS, :, (j - 4 * c) * P:(j - 4 * c + 1) * P]
                            pool.affine_select(out=blk, in_=blk, compare_op=ALU.is_ge, fill=0.0, base=0,
                                               pattern=[[0, 2], [1, P]], channel_multiplier=-1).then_inc(sc_masked, 1)
                        if n == BUILD_STEP and p + 2 < NP:
                            build(b, p + 2)

            batch(0, True)
            with pool.Fori(1, B) as b:
                batch(b, False)
            outputs(B - 1)

        @block.scalar
        def _(act):
            def out_pT(n, m):
                h, t = m // ST, m % ST
                act.wait_ge(pT2_ps, n * 8 + m + 1 + 1)
                act.activation(probT2[h][:, 0:t + 1, t * P:(t + 1) * P],
                               psum[:, 4 + m % 2, 0:(t + 1) * P].rearrange("p (j n) -> p j n", n=P), ACT.Copy).then_inc(pT2_ready, 1)

            for started in (p1_gathered, proj_out):
                act.sem_inc(started, 1)
            with act.Fori(0, B) as b:
                act.wait_ge(p1_row_ps, b + 1)
                act.activation(s_row, psum[:, 0:2, :].rearrange("p a n -> p (a n)"), ACT.Copy).then_inc(p1_row, 1)
                act.wait_ge(p1_gather_ps, b * 3 + 1)
                act.activation(xsel[:, bass.ds(b, 1), :].rearrange("p b d -> p (b d)"), psum[:, 3, :], ACT.Copy).then_inc(p1_gathered, 1)
                act.wait_ge(p1_gather_ps, b * 3 + 2)
                act.activation(tabsel[:, bass.ds(b, 1), :].rearrange("p b d -> p (b d)"), psum[:, 4, 0:FT_W + 1], ACT.Copy).then_inc(p1_gathered, 1)
                act.wait_ge(p1_gather_ps, b * 3 + 3)
                act.activation(onehotT[:, bass.ds(b, 1), :].rearrange("p b t -> p (b t)"),
                               psum[:, 5:7, :].rearrange("p a n -> p (a n)"), ACT.Copy).then_inc(p1_gathered, 1)
            act.wait_ge(p1_gathered, 3 * B + 1)
            act.activation(egate, tabsel[:, :, FT_W], ACT.Exp, scale=-1.0).then_inc(gate_1, 1)

            def turn_h(n):
                for t in range(ST):
                    act.wait_ge(hT_ps, n * ST + t + 1)
                    act.activation(hT[:, :, t * P:(t + 1) * P], psum[:, t, :].rearrange("p (k n) -> p k n", k=KD), ACT.Copy).then_inc(hT_ready, 1)

            turn_h(0)
            act.wait_ge(tabT_ps, 1)
            act.activation(cosT, psum[:, 4, :], ACT.Copy).then_inc(tabT_ready, 1)
            act.activation(sinT, psum[:, 5, :], ACT.Copy).then_inc(tabT_ready, 1)
            act.wait_ge(bias_ps, 1)
            act.activation(biasT, psum[:, 6, 0:FH + FKV], ACT.Copy).then_inc(biasT_ready, 1)
            act.wait_ge(biasT_ready, 1)
            with act.Fori(0, FKV // 2) as i:
                for u in range(2):
                    n = i * 2 + u
                    for r in range(REP + 1):
                        act.wait_ge(proj_ps, n * 4 + r + 1)
                        if r == 0:
                            act.wait_ge(rope_done, n * 3 + 1)
                        if r == 2:
                            act.wait_ge(rope_done, n * 3 + 1 + 1)
                        bcol = biasT[:, bass.ds(n * REP + r, 1)] if r < REP else biasT[:, bass.ds(n + FH, 1)]
                        act.activation(raw[:, r % 2, :], psum[:, r % 2, :], ACT.Identity, bias=bcol).then_inc(proj_out, 1)
                    for m in range(REP * ST):
                        w = (m % ST + 1) * P
                        act.wait_ge(s2_low, n * 8 + m + 1)
                        act.activation(prob2[:, m, 0:w], prob2[:, m, 0:w], ACT.Exp, bias=nmax2[:, m:m + 1], scale=-1.0,
                                       accum_out=den2[:, m:m + 1]).then_inc(s2_exp, 1)
                        if m >= 2:
                            out_pT(n, m - 2)
                    out_pT(n, 6)
                    out_pT(n, 7)
            turn_h(1)
            with act.Fori(0, NC // 2) as i:
                for u in range(2):
                    act.wait_ge(gu_ps, i * 4 + 2 * u + 1)
                    act.wait_ge(sg_3, i * 2 + 1)
                    act.activation(eg[:, u, :], psum[:, 2 * u, :], ACT.Exp, scale=-1.0).then_inc(eg_ready, 1)
            act.wait_ge(delta_done, ST)
            act.activation(ident_r[:, :], ident, ACT.Copy).then_inc(ident_ready, 1)
            sq = psum[:, 6:8, :].rearrange("p a n -> p (a n)")

            def user(b, p, kind, arg):
                q = b * NP + p
                bank = BANK[USERS.index((kind, arg))]
                if kind == "turn":
                    w, h, half = arg
                    n = TURNS.index(arg)
                    if n == 0:
                        wait(act, sc_ps, 2 * (q - 1) * NS)
                        wait(act, m_ps, (q - 1) * len(PIECES))
                    act.wait_ge(stackT_ps, q * 8 + n + 1)
                    dst = kS[p % 2][0:RH, h, half * CH:(half + 1) * CH] if w else qS[p % 2][0:RH, half, h * CH:(h + 1) * CH]
                    act.activation(dst, psum[0:RH, bank, :], ACT.Copy).then_inc(stackT_ready, 1)
                if kind == "top":
                    act.wait_ge(topT_ps, q * 2 + arg + 1)
                    wait(act, row_in[arg], q * 16)
                    act.activation(top_rows[0:NT, arg, :].bitcast(f32r), psum[0:NT, bank, 0:P], ACT.Copy, scale=-1.0).then_inc(toprow_ready, 1)

            def repeat_hi(b, p, w):
                q = b * NP + p
                st = stack[:, w].rearrange("p t (h c) -> p t h c", h=2)
                act.wait_ge(hi_ready[w], q * 2 + 2)
                second = AD if w else 2 * AD
                for h in range(2):
                    last = act.activation(st[:, :, h, second:second + AD], st[:, :, h, 0:AD].bitcast(f32), ACT.Copy)
                last.then_inc(hi2_ready, 1)

            def copy_v(b, t):
                act.wait_ge(v_ps, b * NT + t + 1)
                act.activation(v[:, t, :], psum[:, 4 + t % 2, :], ACT.Copy).then_inc(v_ready, 1)

            def output(b, t, made):
                if t == 0:
                    act.wait_ge(roped_ready, made * NT)
                    act.activation(ohT, onehotT[:, bass.ds(b, 1), :].rearrange("p b t -> p (b t)"), ACT.Copy).then_inc(oh_ready, 1)
                    act.wait_ge(scale_ready, b * 2 + 2)
                    act.wait_ge(shift_ready, b * 2 + 2)
                act.wait_ge(xr_in[t // 2], b * 16 + 16)
                act.activation(xr[:, t, :], xr[:, t, :], ACT.Identity, bias=out_shift[:, t:t + 1],
                               scale=out_scale[:, t:t + 1]).then_inc(xr_ready, 1)

            def batch(b, first):
                wait(act, o_ps, b * NP * NS)
                for t in range(NT):
                    act.wait_ge(xnT_ps, b * NT + t + 1)
                    act.activation(xnT[:, :, t * P:(t + 1) * P], psum[:, 6 + t % 2, :].rearrange("p (k n) -> p k n", k=KD), ACT.Copy).then_inc(xnT_ready, 1)
                for t in range(NT):
                    a = 2 * (t % 2)
                    k = b * NT + t + 1
                    qkp = psum[:, a:a + 2, :].rearrange("p a n -> p (a n)")
                    act.wait_ge(qk_ps, k)
                    if t == 0:
                        act.wait_ge(xnT_ready, b * NT + NT)
                    wait(act, ss3_ready, k - 1)
                    act.activation(sq, qkp, ACT.Square).then_inc(qk_sq, 1)
                    for o in V_AFTER[t]:
                        copy_v(b, o)
                for w in range(2):
                    repeat_hi(b, 0, w)
                for t in range(NT):
                    if not first:
                        output(b - 1, t, b + 1)
                    for u in BESIDE_Y[t]:
                        user(b, 0, *u)
                    if t == BUILD_Y:
                        for w in range(2):
                            repeat_hi(b, 1, w)
                for p in range(NP):
                    for n, (c, j) in enumerate(STEPS):
                        k = p * NS + n
                        lo = max(0, j - 4 * c) * P
                        if k < SLOTS and not first:
                            act.wait_ge(out_done[k], b * 16)
                        if k >= SLOTS:
                            act.wait_ge(o_ps, b * NP * NS + k - SLOTS + 1)
                        for h in range(2):
                            act.wait_ge(sc_ps, 2 * (b * NP * NS + k) + h + 1)
                            act.activation(probT[:, k % SLOTS, h, lo:CH], psum[:, (2 * k + h) % 3, lo:CH], ACT.Exp).then_inc(sc_exp, 1)
                        for q, u in beside(p, n):
                            user(b, q, *u)
                        if p + 2 < NP and n in REPEAT_STEP:
                            repeat_hi(b, p + 2, REPEAT_STEP.index(n))

            batch(0, True)
            with act.Fori(1, B) as b:
                batch(b, False)
            for t in range(NT):
                output(B - 1, t, B)

        @block.tensor
        def _(pe):
            for started in (o2_ps, pT2_ps, s2_ps, wm_free, wo_ps,):
                pe.sem_inc(started, 1)
            pe.wait_ge(consts_in, 16)
            pe.wait_ge(consts1_in, 32)
            pe.wait_ge(p1_tab, 16)
            with pe.Fori(0, B) as b:
                pe.wait_ge(p1_score, b * NT + NT)
                for t in range(NT):
                    last = pe.transpose(psum[:, t // 4, (t % 4) * P:(t % 4 + 1) * P], s_col[:, t:t + 1].to_broadcast([P, P]), ident)
                last.then_inc(p1_row_ps, 1)
                pe.wait_ge(p1_chosen, b + 1)
                pe.matmul(psum[:, 2, 0:NT], tri, chosen, start=True, stop=False)
                for k in range(1, NT):
                    last = pe.matmul(psum[:, 2, k:NT], ones, chosen[:, 0:NT - k], start=False, stop=(k == NT - 1))
                last.then_inc(p1_pos, 1)
                pe.wait_ge(p1_onehot, b + 1)
                pe.wait_ge(p1_gathered, b * 3 + 1)
                for t in range(NT):
                    last = pe.matmul(psum[:, 3, :], onehot[:, t, :], x_all[:, bass.ds(b * NT + t, 1), :].rearrange("p b d -> p (b d)"), start=(t == 0), stop=(t == NT - 1))
                last.then_inc(p1_gather_ps, 1)
                for t in range(NT):
                    last = pe.matmul(psum[:, 4, 0:FT_W + 1], onehot[:, t, :], tab[:, t, :], start=(t == 0), stop=(t == NT - 1))
                last.then_inc(p1_gather_ps, 1)
                for t in range(NT):
                    last = pe.transpose(psum[:, 5 + t // 4, (t % 4) * P:(t % 4 + 1) * P], onehot[:, t, :], ident)
                last.then_inc(p1_gather_ps, 1)

            def turn_h(n):
                for t in range(ST):
                    pe.wait_ge(h_ready, n * ST + t + 1)
                    for k in range(KD):
                        last = pe.transpose(psum[:, t, k * P:(k + 1) * P], hn[:, t, k * P:(k + 1) * P], ident)
                    last.then_inc(hT_ps, 1)

            pe.wait_ge(p1_gathered, 3 * B + 1)
            turn_h(0)
            for w in range(2):
                for t in range(ST):
                    last = pe.transpose(psum[:, 4 + w, t * P:(t + 1) * P], tabsel[:, t, w * FD:(w + 1) * FD], ident)
            last.then_inc(tabT_ps, 1)
            pe.wait_ge(f_const_in, 80)
            pe.transpose(psum[:, 6, 0:FH + FKV], bias_rows[0:FH + FKV, :], ident[0:FH + FKV, 0:FH + FKV]).then_inc(bias_ps, 1)
            pe.wait_ge(hT_ready, ST)
            pe.wait_ge(tabT_ready, 2)
            pe.wait_ge(biasT_ready, 1)
            with pe.Fori(0, FKV // 2) as i:
                for u in range(2):
                    n = i * 2 + u
                    pe.wait_ge((w2_in0, w2_in1)[u], i * 64 + 64)
                    for r in range(REP + 1):
                        if r == 0:
                            pe.wait_ge(proj_out, n * 3 + 1)
                        if r == 1:
                            pe.wait_ge(v2_ready, n + 1)
                        if r == 2:
                            pe.wait_ge(proj_out, n * 3 + 1 + 1)
                        for k in range(KD):
                            w = wq_s[u][:, k, r * FD:(r + 1) * FD] if r < REP else wk_s[u][:, k, :]
                            last = pe.matmul(psum[:, r % 2, :], w, hT[:, k, :], start=(k == 0), stop=(k == KD - 1))
                        last.then_inc(proj_ps, 1)
                    pe.wait_ge(proj_out, n * 3 + 2 + 1)
                    for t in range(ST):
                        for k in range(KD):
                            last = pe.matmul(psum[:, 1, t * P:(t + 1) * P], hT[:, k, t * P:(t + 1) * P], wv_s[u][:, k, :],
                                             start=(k == 0), stop=(k == KD - 1))
                    last.then_inc(proj_ps, 1)
                    pe.wait_ge(rope_done, n * 3 + 3 + 1)

                    def scores(m):
                        h, t = m // ST, m % ST
                        if m >= 2:
                            pe.wait_ge(s2_low, n * 8 + m - 1)
                        pe.matmul(psum[:, 2 + m % 2, 0:(t + 1) * P], qT2[:, h, t * P:(t + 1) * P], kT2[:, 0:(t + 1) * P],
                                  start=True, stop=True).then_inc(s2_ps, 1)

                    def turn(m):
                        t = m % ST
                        pe.wait_ge(s2_prob, n * 8 + m + 1)
                        if m >= 2:
                            pe.wait_ge(pT2_ready, n * 8 + m - 1)
                        for j in range(t + 1):
                            last = pe.transpose(psum[:, 4 + m % 2, j * P:(j + 1) * P], prob2[:, m, j * P:(j + 1) * P], ident)
                        last.then_inc(pT2_ps, 1)

                    def values(h):
                        pe.wait_ge(pT2_ready, n * 8 + (h + 1) * ST)
                        if h == 0:
                            pe.wait_ge(v2_ready, n + 1 + 1)
                            pe.wait_ge(x1_ready, n * ST + 1)
                        if h == 1:
                            pe.wait_ge(o2_ready, n * REP + 1)
                        for j in range(ST):
                            last = pe.matmul(psum[:, 6, j * P:S], v2[:, j, :], probT2[h][:, j, j * P:S], start=(j == 0), stop=(j == ST - 1))
                        last.then_inc(o2_ps, 1)

                    for m in range(REP * ST):
                        scores(m)
                        if m >= 3:
                            turn(m - 3)
                    for m in range(REP * ST - 3, REP * ST):
                        turn(m)
                    values(0)
                    values(1)
                    pe.wait_ge(o2_ready, n * REP + 2)
                    for t in range(ST):
                        if t >= 2:
                            pe.wait_ge(x1_ready, n * ST + t - 1 + 1)
                        for h in range(REP):
                            last = pe.matmul(psum[:, 7 - t % 2, :], oT2[:, h, t * P:(t + 1) * P], wo_s[u][:, h, :], start=(h == 0), stop=(h == REP - 1))
                        last.then_inc(wo_ps, 1)
            turn_h(1)
            pe.wait_ge(hT_ready, 2 * ST)
            pe.wait_ge(zero_ready, 1)
            for t in range(ST):
                pe.matmul(psum[:, 4 + t, :], zrow[:, 0:P], zrow, start=True, stop=False, skip_group_check=True)
            with pe.Fori(0, NC // 2) as i:
                for u in range(2):
                    pe.wait_ge((wm_in0, wm_in1)[u], i * 48 + 48)
                    pe.wait_ge(aT_ready, i * 2 + 1)
                    for w in range(2):
                        for k in range(KD):
                            last = pe.matmul(psum[:, 2 * u + w, :], (wg_s, wu_s)[w][u][:, k, :], hT[:, k, :], start=(k == 0), stop=(k == KD - 1))
                        last.then_inc(gu_ps, 1)
                for u in range(2):
                    pe.wait_ge(aT_ready, i * 2 + u + 1 + 1)
                    for t in range(ST):
                        last = pe.matmul(psum[:, 4 + t, :], aT[:, u, t * P:(t + 1) * P], wd_s[u], start=False, stop=False, skip_group_check=True)
                    last.then_inc(wm_free, 1)
            for t in range(ST):
                last = pe.matmul(psum[:, 4 + t, :], zrow[:, 0:P], zrow, start=False, stop=True, skip_group_check=True)
            last.then_inc(mlp_ps, 1)
            pe.wait_ge(delta_done, ST)
            pe.wait_ge(late_in, 32)
            pe.wait_ge(kones_ready, 2)
            pe.wait_ge(ident_ready, 1)

            def freed(b, p, u):
                q = b * NP + p
                if u < 3 and p == 0:
                    pe.wait_ge(ss3_ready, b * NT + NT)
                    pe.wait_ge(v_ready, b * NT + NT)
                    return
                before = max(i for i in range(-len(USERS), u) if BANK[i] == BANK[u])
                kind, arg = USERS[before]
                if before < 0:
                    q = q - 1
                if kind == "turn":
                    wait(pe, stackT_ready, q * 8 + TURNS.index(arg) + 1)
                if kind == "max":
                    wait(pe, m_seen, q * len(PIECES) + PIECES.index(arg) + 1)
                if kind == "top":
                    wait(pe, toprow_ready, q * 2 + arg + 1)

            def user(b, p, kind, arg):
                q = b * NP + p
                u = USERS.index((kind, arg))
                bank = BANK[u]
                freed(b, p, u)
                if kind == "turn":
                    w, h, half = arg
                    pe.wait_ge(lo_ready[w], q + 1)
                    pe.wait_ge(hi2_ready, q * 2 + w + 1)
                    for i in range(CH // P):
                        t = half * (CH // P) + i
                        last = pe.transpose(psum[0:RH, bank, i * P:(i + 1) * P].bitcast(f32r), stack[:, w, t, h * STK:h * STK + RH], ident_r[:, :])
                    last.then_inc(stackT_ps, 1)
                if kind == "max":
                    t, c, h = arg
                    w = min(CH, (t + 1) * P - c * CH)
                    pe.wait_ge(stackT_ready, q * 8 + (4 if t < 4 else 8))
                    pe.matmul(psum[:, bank, 0:w], qS[p % 2][0:RH, t // 4, h * CH + t % 4 * P:h * CH + (t % 4 + 1) * P], kS[p % 2][0:RH, h, c * CH:c * CH + w],
                              start=True, stop=True).then_inc(m_ps, 1)
                if kind == "top":
                    pe.wait_ge(m_seen, q * len(PIECES) + (len(PIECES) if arg else NT))
                    pe.transpose(psum[0:NT, bank, 0:P], top[:, p % 2, arg * NT:(arg + 1) * NT], ident).then_inc(topT_ps, 1)

            def output(b, t, beside=()):
                if t == 0:
                    pe.wait_ge(oT_ready, b * 2 * NP + 2 * NP)
                if t >= 2:
                    pe.wait_ge(y_ready, b * NT + t - 1)
                elif not isinstance(b, int):
                    pe.wait_ge(v_ready, (b + 1) * NT + NT)
                    pe.wait_ge(scaled, (b + 1) * NT + NT)
                bank = psum[:, 3 + t % 2, :]
                for g in range(NG):
                    pe.matmul(bank, oT[:, g, t * P:(t + 1) * P], w_out[:, g, :], start=(g == 0), stop=False)
                    for u in beside[g:g + 1]:
                        user(b + 1, 0, *u)
                if t == 0:
                    pe.wait_ge(oh_ready, b + 1)
                pe.matmul(bank, ohT[:, t * P:(t + 1) * P], delta[:, bass.ds(b, 1), :].rearrange("p b d -> p (b d)"), start=False, stop=True).then_inc(y_ps, 1)
                for u in beside[NG:]:
                    user(b + 1, 0, *u)

            def score(b, p, n):
                c, j = STEPS[n]
                lo = max(0, j - 4 * c) * P
                k = p * NS + n
                if j == 0:
                    pe.wait_ge(row_in[c], (b * NP + p + 1) * 16)
                for h in range(2):
                    m = 2 * k + h
                    if m >= 3:
                        pe.wait_ge(sc_exp, 2 * b * NP * NS + m - 2)
                    else:
                        pe.wait_ge(scaled, b * NT + NT)
                    pe.matmul(psum[:, m % 3, lo:CH], kS[p % 2][0:RH + 1, h, j * P:(j + 1) * P],
                                     qS[p % 2][0:RH + 1, c, h * CH + lo:(h + 1) * CH], start=True, stop=True).then_inc(sc_ps, 1)

            def value(b, p, n):
                c, j = STEPS[n]
                lo = max(0, j - 4 * c) * P
                k = p * NS + n
                if j >= 4 * c:
                    pe.wait_ge(sc_masked, b * NP * 8 + p * 8 + j + 1)
                else:
                    pe.wait_ge(sc_exp, 2 * (b * NP * NS + k + 1))
                if j == 0:
                    m = b * 2 * NP + 2 * p + c
                    if p == 0:
                        pe.wait_ge(v_ready, b * NT + NT)
                        wait(pe, y_ready, b * NT)
                    else:
                        pe.wait_ge(oT_ready, m - 1)
                bank = 3 + c
                for r in range(4):
                    h = r % 2
                    w = v[:, j, (p * 2 + h) * AD:(p * 2 + h + 1) * AD] if r < 2 else ones[:, 0:AD]
                    last = pe.matmul(psum[AD * r:AD * (r + 1), bank, lo:CH], w, probT[:, k % SLOTS, h, lo:CH],
                                     start=(j == 0), stop=(j == 4 * c + 3))
                last.then_inc(o_ps, 1)

            def batch(b, first):
                for t in range(NT):
                    pe.wait_ge(xn_ready, b * NT + t + 1)
                    if t >= 2:
                        pe.wait_ge(xnT_ready, b * NT + t - 1)
                    else:
                        wait(pe, toprow_ready, b * NP * 2)
                    for k in range(KD):
                        last = pe.transpose(psum[:, 6 + t % 2, k * P:(k + 1) * P], xn[:, t, k * P:(k + 1) * P], ident)
                    last.then_inc(xnT_ps, 1)
                pe.wait_ge(xnT_ready, b * NT + NT)

                def project_v(t):
                    if t >= 2:
                        pe.wait_ge(v_ready, b * NT + t - 1)
                    else:
                        wait(pe, oT_ready, b * 2 * NP)
                    for k in range(KD):
                        last = pe.matmul(psum[:, 4 + t % 2, :], xnT[:, k, t * P:(t + 1) * P], w_qkv[:, k, 2 * D:3 * D], start=(k == 0), stop=(k == KD - 1))
                    last.then_inc(v_ps, 1)

                for t in range(NT):
                    if t >= 2:
                        pe.wait_ge(scaled, b * NT + t - 1)
                    else:
                        wait(pe, sc_exp, 2 * b * NP * NS)
                    if t == 1:
                        wait(pe, oT_ready, b * 2 * NP)
                    for w in range(2):
                        for k in range(KD):
                            last = pe.matmul(psum[:, 2 * (t % 2) + w, :], xnT[:, k, t * P:(t + 1) * P], w_qkv[:, k, w * D:(w + 1) * D], start=(k == 0), stop=(k == KD - 1))
                    last.then_inc(qk_ps, 1)
                    for o in V_AFTER[t]:
                        project_v(o)
                for t in range(NT):
                    if not first:
                        output(b - 1, t, BESIDE_Y[t])
                    else:
                        for u in BESIDE_Y[t]:
                            user(b, 0, *u)
                for p in range(NP):
                    for n in range(NS):
                        score(b, p, n)
                        users = beside(p, n)
                        for q, u in users[:len(users) // 2]:
                            user(b, q, *u)
                        if p * NS + n >= 2:
                            value(b, *divmod(p * NS + n - 2, NS))
                        for q, u in users[len(users) // 2:]:
                            user(b, q, *u)
                value(b, NP - 1, NS - 2)
                value(b, NP - 1, NS - 1)

            batch(0, True)
            with pe.Fori(1, B) as b:
                batch(b, False)
            for t in range(NT):
                output(B - 1, t)

        @block.vector
        def _(dve):
            for started in (rope_done, sg_3, aT_ready, v2_ready, x1_ready,):
                dve.sem_inc(started, 1)
            dve.wait_ge(consts1_in, 32)
            dve.wait_ge(p1_tab, 16)
            dve.memset(earlier[:, 0:1], 0.0)

            def tile_x(b, t):
                return x_all[:, bass.ds(b * NT + t, 1), :].rearrange("p b d -> p (b d)")

            def statistics(b):
                dve.wait_ge(x_in, b * 16 + 16)
                for t in range(NT):
                    dve.bn_stats(stats[:, t, :], tile_x(b, t)).then_inc(p1_stats, 1)
                wait_apart(dve, p1_stats, b * 2 * NT + NT)
                wait_apart(dve, p1_mean, b * 2 + 1)
                for t in range(NT):
                    dve.bn_aggr(mv[:, t, :], stats[:, t, :]).then_inc(p1_stats, 1)

            def select(b, last):
                dve.wait_ge(p1_rstd, b + 1)
                for t in range(NT):
                    dve.tensor_scalar(tile_x(b, t), tile_x(b, t), mv[:, t, 0:1], rstd1[:, t:t + 1], ALU.subtract, ALU.mult).then_inc(p1_norm, 1)
                for t in range(NT):
                    wait_apart(dve, p1_norm, b * NT + t + 1)
                    if t >= 2:
                        wait_apart(dve, p1_score, b * NT + t - 1)
                    dve.scalar_tensor_tensor(out=s_row[:, (t % 2) * D:(t % 2 + 1) * D], in0=tile_x(b, t), scalar=1.0, in1=wr_b,
                                             op0=ALU.mult, op1=ALU.mult, accum_out=s_col[:, t:t + 1]).then_inc(p1_score, 1)
                if not last:
                    statistics(b + 1)
                dve.wait_ge(p1_score, b * NT + NT)
                dve.wait_ge(p1_gathered, b * 3 + 1)
                dve.tensor_copy(tab[:, :, FT_W], s_col).then_inc(p1_tab_score, 1)
                dve.wait_ge(p1_row, b + 1)
                for t in range(NT):
                    own = slice(t * P, (t + 1) * P)
                    if t >= 1:
                        dve.wait_ge(p1_cnt, b * NT + t)
                        dve.tensor_scalar(junk1[:, 0, 0:t * P], s_row[:, 0:t * P], s_col[:, t:t + 1], 0.0, ALU.is_ge, ALU.add, accum_out=earlier[:, t:t + 1])
                    dve.tensor_scalar(junk1[:, 0, t * P:T], s_row[:, t * P:T], s_col[:, t:t + 1], 0.0, ALU.is_gt, ALU.add, accum_out=above[:, t:t + 1])
                    dve.scalar_tensor_tensor(out=junk1[:, 1, 0:P], in0=s_row[:, own], scalar=s_col[:, t:t + 1], in1=tie,
                                             op0=ALU.is_equal, op1=ALU.mult, accum_out=tied[:, t:t + 1]).then_inc(p1_cnt, 1)
                dve.wait_ge(p1_cnt, b * NT + NT)
                dve.tensor_tensor(rank, above, tied, ALU.add).then_inc(p1_rank, 1)
                dve.wait_ge(p1_rank, b * 2 + 1)
                dve.tensor_tensor(rank, rank, earlier, ALU.add).then_inc(p1_rank, 1)
                dve.wait_ge(p1_rank, b * 2 + 2)
                dve.tensor_scalar(chosen, rank, float(SEL), None, ALU.is_lt).then_inc(p1_chosen, 1)
                dve.wait_ge(p1_pos, b + 1)
                dve.scalar_tensor_tensor(out=slot, in0=psum[:, 2, 0:NT], scalar=1.0, in1=chosen, op0=ALU.add, op1=ALU.mult).then_inc(p1_slot, 1)
                dve.wait_ge(p1_slot, b + 1)
                for t in range(NT):
                    chose = dve.tensor_scalar(onehot[:, t, :], iota1, slot[:, t:t + 1], None, ALU.is_equal)
                chose.then_inc(p1_onehot, 1)

            statistics(0)
            with dve.Fori(0, B - 1) as b:
                select(b, False)
            select(B - 1, True)

            dve.wait_ge(gate_1, 1)
            dve.tensor_scalar(dgate, egate, 1.0, None, ALU.add).then_inc(gate_2, 1)
            dve.wait_ge(gate_2, 1)
            dve.reciprocal(gate, dgate).then_inc(gate_3, 1)

            def norm(src, w_b, n):
                for t in range(ST):
                    dve.tensor_tensor_reduce(hn[:, t, :], src[:, t, :], src[:, t, :], 1.0, 0.0, ALU.mult, ALU.add, ss2[:, t:t + 1]).then_inc(ss2_ready, 1)
                dve.wait_ge(rs2_ready, n + 1)
                for t in range(ST):
                    dve.scalar_tensor_tensor(out=hn[:, t, :], in0=src[:, t, :], scalar=rs2[:, t:t + 1], in1=w_b, op0=ALU.mult, op1=ALU.mult).then_inc(h_ready, 1)

            dve.wait_ge(p1_gathered, 3 * B + 1)
            dve.wait_ge(rope_ready, 5)
            dve.wait_ge(f_const_in, 80)
            norm(xsel, ln1_b, 0)
            dve.tensor_copy(x1, xsel).then_inc(delta_a, 1)
            dve.wait_ge(tabT_ready, 2)
            dve.wait_ge(delta_a, 1)
            with dve.Fori(0, FKV // 2) as i:
                for u in range(2):
                    n = i * 2 + u
                    for r in range(REP + 1):
                        dst = qT2[:, r, :] if r < REP else kT2
                        half = FD // 2
                        dve.wait_ge(proj_out, n * 3 + r + 1 + 1)
                        dve.wait_ge(rope_done, n * 3 + r + 1)
                        dve.tensor_tensor(rotd[0:half, :], raw[half:FD, r % 2, :], sinT[half:FD, :], ALU.mult).then_inc(rope_a, 1)
                        dve.tensor_tensor(rotd[half:FD, :], raw[0:half, r % 2, :], sinT[0:half, :], ALU.mult).then_inc(rope_a, 1)
                        if r == 0:
                            dve.wait_ge(s2_ps, n * 8 + 1)
                        dve.tensor_tensor(dst, raw[:, r % 2, :], cosT, ALU.mult).then_inc(rope_a, 1)
                        dve.wait_ge(rope_a, n * 9 + 3 * r + 3)
                        dve.tensor_tensor(dst, dst, rotd, ALU.add).then_inc(rope_done, 1)
                    dve.wait_ge(proj_ps, n * 4 + 4)
                    dve.wait_ge(o2_ps, n * REP + 1)
                    dve.tensor_tensor(v2, psum[:, 1, :].rearrange("p (t d) -> p t d", d=FD),
                                      bv_b[:, bass.ds(n * FD, FD)].unsqueeze(1).to_broadcast([P, ST, FD]), ALU.add).then_inc(v2_ready, 1)

                    def normalise(m):
                        w = (m % ST + 1) * P
                        dve.wait_ge(s2_exp, n * 8 + m + 1)
                        dve.reciprocal(rden2[:, m:m + 1], den2[:, m:m + 1]).then_inc(s2_den, 1)
                        dve.wait_ge(s2_den, n * 8 + m + 1)
                        dve.tensor_scalar(prob2[:, m, 0:w], prob2[:, m, 0:w], rden2[:, m:m + 1], None, ALU.mult).then_inc(s2_prob, 1)

                    for m in range(REP * ST):
                        w = (m % ST + 1) * P
                        if m == 0:
                            wait_apart(dve, pT2_ps, n * 8 + 1)
                        wait_apart(dve, s2_ps, n * 8 + m + 1 + 1)
                        dve.tensor_tensor_reduce(prob2[:, m, 0:w], psum[:, 2 + m % 2, 0:w], mask[:, CH - w:CH], -(FD ** -0.5), 3e38,
                                                 ALU.add, ALU.min, nmax2[:, m:m + 1]).then_inc(s2_low, 1)
                        if m >= 1:
                            normalise(m - 1)
                    normalise(REP * ST - 1)
                    for h in range(REP):
                        dve.wait_ge(o2_ps, n * REP + h + 1 + 1)
                        if h == 0:
                            dve.wait_ge(wo_ps, n * ST + 1)
                        dve.tensor_copy(oT2[:, h, :], psum[:, 6, :]).then_inc(o2_ready, 1)
                    for t in range(ST):
                        dve.wait_ge(wo_ps, n * ST + t + 1 + 1)
                        dve.tensor_tensor(x1[:, t, :], psum[:, 7 - t % 2, :], x1[:, t, :], ALU.add).then_inc(x1_ready, 1)
            dve.wait_ge(x1_ready, FKV * ST + 1)
            norm(x1, ln2_b, 1)
            dve.memset(zrow, 0.0).then_inc(zero_ready, 1)
            with dve.Fori(0, NC // 2) as i:
                for u in range(2):
                    n = i * 2 + u
                    dve.wait_ge(eg_ready, n + 1)
                    dve.tensor_scalar(sg[:, u, :], eg[:, u, :], 1.0, None, ALU.add).then_inc(sg_1, 1)
                    dve.wait_ge(sg_1, n + 1)
                    dve.reciprocal(eg[:, u, :], sg[:, u, :]).then_inc(sg_2, 1)
                    dve.wait_ge(sg_2, n + 1)
                    dve.tensor_tensor(sg[:, u, :], psum[:, 2 * u, :], eg[:, u, :], ALU.mult).then_inc(sg_3, 1)
                    dve.wait_ge(sg_3, n + 1 + 1)
                    dve.wait_ge(gu_ps, n * 2 + 2)
                    dve.wait_ge(wm_free, i * 2 + 1)
                    dve.tensor_tensor(aT[:, u, :], psum[:, 2 * u + 1, :], sg[:, u, :], ALU.mult).then_inc(aT_ready, 1)
            dve.wait_ge(mlp_ps, 1)
            for t in range(ST):
                dve.tensor_tensor(x1[:, t, :], psum[:, 4 + t, :], x1[:, t, :], ALU.add).then_inc(delta_a, 1)
            for t in range(ST):
                dve.wait_ge(delta_a, t + 2)
                dve.tensor_tensor(hn[:, t, :], x1[:, t, :], xsel[:, t, :], ALU.subtract).then_inc(delta_b, 1)
            for t in range(ST):
                dve.wait_ge(delta_b, t + 1)
                dve.tensor_scalar(delta[:, t, :], hn[:, t, :], gate[:, t:t + 1], None, ALU.mult).then_inc(delta_done, 1)

            sq = psum[:, 6:8, :].rearrange("p a n -> p (a n)")
            qk3 = qk.rearrange("p (h d) -> p h d", d=AD)
            rot4 = rot.rearrange("p (w h d) -> p w h d", w=2, d=AD)
            qk4 = qk.rearrange("p (w h d) -> p w h d", w=2, d=AD)

            def norm_tile(b, t):
                nb = b % B
                if t == 0:
                    dve.wait_ge(xb_in, b * 16 + 16)
                dve.tensor_scalar(xn[:, t, :], xn[:, t, :], ln_mean[:, bass.ds(nb, 1), t], ln_rstd[:, bass.ds(nb, 1), t],
                                  ALU.subtract, ALU.mult).then_inc(xn_ready, 1)

            def user(b, p, kind, arg):
                if kind != "max":
                    return
                t, c, h = arg
                n = PIECES.index(arg)
                w = min(CH, (t + 1) * P - c * CH)
                q = b * NP + p
                bank = BANK[USERS.index((kind, arg))]
                past = past_top[:, 2 * (t % 2) + h:2 * (t % 2) + h + 1]
                diag = c == t // 4
                place = (t // 4) * NT + h * 4 + t % 4
                wait_apart(dve, m_ps, q * len(PIECES) + n + 1)
                if n == 0:
                    wait_apart(dve, topT_ps, (q - 1) * 2)
                if not diag:
                    dve.tensor_reduce(past, psum[:, bank, :], AX.X, ALU.max).then_inc(m_seen, 1)
                    return
                if c:
                    wait_apart(dve, m_seen, q * len(PIECES) + PIECES.index((t, c - 1, h)) + 1)
                dve.tensor_tensor_reduce(psum[:, bank, 0:w], psum[:, bank, 0:w], mask[:, CH - w:CH], 1.0,
                                         past if c else -3e38, ALU.add, ALU.max, top[:, p % 2, place:place + 1]).then_inc(m_seen, 1)

            def turn_sums(b, p, c):
                m = b * 2 * NP + 2 * p + c
                half = 2 * AD
                dve.wait_ge(o_ps, b * NP * NS + p * NS + (4 if c == 0 else NS))
                wait(dve, oT_ready, m)
                dve.transpose(rden[0:half, :], psum[half:P, 3 + c, :]).then_inc(den_turned, 1)

            def invert_sums(b, p, c):
                m = b * 2 * NP + 2 * p + c
                half = 2 * AD
                dve.wait_ge(den_turned, m + 1)
                dve.reciprocal(rden_t[0:half, :], rden[0:half, :].rearrange("p (g r) -> p g r", r=32)[:, :, 0]).then_inc(rden_ready, 1)
                dve.wait_ge(rden_ready, m + 1)
                dve.transpose(rden[0:half, :], rden_t[0:half, :].unsqueeze(2).to_broadcast([half, CH // 32, 32])).then_inc(rden_turned, 1)

            def divide(b, p, c):
                m = b * 2 * NP + 2 * p + c
                half = 2 * AD
                r = (p % 2) * half
                dve.wait_ge(rden_turned, m + 1)
                dve.tensor_tensor(oT[r:r + half, p // 2, c * CH:(c + 1) * CH], psum[0:half, 3 + c, :], rden[0:half, :], ALU.mult).then_inc(oT_ready, 1)

            def output(b, t):
                dve.wait_ge(y_ps, b * NT + t + 1)
                dve.wait_ge(xr_ready, b * NT + t + 1)
                dve.tensor_tensor(xr[:, t, :], psum[:, 3 + t % 2, :], xr[:, t, :], ALU.add).then_inc(y_ready, 1)

            def batch(b, first):
                def sums(t):
                    k = b * NT + t + 1
                    dve.wait_ge(qk_sq, k)
                    wait(dve, ms3_ready, k - 1)
                    dve.tensor_reduce(ss3, sq.rearrange("p (h d) -> p h d", d=AD), AX.X, ALU.add).then_inc(ss3_ready, 1)

                sums(0)
                for t in range(NT):
                    k = b * NT + t + 1
                    if t + 1 < NT:
                        sums(t + 1)
                    dve.wait_ge(rs3_ready, k)
                    wait(dve, rotated, k - 1)
                    wait(dve, cosed, k - 1)
                    qkp = psum[:, 2 * (t % 2):2 * (t % 2) + 2, :].rearrange("p a n -> p (a n)").rearrange("p (h d) -> p h d", d=AD)
                    dve.tensor_tensor(qk3, qkp, rs3[:, t % 2, :].unsqueeze(2).to_broadcast([P, 2 * AH, AD]), ALU.mult).then_inc(scaled, 1)
                    dve.wait_ge(scaled, k)
                    if t == 0:
                        for w in range(2):
                            wait(dve, lo_ready[w], b * NP)
                    tile = roped[:, t, :].rearrange("p (w h d) -> p w h d", w=2, d=AD)
                    for w in range(2):
                        dve.tensor_tensor(tile[:, w], qk4[:, w], cosG[:, t, w, :].unsqueeze(1).to_broadcast([P, AH, AD]), ALU.mult)
                    for h in range(2):
                        o = h * (AD // 2)
                        sn = sinG[:, t, 1, o:o + AD // 2].unsqueeze(1).to_broadcast([P, AH, AD // 2])
                        last = dve.tensor_tensor(rot4[:, 1, :, o:o + AD // 2], qk4[:, 1, :, AD // 2 - o:AD - o], sn, ALU.mult)
                    last.then_inc(cosed, 1)
                    dve.wait_ge(rotated, k)
                    dve.wait_ge(cosed, k)
                    dve.tensor_tensor(roped[:, t, :], roped[:, t, :], rot, ALU.add).then_inc(roped_ready, 1)
                src = roped[:, :, D:D + 2 * AD].rearrange("p t (h d) -> p t h d", h=2)
                st = stack[:, 1].rearrange("p t (h c) -> p t h c", h=2)
                wait(dve, stackT_ps, b * NP * 8)
                dve.wait_ge(roped_ready, b * NT + NT)
                for h in range(2):
                    dve.tensor_copy(st[:, :, h, 0:AD], src[:, :, h]).then_inc(hi_ready[1], 1)
                dve.wait_ge(hi_ready[1], b * NP * 2 + 2)
                for h in range(2):
                    last = dve.tensor_tensor(st[:, :, h, 2 * AD:3 * AD], src[:, :, h], st[:, :, h, 0:AD].bitcast(f32), ALU.subtract)
                last.then_inc(lo_ready[1], 1)
                for t in range(NT):
                    for u in BESIDE_Y[t]:
                        user(b, 0, *u)
                    if not first:
                        output(b - 1, t)
                for p in range(NP):
                    for n in range(NS):
                        for q, u in beside(p, n):
                            user(b, q, *u)
                        if n == 2 and p > 0:
                            turn_sums(b, p - 1, 1)
                        if n == 3 and p > 0:
                            invert_sums(b, p - 1, 1)
                        if n == 4 and p > 0:
                            divide(b, p - 1, 1)
                        if n == 6:
                            turn_sums(b, p, 0)
                        if n == 7:
                            invert_sums(b, p, 0)
                        if n == 8:
                            divide(b, p, 0)
                        if p == NP - 1 and 2 <= n < 2 + NT:
                            norm_tile(b + 1, n - 2)
                turn_sums(b, NP - 1, 1)
                invert_sums(b, NP - 1, 1)
                divide(b, NP - 1, 1)

            for t in range(NT):
                norm_tile(0, t)
            batch(0, True)
            with dve.Fori(1, B) as b:
                batch(b, False)
            for t in range(NT):
                output(B - 1, t)



STEPS = [(c, j) for c in range(T // CH) for j in range((c + 1) * CH // P)]
NS = len(STEPS)
TURNS = [(w, h, half) for half in range(2) for h in range(2) for w in range(2)]
PIECES = [(t, c, h) for t in range(NT) for c in range(t // 4 + 1) for h in range(2)]
_T, _M = [("turn", a) for a in TURNS], [("max", a) for a in PIECES]
USERS = (_T[:4] + _T[4:5] + _M[:2] + _T[5:6] + _M[2:4] + _T[6:7] + _M[4:6] + _T[7:] + _M[6:NT] +
         [("top", 0)] + _M[NT:] + [("top", 1)])


BANK = [5 + i % 3 for i in range(len(USERS) - 1)] + [6]


def dealt(counts):
    out, at = [], 0
    for n in counts:
        out.append(USERS[at:at + n])
        at += n
    return out


V_AFTER = [[], [0], [], [1], [2], [3], [4], [5, 6, 7]]
BESIDE_Y = dealt([1, 3, 5, 5, 5, 5, 5, 4])
BESIDE_STEP = dealt([3, 4, 4, 4, 4, 4, 3, 3, 2, 1, 1, 0])
LEFT_OVER = USERS[33:]


def beside(p, n):
    own = [(p, u) for u in LEFT_OVER] if n == 0 else []
    return own + ([(p + 1, u) for u in BESIDE_STEP[n]] if p + 1 < NP else [])


BUILD_Y = 3
BUILD_STEP = 3
REPEAT_STEP = (6, 8)
BESIDE_STEP = dealt([2, 3, 4, 4, 4, 4, 4, 4, 3, 1, 0, 0])

_INS = ["L0_attn_x", "L0_attn_w_qkv", "L0_attn_w_out", "L0_attn_q_gamma", "L0_attn_k_gamma", "L0_ffn_w_router",
        "L0_ffn_wq", "L0_ffn_bq", "L0_ffn_wk", "L0_ffn_bk", "L0_ffn_wv", "L0_ffn_bv", "L0_ffn_wo",
        "L0_ffn_w_gate", "L0_ffn_w_up", "L0_ffn_w_down", "L0_ffn_ln1_w", "L0_ffn_ln2_w"]


def shape_constants():
    import numpy as np
    p = np.arange(P)[:, None]
    const = np.zeros((P, C_W), np.float32)
    const[:, C_ID:C_ID + P] = np.eye(P)
    const[:, C_ONE:C_ONE + P] = 1
    const[:, C_MASK + CH - P:C_MASK + CH] = np.where(np.arange(P)[None] <= p, 0, MASKED)
    const[:, C_TRI:C_TRI + P] = p < np.arange(P)[None]
    const[:, C_IOTA:C_IOTA + P] = np.arange(P)[None] + 1
    const[:, C_TIE:] = np.arange(P)[None] < p

    def angles(width):
        e = np.arange(0, width, 2, dtype=np.float32) / np.float32(width)
        inv = (np.float32(1) / np.power(np.float32(10000.0), e)).astype(np.float32)
        a = np.arange(T, dtype=np.float32)[:, None] * inv[None]
        return np.cos(a).astype(np.float32), np.sin(a).astype(np.float32)

    c, sn = angles(AD)
    rope = np.concatenate([c, c, -sn, sn], 1)
    c, sn = angles(FD)
    frope = np.concatenate([c, c, sn, -sn], 1)
    return {"const": const, "rope": rope, "frope": frope}


def kernel(**inputs):
    import numpy as _np
    import concourse.bacc as _bacc
    from concourse import mybir as _mybir
    from concourse.bass_utils import run_bass_kernel_spmd as _run

    nc = _bacc.Bacc("TRN2", target_bir_lowering=False, num_devices=1)
    arrays, args = {}, []
    given = {n: _np.ascontiguousarray(inputs[n]) for n in _INS}
    given.update(shape_constants())
    for name, a in given.items():
        arrays[f"in_{name}"] = a
        args.append(nc.dram_tensor(f"in_{name}", a.shape, _mybir.dt.from_np(a.dtype), kind="ExternalInput").ap())
    args.append(nc.dram_tensor("out_y", (B, T, D), _mybir.dt.float32, kind="ExternalOutput").ap())
    build(nc, *args)
    r = _run(nc, [arrays], core_ids=[0])
    return r.results[0]["out_y"]
```

```python
import concourse.bass as bass
from concourse import mybir
from contextlib import ExitStack

P = 128
B, T, D = 4, 1024, 512
NT = T // P
KD = D // P
AH, AD = 16, 32
HG = P // AD
NG = AH // HG
FH, FKV, FD = 16, 8, 128
REP = FH // FKV
SEL = T // 8
S = B * SEL
ST = S // P
FI = 2048
NC = FI // P
CH = 512
LN_EPS, RMS_EPS = 1e-5, 1e-6
NP = AH // 2
STK = 3 * AD
RH = STK
SLOTS = 4
MASKED = -1e30

C_ID, C_ONE, C_MASK, C_TRI, C_IOTA, C_TIE = 0, 128, 256, 768, 896, 1024
C_W = C_TIE + P
FT_W = 4 * (FD // 2)


def build(nc, x_d, w_qkv_d, w_out_d, qg_d, kg_d, wr_d, wq_d, bq_d, wk_d, bk_d, wv_d, bv_d, wo_d,
          wg_d, wu_d, wd_d, ln1_d, ln2_d, const_d, rope_d, frope_d, out_d):
    f32, f32r, bf16 = mybir.dt.float32, mybir.dt.float32r, mybir.dt.bfloat16
    ALU, ACT, AX = mybir.AluOpType, mybir.ActivationFunctionType, mybir.AxisListType

    x_v = x_d.rearrange("b (t p) d -> b p t d", p=P)
    out_v = out_d.rearrange("b (t p) d -> b p t d", p=P)
    wqkv_v = w_qkv_d.rearrange("(k p) n -> p k n", p=P)
    wout_v = w_out_d.rearrange("(k p) n -> p k n", p=P)
    wq_v = wq_d.rearrange("(k p) (n c) -> n p k c", p=P, c=REP * FD)
    wk_v = wk_d.rearrange("(k p) (n c) -> n p k c", p=P, c=FD)
    wv_v = wv_d.rearrange("(k p) (n c) -> n p k c", p=P, c=FD)
    wo_v = wo_d.rearrange("(n r p) d -> n p r d", p=P, r=REP)
    wg_v = wg_d.rearrange("(k p) (n c) -> n p k c", p=P, c=P)
    wu_v = wu_d.rearrange("(k p) (n c) -> n p k c", p=P, c=P)
    wd_v = wd_d.rearrange("(n p) d -> n p d", p=P)

    ctx = ExitStack()
    with ctx:
        ARENA = 53200 - 8 * T - 4 * NT * STK - P
        arena = ctx.enter_context(nc.sbuf_tensor("arena", [P, ARENA], f32))
        qS = [ctx.enter_context(nc.sbuf_tensor(f"q_stack{i}", [P, 2, T], f32r)) for i in range(2)]
        kS = [ctx.enter_context(nc.sbuf_tensor(f"k_stack{i}", [P, 2, T], f32r)) for i in range(2)]
        stack = ctx.enter_context(nc.sbuf_tensor("stack", [P, 2, NT, 2 * STK], f32r))
        ident_r = ctx.enter_context(nc.sbuf_tensor("ident_r", [P, P], f32r))
        psum = ctx.enter_context(nc.psum_tensor("psum", [P, 8, 512], f32))

        def sem(name):
            return ctx.enter_context(nc.semaphore(name))

        class Place:
            def __init__(self, at, end):
                self.at, self.end = at, end

            def f(self, *shape):
                n = 1
                for s in shape:
                    n *= s
                a = arena[:, self.at:self.at + n]
                self.at += n
                assert self.at <= self.end, (self.at, self.end)
                if len(shape) == 2:
                    a = a.rearrange("p (a b) -> p a b", b=shape[1])
                if len(shape) == 3:
                    a = a.rearrange("p (a b c) -> p a b c", b=shape[1], c=shape[2])
                return a

            def h(self, *shape):
                n = 1
                for s in shape:
                    n *= s
                a = arena[:, self.at:self.at + n // 2].bitcast(bf16)
                self.at += n // 2
                assert self.at <= self.end, (self.at, self.end)
                if len(shape) == 2:
                    a = a.rearrange("p (a b) -> p a b", b=shape[1])
                return a

        keep = Place(0, ARENA)
        ident = keep.f(P)
        ones = keep.f(P)
        mask = keep.f(CH)
        onehotT = keep.h(B, T)
        delta = keep.f(B, D)
        ln_mean = keep.f(B, NT)
        ln_rstd = keep.f(B, NT)
        half_neg = keep.f(32)
        cosG = keep.f(NT, 2, AD)
        sinG = keep.f(NT, 2, AD)
        w_qkv_at = keep.at
        w_qkv = keep.f(KD, 3 * D)
        w_out_at = keep.at
        w_out = keep.f(KD, D)
        rest = keep.at

        p1 = Place(w_out_at, ARENA)
        x_all = p1.f(B * NT, D)
        x_end = p1.at
        xsel = p1.f(ST, D)
        tabsel = p1.f(ST, FT_W + 1)
        rest2 = p1.at
        tab = p1.f(NT, FT_W + 1)
        s_row = p1.f(T)
        onehot = p1.f(NT, P)
        junk1 = p1.h(2, T)
        wr_b = p1.f(D)
        cst1 = p1.f(C_W - C_TRI)
        tri = cst1[:, 0:P]
        iota1 = cst1[:, C_IOTA - C_TRI:C_IOTA - C_TRI + P]
        tie = cst1[:, C_TIE - C_TRI:]
        gam = p1.f(2, AD)
        rope_raw = p1.f(NT, 2 * AD)
        stats = p1.f(NT, 6)
        mv = p1.f(NT, 2)
        vpe = p1.f(NT)
        rstd1 = p1.f(NT)
        s_col = p1.f(NT)
        above = p1.f(NT)
        earlier = p1.f(NT)
        tied = p1.f(NT)
        rank = p1.f(NT)
        chosen = p1.f(NT)
        slot = p1.f(NT)

        p2 = Place(rest, x_end)
        hn = p2.f(ST, D)
        raw = p2.f(2, S)
        qT2_0 = p2.f(REP, S)
        x1 = p2.f(ST, D)
        mlp_at = p2.at
        prob2 = p2.f(REP * ST, S)
        probT2 = [p2.f(ST, S) for _ in range(REP)]
        mlp_end = p2.at
        p2 = Place(rest2, ARENA)
        cosT = p2.f(S)
        sinT = p2.f(S)
        biasT = p2.f(FH + FKV)
        p2w = Place(w_qkv_at, w_out_at)
        wq_s = [p2w.f(KD, REP * FD) for _ in range(2)]
        wk_s = [p2w.f(KD, FD) for _ in range(2)]
        wv_s = [p2w.f(KD, FD) for _ in range(2)]
        wo_s = [p2w.f(REP, D) for _ in range(2)]
        rotd = p2.f(S)
        qT2 = [qT2_0, p2.f(REP, S)]
        kT2 = [p2.f(S) for _ in range(2)]
        v2 = [p2.f(ST, FD) for _ in range(2)]
        oT2 = p2.f(REP, S)
        nmax2 = p2.f(REP * ST)
        den2 = p2.f(REP * ST)
        rden2 = p2.f(REP * ST)
        gate = p2.f(ST)
        egate = p2.f(ST)
        dgate = p2.f(ST)
        early = Place(max(p1.at, p2.at), ARENA)
        bias_rows = early.f(FD)
        bv_b = early.f(FKV * FD)
        ln1_b = early.f(D)
        ln2_b = early.f(D)
        ss2 = early.f(ST)
        ms2 = early.f(ST)
        rs2 = early.f(ST)
        p2m = Place(mlp_at, mlp_end)
        wg_s = [p2m.f(KD, P) for _ in range(2)]
        wu_s = [p2m.f(KD, P) for _ in range(2)]
        wd_s = [p2m.f(D) for _ in range(2)]
        gain = arena[:, p2m.at:p2m.at + ST * D].rearrange("p (t d) -> p t d", d=D)
        eg = p2m.f(2, S)
        sg = p2m.f(2, S)
        aT = p2m.f(2, S)
        zrow = p2m.f(D)
        hS = [qS[i][:, :, :].rearrange("p a n -> p (a n)").rearrange("p (k s) -> p k s", k=KD) for i in range(2)]
        wqS, wkS, wvS = ([kS[i][:, 0, :].rearrange("p (k c) -> p k c", k=KD) for i in range(2)],
                         [kS[i][:, 1, 0:KD * FD].rearrange("p (k c) -> p k c", k=KD) for i in range(2)],
                         [kS[i][:, 1, KD * FD:].rearrange("p (k c) -> p k c", k=KD) for i in range(2)])
        wguS = [kS[u][:, :, :].rearrange("p a n -> p (a n)").rearrange("p (w i k c) -> p w i k c", w=2, i=2, k=KD) for u in range(2)]
        stack_flat = stack[:, :, :, :].rearrange("p w t c -> p (w t c)")
        wdS = [stack_flat[:, u * 2 * D:(u + 1) * 2 * D].rearrange("p (i d) -> p i d", i=2) for u in range(2)]
        aS = stack_flat[:, 4 * D:4 * D + 2 * S].rearrange("p (i s) -> p i s", i=2)
        PARTS = [(0, 0), (0, 1), (1, 0)]

        p3 = Place(rest, ARENA)
        xn = p3.f(NT, D)
        xnT = p3.f(KD, T)
        probT = xnT.rearrange("p k n -> p (k n)").rearrange("p (s h n) -> p s h n", s=SLOTS, h=2)
        roped = p3.f(NT, 2 * D)
        v = p3.f(NT, D)
        oT = p3.f(NG, T)
        xr = xnT.rearrange("p k n -> p (k n)").rearrange("p (t d) -> p t d", d=D)
        qk = p3.f(2 * D)
        ohT = p3.f(T)
        rot = ohT
        top = p3.f(2, 2 * NT)
        top_rows = p3.f(2, P)
        ss3 = p3.f(2 * AH)
        ms3 = p3.f(2 * AH)
        rs3 = p3.f(2, 2 * AH)
        past_top = p3.f(4)
        rden = p3.f(CH)
        rden_t = p3.f(CH // 32)
        out_scale = p3.f(NT)
        out_shift = p3.f(NT)
        assert p3.at <= ARENA

        consts_in = sem("consts_in")
        consts1_in = sem("consts1_in")
        x0_in = [sem(f"x0_in{half}") for half in range(2)]
        x_in = sem("x_in")
        late_in = sem("late_in")
        gam_ready = sem("gam_ready")
        rope_ready = sem("rope_ready")
        p1_stats = sem("p1_stats")
        p1_vpe = sem("p1_vpe")
        p1_rstd = sem("p1_rstd")
        p1_norm = sem("p1_norm")
        p1_score = sem("p1_score")
        p1_row_ps = sem("p1_row_ps")
        p1_row = sem("p1_row")
        p1_cnt = sem("p1_cnt")
        p1_rank = sem("p1_rank")
        p1_chosen = sem("p1_chosen")
        p1_pos = sem("p1_pos")
        p1_slot = sem("p1_slot")
        p1_onehot = sem("p1_onehot")
        p1_tab = sem("p1_tab")
        p1_gather_ps = sem("p1_gather_ps")
        p1_gathered = sem("p1_gathered")
        p1_mean = sem("p1_mean")
        init_done = sem("init_done")
        f_const_in = sem("f_const_in")
        wo_in = [sem(f"wo_in{u}") for u in range(2)]
        w2_in0 = sem("w2_in0")
        w2_in1 = sem("w2_in1")
        ss2_ready = sem("ss2_ready")
        ms2_ready = sem("ms2_ready")
        rs2_ready = sem("rs2_ready")
        h_ready = sem("h_ready")
        hT_ps = sem("hT_ps")
        hT_ready = sem("hT_ready")
        tabT_ps = sem("tabT_ps")
        tabT_ready = sem("tabT_ready")
        bias_ps = sem("bias_ps")
        biasT_ready = sem("biasT_ready")
        proj_ps = sem("proj_ps")
        proj_out = sem("proj_out")
        rope_a = sem("rope_a")
        rope_done = sem("rope_done")
        v2_ready = sem("v2_ready")
        s2_ps = sem("s2_ps")
        s2_low = sem("s2_low")
        s2_exp = sem("s2_exp")
        s2_den = sem("s2_den")
        s2_prob = sem("s2_prob")
        pT2_ps = sem("pT2_ps")
        pT2_ready = sem("pT2_ready")
        o2_ps = sem("o2_ps")
        o2_ready = sem("o2_ready")
        wo_ps = sem("wo_ps")
        x1_ready = sem("x1_ready")
        wm_in0 = sem("wm_in0")
        wm_in1 = sem("wm_in1")
        gu_ps = sem("gu_ps")
        eg_ready = sem("eg_ready")
        sg_1 = sem("sg_1")
        sg_2 = sem("sg_2")
        sg_3 = sem("sg_3")
        aT_ready = sem("aT_ready")
        wm_free = sem("wm_free")
        h_lo = sem("h_lo")
        w2_hi = sem("w2_hi")
        w2_lo = sem("w2_lo")
        gu_hi = sem("gu_hi")
        gu_lo = sem("gu_lo")
        wd_hi = sem("wd_hi")
        wd_lo = sem("wd_lo")
        aS_hi = sem("aS_hi")
        aT_made = sem("aT_made")
        zero_ready = sem("zero_ready")
        mlp_ps = sem("mlp_ps")
        delta_a = sem("delta_a")
        delta_b = sem("delta_b")
        delta_done = sem("delta_done")
        gate_1 = sem("gate_1")
        gate_2 = sem("gate_2")
        xb_in = sem("xb_in")
        xn_ready = sem("xn_ready")
        xnT_ps = sem("xnT_ps")
        xnT_ready = sem("xnT_ready")
        qk_ps = sem("qk_ps")
        qk_sq = sem("qk_sq")
        ss3_ready = sem("ss3_ready")
        ms3_ready = sem("ms3_ready")
        rs3_ready = sem("rs3_ready")
        scaled = sem("scaled")
        rotated = sem("rotated")
        cosed = sem("cosed")
        roped_ready = sem("roped_ready")
        v_ps = sem("v_ps")
        v_ready = sem("v_ready")
        hi_ready = [sem("q_hi_ready"), sem("k_hi_ready")]
        lo_ready = [sem("q_lo_ready"), sem("k_lo_ready")]
        ident_ready = sem("ident_ready")
        stackT_ps = sem("stackT_ps")
        stackT_ready = sem("stackT_ready")
        m_ps = sem("m_ps")
        m_seen = sem("m_seen")
        topT_ps = sem("topT_ps")
        toprow_ready = sem("toprow_ready")
        row_in = [sem(f"row_in{half}") for half in range(2)]
        sc_ps = sem("sc_ps")
        sc_exp = sem("sc_exp")
        sc_masked = sem("sc_masked")
        o_ps = sem("o_ps")
        den_turned = sem("den_turned")
        rden_ready = sem("rden_ready")
        rden_turned = sem("rden_turned")
        oT_ready = sem("oT_ready")
        kones_ready = sem("kones_ready")
        shift_ready = sem("shift_ready")
        scale_ready = sem("scale_ready")
        hi2_ready = sem("hi2_ready")
        xr_ready = sem("xr_ready")
        oh_ready = sem("oh_ready")
        y_ps = sem("y_ps")
        y_ready = sem("y_ready")
        xr_in = [sem(f"xr_in{i}") for i in range(SLOTS)]
        out_done = [sem(f"out_done{i}") for i in range(SLOTS)]

        def wait(eng, semaphore, value):
            if not isinstance(value, int) or value > 0:
                eng.wait_ge(semaphore, value)

        passed = {e.engine: sem(f"passed_{n}") for n, e in (("sync", nc.sync), ("gpsimd", nc.gpsimd), ("vector", nc.vector))}

        def wait_apart(eng, semaphore, value):
            if isinstance(value, int):
                wait(eng, semaphore, value)
            else:
                eng.wait_ge(semaphore, value)
                eng.sem_inc(passed[eng.engine], 1)

        block = ctx.enter_context(nc.Block())

        @block.sync
        def _(sp):
            for half in range(2):
                tiles = slice(half * NT // 2, (half + 1) * NT // 2)
                sp.dma_start(x_all[:, tiles, :], x_v[0, :, tiles, :]).then_inc(x0_in[half], 16)
            sp.dma_start(arena[:, 0:C_TRI], const_d[:, 0:C_TRI]).then_inc(consts_in, 16)
            sp.dma_start(cst1, const_d[:, C_TRI:C_W]).then_inc(consts1_in, 16)
            sp.dma_start(wr_b, wr_d.partition_broadcast(P)).then_inc(consts1_in, 16)
            with sp.Fori(1, B) as b:
                sp.dma_start(x_all[:, bass.ds(b * NT, NT), :], x_v[bass.ds(b, 1), :, :, :].rearrange("b p t d -> p (b t) d")).then_inc(x_in, 16)
                wait_apart(sp, x_in, b * 16)
            def load_proj(n, u):
                for dst, src in ((wq_s, wq_v), (wk_s, wk_v), (wv_s, wv_v)):
                    sp.dma_start(dst[u], src[bass.ds(n, 1), :, :, :].rearrange("n p k c -> p (n k) c")).then_inc((w2_in0, w2_in1)[u], 16)

            def load_wo(n, u):
                sp.dma_start(wo_s[u], wo_v[bass.ds(n, 1), :, :, :].rearrange("n p r d -> p (n r) d")).then_inc(wo_in[u], 16)

            for u in range(2):
                load_proj(u, u)
                load_wo(u, u)
            sp.dma_start(bias_rows[0:FH, :], bq_d.rearrange("(h d) -> h d", d=FD)).then_inc(f_const_in, 16)
            sp.dma_start(bias_rows[FH:FH + FKV, :], bk_d.rearrange("(h d) -> h d", d=FD)).then_inc(f_const_in, 16)
            sp.dma_start(bv_b, bv_d.partition_broadcast(P)).then_inc(f_const_in, 16)
            sp.dma_start(ln1_b, ln1_d.partition_broadcast(P)).then_inc(f_const_in, 16)
            sp.dma_start(ln2_b, ln2_d.partition_broadcast(P)).then_inc(f_const_in, 16)
            with sp.Fori(1, FKV // 2) as i:
                for u in range(2):
                    sp.wait_ge(w2_lo, i * 6 + u * 3 - 3)
                    load_proj(i * 2 + u, u)
                    sp.wait_ge(wo_ps, i * (2 * ST) + (u - 1) * ST + 1)
                    load_wo(i * 2 + u, u)

            def load_mlp(n, u):
                filled = (wm_in0, wm_in1)[u]
                for dst, src in ((wg_s, wg_v), (wu_s, wu_v)):
                    sp.dma_start(dst[u], src[bass.ds(n, 1), :, :, :].rearrange("n p k c -> p (n k) c")).then_inc(filled, 16)
                if not isinstance(n, int):
                    sp.wait_ge(wd_lo, n - 1)
                sp.dma_start(wd_s[u], wd_v[bass.ds(n, 1), :, :].rearrange("n p c -> p (n c)")).then_inc(filled, 16)

            sp.wait_ge(pT2_ready, FKV * REP * ST)
            sp.wait_ge(o2_ps, FKV * REP + 1)
            for u in range(2):
                load_mlp(u, u)
            sp.dma_start(w_out, wout_v).then_inc(late_in, 16)
            sp.wait_ge(wo_ps, FKV * ST + 1)
            sp.dma_start(w_qkv, wqkv_v).then_inc(late_in, 16)
            with sp.Fori(1, NC // 2) as i:
                for u in range(2):
                    sp.wait_ge(gu_lo, i * 4 + 2 * u - 2)
                    load_mlp(i * 2 + u, u)
            sp.wait_ge(hT_ps, 2 * ST)
            sp.dma_start(xn, x_v[0, :, :, :]).then_inc(xb_in, 16)

            def batch(b, first):
                sp.wait_ge(xnT_ps, b * NT + NT)
                nb = (b + 1) % B
                sp.dma_start(xn, x_v[bass.ds(nb, 1), :, :, :].rearrange("b p t d -> p (b t) d")).then_inc(xb_in, 16)
                if not first:
                    sp.wait_ge(v_ps, b * NT + NT)
                    outputs(b - 1, True)
                else:
                    rows(b, 0, 0)
                for p in range(NP):
                    for half in range(2):
                        if p or half:
                            rows(b, p, half)

            def rows(b, p, half):
                sp.wait_ge(toprow_ready, (b * NP + p) * 2 + half + 1)
                sp.dma_start(qS[p % 2][RH:RH + 1, half, :].bitcast(f32), top_rows[0:NT, half, :]).then_inc(row_in[half], 16)

            def outputs(b, more):
                for i in range(SLOTS):
                    sp.dma_start(xr[:, 2 * i:2 * i + 2, :], x_v[bass.ds(b, 1), :, 2 * i:2 * i + 2, :].rearrange("b p t d -> p (b t) d")).then_inc(xr_in[i], 16)
                for i in range(SLOTS):
                    sp.wait_ge(y_ready, b * NT + 2 * i + 2)
                    sp.dma_start(out_v[bass.ds(b, 1), :, 2 * i:2 * i + 2, :].rearrange("b p t d -> p (b t) d"), xr[:, 2 * i:2 * i + 2, :]).then_inc(out_done[i], 16)
                    if i == SLOTS - 2 and more:
                        rows(b + 1, 0, 0)

            batch(0, True)
            with sp.Fori(1, B) as b:
                batch(b, False)
            sp.wait_ge(o_ps, B * NP * NS)
            outputs(B - 1, False)
            sp.wait_ge(xb_in, 16 * (B + 1))
            for i in range(SLOTS):
                sp.wait_ge(out_done[i], B * 16)

        @block.gpsimd
        def _(pool):
            for started in (p1_mean,):
                pool.sem_inc(started, 1)
            pool.memset(half_neg, -0.5).then_inc(init_done, 1)
            pool.dma_start(gam[:, 0, :], qg_d.partition_broadcast(P)).then_inc(gam_ready, 16)
            pool.dma_start(gam[:, 1, :], kg_d.partition_broadcast(P)).then_inc(gam_ready, 16)
            pool.dma_start(rope_raw, rope_d.rearrange("(t p) c -> p t c", p=P)).then_inc(gam_ready, 16)
            pool.dma_start(tab[:, :, 0:FT_W], frope_d.rearrange("(t p) c -> p t c", p=P)).then_inc(p1_tab, 16)
            pool.wait_ge(init_done, 1)
            with pool.Fori(0, B) as b:
                wait_apart(pool, p1_stats, b * 2 * NT + 2 * NT)
                pool.tensor_scalar(vpe, mv[:, :, 1], LN_EPS, None, ALU.add).then_inc(p1_vpe, 1)
                pool.wait_ge(p1_vpe, b + 1)
                pool.tensor_tensor(rstd1, vpe, half_neg[:, 0:NT], ALU.pow).then_inc(p1_rstd, 1)
                wait_apart(pool, p1_rstd, b + 1)
                pool.tensor_copy(ln_mean[:, bass.ds(b, 1), :].rearrange("p b t -> p (b t)"), mv[:, :, 0]).then_inc(p1_mean, 1)
                pool.tensor_copy(ln_rstd[:, bass.ds(b, 1), :].rearrange("p b t -> p (b t)"), rstd1).then_inc(p1_mean, 1)
            pool.wait_ge(gam_ready, 48)
            for w in range(2):
                g = gam[:, w, :]
                gb = g.unsqueeze(1).to_broadcast([P, NT, AD])
                scale = AD ** -0.5 if w == 0 else 1.0
                pool.tensor_tensor(cosG[:, :, w, :], rope_raw[:, :, 0:AD], gb, ALU.mult).then_inc(rope_ready, 1)
                for h in range(2):
                    o = h * (AD // 2)
                    gr = g[:, AD // 2 - o:AD - o].unsqueeze(1).to_broadcast([P, NT, AD // 2])
                    last = pool.tensor_tensor(sinG[:, :, w, o:o + AD // 2], rope_raw[:, :, AD + o:AD + o + AD // 2], gr, ALU.mult)
                last.then_inc(rope_ready, 1)
            pool.wait_ge(rope_ready, 4)
            pool.tensor_scalar(cosG[:, :, 0, :], cosG[:, :, 0, :], AD ** -0.5, None, ALU.mult)
            pool.tensor_scalar(sinG[:, :, 0, :], sinG[:, :, 0, :], AD ** -0.5, None, ALU.mult).then_inc(rope_ready, 1)
            def inverse_rms2(n):
                pool.wait_ge(ss2_ready, ST * (n + 1))
                pool.tensor_scalar(ms2, ss2, 1.0 / D, RMS_EPS, ALU.mult, ALU.add).then_inc(ms2_ready, 1)
                pool.wait_ge(ms2_ready, n + 1)
                pool.tensor_tensor(rs2, ms2, half_neg[:, 0:ST], ALU.pow).then_inc(rs2_ready, 1)

            inverse_rms2(0)
            with pool.Fori(0, FKV // 2) as i:
                for u in range(2):
                    for w, (dst, src) in enumerate(((wqS, wq_s), (wkS, wk_s), (wvS, wv_s))):
                        wait_apart(pool, w2_hi, i * 6 + u * 3 + w + 1)
                        pool.tensor_tensor(dst[1], src[u], dst[0].bitcast(f32), ALU.subtract).then_inc(w2_lo, 1)
            inverse_rms2(1)
            def gu_low(n, u):
                for w, raw_w in enumerate((wg_s, wu_s)):
                    wait_apart(pool, gu_hi, 2 * n + w + 1)
                    pool.tensor_tensor(wguS[u][:, w, 1], raw_w[u], wguS[u][:, w, 0].bitcast(f32), ALU.subtract).then_inc(gu_lo, 1)

            def wd_low(n, u):
                wait_apart(pool, wd_hi, n + 1)
                pool.tensor_tensor(wdS[u][:, 1], wd_s[u], wdS[u][:, 0].bitcast(f32), ALU.subtract).then_inc(wd_lo, 1)

            gu_low(0, 0)
            gu_low(1, 1)
            wd_low(0, 0)
            with pool.Fori(0, NC // 2 - 1) as i:
                for u in range(2):
                    gu_low(i * 2 + u + 2, u)
                    wd_low(i * 2 + u + 1, 1 - u)
            wd_low(NC - 1, 1)
            pool.wait_ge(mlp_ps, 1)
            for i in range(2):
                pool.memset(kS[i][RH:RH + 1, :, :].bitcast(f32), 1.0).then_inc(kones_ready, 1)
                pool.wait_ge(kones_ready, i + 1)
            pool.wait_ge(delta_done, ST)
            qk4 = qk.rearrange("p (w h d) -> p w h d", w=2, d=AD)
            rot4 = rot.rearrange("p (w h d) -> p w h d", w=2, d=AD)

            def outputs(b):
                mean = ln_mean[:, bass.ds(b, 1), :].rearrange("p b t -> p (b t)")
                rstd = ln_rstd[:, bass.ds(b, 1), :].rearrange("p b t -> p (b t)")
                pool.tensor_tensor(out_shift, mean, rstd, ALU.mult).then_inc(shift_ready, 1)
                pool.tensor_copy(out_scale, rstd).then_inc(scale_ready, 1)
                wait_apart(pool, scale_ready, b * 2 + 1)
                wait_apart(pool, shift_ready, b * 2 + 1)
                pool.tensor_scalar(out_scale, out_scale, 1.0, None, ALU.add).then_inc(scale_ready, 1)
                pool.tensor_scalar(out_shift, out_shift, -1.0, None, ALU.mult).then_inc(shift_ready, 1)

            def build(b, p):
                q = b * NP + p
                wait_apart(pool, stackT_ps, q * 8)
                if p == 0:
                    wait_apart(pool, roped_ready, b * NT + NT)
                for w in range(1 if p == 0 else 2):
                    src = roped[:, :, w * D + p * 2 * AD:w * D + (p + 1) * 2 * AD].rearrange("p t (h d) -> p t h d", h=2)
                    st = stack[:, w].rearrange("p t (h c) -> p t h c", h=2)
                    lo = 2 * AD if w else AD
                    for h in range(2):
                        pool.tensor_copy(st[:, :, h, 0:AD], src[:, :, h]).then_inc(hi_ready[w], 1)
                    wait_apart(pool, hi_ready[w], q * 2 + 2)
                    for h in range(2):
                        last = pool.tensor_tensor(st[:, :, h, lo:lo + AD], src[:, :, h], st[:, :, h, 0:AD].bitcast(f32), ALU.subtract)
                    last.then_inc(lo_ready[w], 1)

            def batch(b, first):
                if not first:
                    outputs(b - 1)
                def inverse_rms(t):
                    k = b * NT + t + 1
                    wait_apart(pool, ss3_ready, k)
                    if t >= 1:
                        wait_apart(pool, rs3_ready, k - 1)
                    if t >= 2:
                        wait_apart(pool, scaled, k - 2)
                    pool.tensor_scalar(ms3, ss3, 1.0 / AD, RMS_EPS, ALU.mult, ALU.add).then_inc(ms3_ready, 1)
                    pool.wait_ge(ms3_ready, k)
                    pool.tensor_tensor(rs3[:, t % 2, :], ms3, half_neg, ALU.pow).then_inc(rs3_ready, 1)

                inverse_rms(0)
                for t in range(NT):
                    k = b * NT + t + 1
                    if t + 1 < NT:
                        inverse_rms(t + 1)
                    pool.wait_ge(scaled, k)
                    wait(pool, roped_ready, k - 1)
                    for h in range(2):
                        o = h * (AD // 2)
                        sn = sinG[:, t, 0, o:o + AD // 2].unsqueeze(1).to_broadcast([P, AH, AD // 2])
                        last = pool.tensor_tensor(rot4[:, 0, :, o:o + AD // 2], qk4[:, 0, :, AD // 2 - o:AD - o], sn, ALU.mult)
                    last.then_inc(rotated, 1)
                build(b, 0)
                build(b, 1)
                for p in range(NP):
                    for n, (c, j) in enumerate(STEPS):
                        if j >= 4 * c:
                            k = p * NS + n
                            wait_apart(pool, sc_exp, 2 * (b * NP * NS + k + 1))
                            blk = probT[:, k % SLOTS, :, (j - 4 * c) * P:(j - 4 * c + 1) * P]
                            pool.affine_select(out=blk, in_=blk, compare_op=ALU.is_ge, fill=0.0, base=0,
                                               pattern=[[0, 2], [1, P]], channel_multiplier=-1).then_inc(sc_masked, 1)
                        if n == BUILD_STEP and p + 2 < NP:
                            build(b, p + 2)

            batch(0, True)
            with pool.Fori(1, B) as b:
                batch(b, False)
            outputs(B - 1)

        @block.scalar
        def _(act):
            def out_pT(n, m):
                h, t = m // ST, m % ST
                act.wait_ge(pT2_ps, n * 8 + m + 1 + 1)
                act.activation(probT2[h][:, 0:t + 1, t * P:(t + 1) * P],
                               psum[:, 4 + m % 2, 0:(t + 1) * P].rearrange("p (j n) -> p j n", n=P), ACT.Copy).then_inc(pT2_ready, 1)

            for started in (p1_gathered, proj_out):
                act.sem_inc(started, 1)
            def score_row(b):
                act.wait_ge(p1_row_ps, b + 1)
                act.activation(s_row, psum[:, 0:2, :].rearrange("p a n -> p (a n)"), ACT.Copy).then_inc(p1_row, 1)

            def gathered(b, last):
                act.wait_ge(p1_gather_ps, b * 3 + 1)
                act.activation(xsel[:, bass.ds(b, 1), :].rearrange("p b d -> p (b d)"), psum[:, 3, :], ACT.Copy).then_inc(p1_gathered, 1)
                if not last:
                    score_row(b + 1)
                act.wait_ge(p1_gather_ps, b * 3 + 2)
                act.activation(tabsel[:, bass.ds(b, 1), :].rearrange("p b d -> p (b d)"), psum[:, 4, 0:FT_W + 1], ACT.Copy).then_inc(p1_gathered, 1)
                act.wait_ge(p1_gather_ps, b * 3 + 3)
                act.activation(onehotT[:, bass.ds(b, 1), :].rearrange("p b t -> p (b t)"),
                               psum[:, 5:7, :].rearrange("p a n -> p (a n)"), ACT.Copy).then_inc(p1_gathered, 1)

            score_row(0)
            with act.Fori(0, B - 1) as b:
                gathered(b, False)
            gathered(B - 1, True)
            act.wait_ge(p1_gathered, 3 * B + 1)
            act.activation(egate, tabsel[:, :, FT_W], ACT.Exp, scale=-1.0).then_inc(gate_1, 1)

            def turn_h(n):
                for t in range(ST):
                    act.wait_ge(hT_ps, n * ST + t + 1)
                    act.activation(hS[0][:, :, t * P:(t + 1) * P], psum[:, t, :].rearrange("p (k n) -> p k n", k=KD), ACT.Copy).then_inc(hT_ready, 1)

            turn_h(0)
            act.wait_ge(tabT_ps, 1)
            act.activation(cosT, psum[:, 4, :], ACT.Copy).then_inc(tabT_ready, 1)
            act.activation(sinT, psum[:, 5, :], ACT.Copy).then_inc(tabT_ready, 1)
            act.wait_ge(bias_ps, 1)
            act.activation(biasT, psum[:, 6, 0:FH + FKV], ACT.Copy).then_inc(biasT_ready, 1)
            act.wait_ge(biasT_ready, 1)
            def w2_high(n, u, loads):
                act.wait_ge((w2_in0, w2_in1)[u], loads * 48)
                for dst, src, used in ((wqS, wq_s, REP), (wkS, wk_s, REP + 1), (wvS, wv_s, REP + 2)):
                    wait(act, proj_ps, (n - 1) * 4 + used)
                    act.activation(dst[0], src[u], ACT.Copy).then_inc(w2_hi, 1)

            def project(n, r):
                act.wait_ge(proj_ps, n * 4 + r + 1)
                if r == 0:
                    act.wait_ge(rope_done, n * 3 + 1)
                if r == 2:
                    act.wait_ge(rope_done, n * 3 + 1 + 1)
                bcol = biasT[:, bass.ds(n * REP + r, 1)] if r < REP else biasT[:, bass.ds(n + FH, 1)]
                act.activation(raw[:, r % 2, :], psum[:, r % 2, :], ACT.Identity, bias=bcol).then_inc(proj_out, 1)

            def heads(i, last):
                for u in range(2):
                    n = i * 2 + u
                    for m in range(REP * ST):
                        w = (m % ST + 1) * P
                        act.wait_ge(s2_low, n * 8 + m + 1)
                        act.activation(prob2[:, m, 0:w], prob2[:, m, 0:w], ACT.Exp, bias=nmax2[:, m:m + 1], scale=-1.0,
                                       accum_out=den2[:, m:m + 1]).then_inc(s2_exp, 1)
                        if m >= 2:
                            out_pT(n, m - 2)
                        if m in PROJECT_OUT and not (last and u):
                            project(n + 1, PROJECT_OUT.index(m))
                    out_pT(n, 6)
                    out_pT(n, 7)
                    if not last:
                        w2_high(n + 2, u, i + 2)

            w2_high(0, 0, 1)
            for r in range(REP + 1):
                project(0, r)
            w2_high(1, 1, 1)
            with act.Fori(0, FKV // 2 - 1) as i:
                heads(i, False)
            heads(FKV // 2 - 1, True)
            turn_h(1)
            def gu_high(n, u, loads):
                if isinstance(n, int):
                    act.wait_ge(proj_ps, FKV * 4)
                act.wait_ge((wm_in0, wm_in1)[u], loads * 48)
                if not isinstance(n, int):
                    act.wait_ge(gu_ps, 2 * n - 2)
                for w, raw_w in enumerate((wg_s, wu_s)):
                    act.activation(wguS[u][:, w, 0], raw_w[u], ACT.Copy).then_inc(gu_hi, 1)

            def wd_high(n, u):
                act.wait_ge(wm_free, n)
                act.activation(wdS[u][:, 0], wd_s[u], ACT.Copy).then_inc(wd_hi, 1)

            def expo(n, u):
                act.wait_ge(gu_ps, 2 * n + 1)
                act.wait_ge(sg_3, n + 1 - u)
                act.activation(eg[:, u, :], psum[:, 2 * u, :], ACT.Exp, scale=-1.0).then_inc(eg_ready, 1)

            gu_high(0, 0, 1)
            gu_high(1, 1, 1)
            act.activation(wdS[0][:, 0], wd_s[0], ACT.Copy).then_inc(wd_hi, 1)
            with act.Fori(0, NC // 2 - 1) as i:
                for u in range(2):
                    expo(i * 2 + u, u)
                    gu_high(i * 2 + u + 2, u, i + 2)
                    wd_high(i * 2 + u + 1, 1 - u)
            expo(NC - 2, 0)
            wd_high(NC - 1, 1)
            expo(NC - 1, 1)
            act.wait_ge(delta_b, ST)
            act.activation(ident_r[:, :], ident, ACT.Copy).then_inc(ident_ready, 1)
            sq = psum[:, 6:8, :].rearrange("p a n -> p (a n)")

            def user(b, p, kind, arg):
                q = b * NP + p
                bank = BANK[USERS.index((kind, arg))]
                if kind == "turn":
                    w, h, half = arg
                    n = TURNS.index(arg)
                    if n == 0:
                        wait(act, sc_ps, 2 * (q - 1) * NS)
                        wait(act, m_ps, (q - 1) * len(PIECES))
                    act.wait_ge(stackT_ps, q * 8 + n + 1)
                    dst = kS[p % 2][0:RH, h, half * CH:(half + 1) * CH] if w else qS[p % 2][0:RH, half, h * CH:(h + 1) * CH]
                    act.activation(dst, psum[0:RH, bank, :], ACT.Copy).then_inc(stackT_ready, 1)
                if kind == "top":
                    act.wait_ge(topT_ps, q * 2 + arg + 1)
                    wait(act, row_in[arg], q * 16)
                    act.activation(top_rows[0:NT, arg, :].bitcast(f32r), psum[0:NT, bank, 0:P], ACT.Copy, scale=-1.0).then_inc(toprow_ready, 1)

            def repeat_hi(b, p, w):
                q = b * NP + p
                st = stack[:, w].rearrange("p t (h c) -> p t h c", h=2)
                act.wait_ge(hi_ready[w], q * 2 + 2)
                second = AD if w else 2 * AD
                for h in range(2):
                    last = act.activation(st[:, :, h, second:second + AD], st[:, :, h, 0:AD].bitcast(f32), ACT.Copy)
                last.then_inc(hi2_ready, 1)

            def copy_v(b, t):
                act.wait_ge(v_ps, b * NT + t + 1)
                act.activation(v[:, t, :], psum[:, 4 + t % 2, :], ACT.Copy).then_inc(v_ready, 1)

            def output(b, t, made):
                if t == 0:
                    act.wait_ge(roped_ready, made * NT)
                    act.activation(ohT, onehotT[:, bass.ds(b, 1), :].rearrange("p b t -> p (b t)"), ACT.Copy).then_inc(oh_ready, 1)
                    act.wait_ge(scale_ready, b * 2 + 2)
                    act.wait_ge(shift_ready, b * 2 + 2)
                act.wait_ge(xr_in[t // 2], b * 16 + 16)
                act.activation(xr[:, t, :], xr[:, t, :], ACT.Identity, bias=out_shift[:, t:t + 1],
                               scale=out_scale[:, t:t + 1]).then_inc(xr_ready, 1)

            def batch(b, first):
                wait(act, o_ps, b * NP * NS)
                for t in range(NT):
                    act.wait_ge(xnT_ps, b * NT + t + 1)
                    act.activation(xnT[:, :, t * P:(t + 1) * P], psum[:, 6 + t % 2, :].rearrange("p (k n) -> p k n", k=KD), ACT.Copy).then_inc(xnT_ready, 1)
                for t in range(NT):
                    a = 2 * (t % 2)
                    k = b * NT + t + 1
                    qkp = psum[:, a:a + 2, :].rearrange("p a n -> p (a n)")
                    act.wait_ge(qk_ps, k)
                    if t == 0:
                        act.wait_ge(xnT_ready, b * NT + NT)
                    wait(act, ss3_ready, k - 1)
                    act.activation(sq, qkp, ACT.Square).then_inc(qk_sq, 1)
                    for o in V_AFTER[t]:
                        copy_v(b, o)
                for t in range(NT):
                    if not first:
                        output(b - 1, t, b + 1)
                    if t == 0:
                        for w in range(2):
                            repeat_hi(b, 0, w)
                    for u in BESIDE_Y[t]:
                        user(b, 0, *u)
                    if t == BUILD_Y:
                        for w in range(2):
                            repeat_hi(b, 1, w)
                for p in range(NP):
                    for n, (c, j) in enumerate(STEPS):
                        k = p * NS + n
                        lo = max(0, j - 4 * c) * P
                        if k < SLOTS and not first:
                            act.wait_ge(out_done[k], b * 16)
                        if k >= SLOTS:
                            act.wait_ge(o_ps, b * NP * NS + k - SLOTS + 1)
                        for h in range(2):
                            act.wait_ge(sc_ps, 2 * (b * NP * NS + k) + h + 1)
                            act.activation(probT[:, k % SLOTS, h, lo:CH], psum[:, (2 * k + h) % 3, lo:CH], ACT.Exp).then_inc(sc_exp, 1)
                        for q, u in beside(p, n):
                            user(b, q, *u)
                        if p + 2 < NP and n in REPEAT_STEP:
                            repeat_hi(b, p + 2, REPEAT_STEP.index(n))

            batch(0, True)
            with act.Fori(1, B) as b:
                batch(b, False)
            for t in range(NT):
                output(B - 1, t, B)

        @block.tensor
        def _(pe):
            for started in (o2_ps, pT2_ps, s2_ps, wm_free, wo_ps,):
                pe.sem_inc(started, 1)
            pe.wait_ge(consts_in, 16)
            pe.wait_ge(consts1_in, 32)
            pe.wait_ge(p1_tab, 16)

            def score_row(b):
                pe.wait_ge(p1_score, b * NT + NT)
                for t in range(NT):
                    last = pe.transpose(psum[:, t // 4, (t % 4) * P:(t % 4 + 1) * P], s_col[:, t:t + 1].to_broadcast([P, P]), ident)
                last.then_inc(p1_row_ps, 1)

            def gather(b, last_batch):
                pe.wait_ge(p1_chosen, b + 1)
                pe.matmul(psum[:, 2, 0:NT], tri, chosen, start=True, stop=False)
                for k in range(1, NT):
                    last = pe.matmul(psum[:, 2, k:NT], ones, chosen[:, 0:NT - k], start=False, stop=(k == NT - 1))
                last.then_inc(p1_pos, 1)
                pe.wait_ge(p1_onehot, b + 1)
                pe.wait_ge(p1_gathered, b * 3 + 1)
                for t in range(NT):
                    last = pe.matmul(psum[:, 3, :], onehot[:, t, :], x_all[:, bass.ds(b * NT + t, 1), :].rearrange("p b d -> p (b d)"), start=(t == 0), stop=(t == NT - 1))
                last.then_inc(p1_gather_ps, 1)
                if not last_batch:
                    score_row(b + 1)
                for t in range(NT):
                    last = pe.matmul(psum[:, 4, 0:FT_W + 1], onehot[:, t, :], tab[:, t, :], start=(t == 0), stop=(t == NT - 1))
                last.then_inc(p1_gather_ps, 1)
                for t in range(NT):
                    last = pe.transpose(psum[:, 5 + t // 4, (t % 4) * P:(t % 4 + 1) * P], onehot[:, t, :], ident)
                last.then_inc(p1_gather_ps, 1)

            score_row(0)
            with pe.Fori(0, B - 1) as b:
                gather(b, False)
            gather(B - 1, True)

            def turn_h(n):
                for t in range(ST):
                    pe.wait_ge(h_ready, n * ST + t + 1)
                    for k in range(KD):
                        last = pe.transpose(psum[:, t, k * P:(k + 1) * P], hn[:, t, k * P:(k + 1) * P], ident)
                    last.then_inc(hT_ps, 1)

            pe.wait_ge(p1_gathered, 3 * B + 1)
            turn_h(0)
            for w in range(2):
                for t in range(ST):
                    last = pe.transpose(psum[:, 4 + w, t * P:(t + 1) * P], tabsel[:, t, w * FD:(w + 1) * FD], ident)
            last.then_inc(tabT_ps, 1)
            pe.wait_ge(f_const_in, 80)
            pe.transpose(psum[:, 6, 0:FH + FKV], bias_rows[0:FH + FKV, :], ident[0:FH + FKV, 0:FH + FKV]).then_inc(bias_ps, 1)
            pe.wait_ge(hT_ready, ST)
            pe.wait_ge(h_lo, ST)
            pe.wait_ge(tabT_ready, 2)
            pe.wait_ge(biasT_ready, 1)

            def project(n, r):
                if r == 0:
                    pe.wait_ge(proj_out, n * 3 + 1)
                if r == 1:
                    pe.wait_ge(v2_ready, n + 1)
                if r == 2:
                    pe.wait_ge(proj_out, n * 3 + 1 + 1)
                pe.wait_ge(w2_lo, n * 3 + (1 if r < REP else 2))
                for k in range(KD):
                    for a, c in PARTS:
                        w = wqS[a][:, k, r * FD:(r + 1) * FD] if r < REP else wkS[a][:, k, :]
                        last = pe.matmul(psum[:, r % 2, :], w, hS[c][:, k, :], start=(k == 0 and a + c == 0), stop=(k == KD - 1 and a == 1))
                last.then_inc(proj_ps, 1)

            def project_v2(n, tiles):
                pe.wait_ge(proj_out, n * 3 + 2 + 1)
                pe.wait_ge(w2_lo, n * 3 + 3)
                for t in tiles:
                    for k in range(KD):
                        for a, c in PARTS:
                            last = pe.matmul(psum[:, 1, t * P:(t + 1) * P], hS[a][:, k, t * P:(t + 1) * P], wvS[c][:, k, :],
                                             start=(k == 0 and a + c == 0), stop=(k == KD - 1 and a == 1))
                if t == ST - 1:
                    last.then_inc(proj_ps, 1)

            def heads(i, final):
                for u in range(2):
                    n = i * 2 + u
                    more = not (final and u)
                    pe.wait_ge(rope_done, n * 3 + 3 + 1)

                    def scores(m):
                        h, t = m // ST, m % ST
                        if m >= 2:
                            pe.wait_ge(s2_low, n * 8 + m - 1)
                        pe.matmul(psum[:, 2 + m % 2, 0:(t + 1) * P], qT2[u][:, h, t * P:(t + 1) * P], kT2[u][:, 0:(t + 1) * P],
                                  start=True, stop=True).then_inc(s2_ps, 1)

                    def turn(m):
                        t = m % ST
                        pe.wait_ge(s2_prob, n * 8 + m + 1)
                        if m >= 2:
                            pe.wait_ge(pT2_ready, n * 8 + m - 1)
                        for j in range(t + 1):
                            last = pe.transpose(psum[:, 4 + m % 2, j * P:(j + 1) * P], prob2[:, m, j * P:(j + 1) * P], ident)
                        last.then_inc(pT2_ps, 1)

                    def values(h):
                        pe.wait_ge(pT2_ready, n * 8 + (h + 1) * ST)
                        if h == 0:
                            pe.wait_ge(v2_ready, n + 1 + 1)
                            pe.wait_ge(x1_ready, n * ST + 1)
                        for j in range(ST):
                            last = pe.matmul(psum[:, 6 + h, j * P:S], v2[u][:, j, :], probT2[h][:, j, j * P:S], start=(j == 0), stop=(j == ST - 1))
                        last.then_inc(o2_ps, 1)

                    for m in range(REP * ST):
                        scores(m)
                        if m >= 3:
                            turn(m - 3)
                        if more and m in PROJECT:
                            project(n + 1, PROJECT.index(m))
                    if more:
                        project_v2(n + 1, range(ST))
                    for m in range(REP * ST - 3, REP * ST):
                        turn(m)
                    values(0)
                    values(1)
                    pe.wait_ge(o2_ready, n * REP + 2)
                    pe.wait_ge(wo_in[u], i * 16 + 16)
                    for t in range(ST):
                        if t >= 2:
                            pe.wait_ge(x1_ready, n * ST + t - 1 + 1)
                        for h in range(REP):
                            last = pe.matmul(psum[:, 7 - t % 2, :], oT2[:, h, t * P:(t + 1) * P], wo_s[u][:, h, :], start=(h == 0), stop=(h == REP - 1))
                        last.then_inc(wo_ps, 1)

            for r in range(REP + 1):
                project(0, r)
            project_v2(0, range(ST))
            with pe.Fori(0, FKV // 2 - 1) as i:
                heads(i, False)
            heads(FKV // 2 - 1, True)
            turn_h(1)
            pe.wait_ge(hT_ready, 2 * ST)
            pe.wait_ge(zero_ready, 1)
            for t in range(ST):
                pe.matmul(psum[:, 4 + t, :], zrow[:, 0:P], zrow, start=True, stop=False, skip_group_check=True)

            def gate_up(n, u):
                pe.wait_ge(gu_lo, 2 * n + 2)
                wait(pe, aT_made, n - 1)
                for w in range(2):
                    for k in range(KD):
                        for a, b in PARTS:
                            last = pe.matmul(psum[:, 2 * u + w, :], wguS[u][:, w, a, k, :], hS[b][:, k, :], start=(k == 0 and a + b == 0), stop=(k == KD - 1 and a == 1))
                    last.then_inc(gu_ps, 1)

            def down(n, u):
                pe.wait_ge(aT_ready, n + 1 + 1)
                pe.wait_ge(wd_lo, n + 1)
                for t in range(ST):
                    for a, b in PARTS:
                        last = pe.matmul(psum[:, 4 + t, :], aS[:, a, t * P:(t + 1) * P], wdS[u][:, b, :], start=False, stop=False, skip_group_check=True)
                last.then_inc(wm_free, 1)

            pe.wait_ge(h_lo, 2 * ST)
            gate_up(0, 0)
            gate_up(1, 1)
            down(0, 0)
            with pe.Fori(1, NC // 2) as i:
                gate_up(i * 2, 0)
                down(i * 2 - 1, 1)
                gate_up(i * 2 + 1, 1)
                down(i * 2, 0)
            down(NC - 1, 1)
            for t in range(ST):
                last = pe.matmul(psum[:, 4 + t, :], zrow[:, 0:P], zrow, start=False, stop=True, skip_group_check=True)
            last.then_inc(mlp_ps, 1)
            pe.wait_ge(late_in, 32)
            pe.wait_ge(ident_ready, 1)

            def freed(b, p, u):
                q = b * NP + p
                if u < 3 and p == 0:
                    pe.wait_ge(ss3_ready, b * NT + NT)
                    pe.wait_ge(v_ready, b * NT + NT)
                    return
                before = max(i for i in range(-len(USERS), u) if BANK[i] == BANK[u])
                kind, arg = USERS[before]
                if before < 0:
                    q = q - 1
                if kind == "turn":
                    wait(pe, stackT_ready, q * 8 + TURNS.index(arg) + 1)
                if kind == "max":
                    wait(pe, m_seen, q * len(PIECES) + PIECES.index(arg) + 1)
                if kind == "top":
                    wait(pe, toprow_ready, q * 2 + arg + 1)

            def user(b, p, kind, arg):
                q = b * NP + p
                u = USERS.index((kind, arg))
                bank = BANK[u]
                freed(b, p, u)
                if kind == "turn":
                    w, h, half = arg
                    pe.wait_ge(lo_ready[w], q + 1)
                    pe.wait_ge(hi2_ready, q * 2 + w + 1)
                    for i in range(CH // P):
                        t = half * (CH // P) + i
                        last = pe.transpose(psum[0:RH, bank, i * P:(i + 1) * P].bitcast(f32r), stack[:, w, t, h * STK:h * STK + RH], ident_r[:, :])
                    last.then_inc(stackT_ps, 1)
                if kind == "max":
                    t, c, h = arg
                    w = min(CH, (t + 1) * P - c * CH)
                    pe.wait_ge(stackT_ready, q * 8 + (4 if t < 4 else 8))
                    pe.matmul(psum[:, bank, 0:w], qS[p % 2][0:RH, t // 4, h * CH + t % 4 * P:h * CH + (t % 4 + 1) * P], kS[p % 2][0:RH, h, c * CH:c * CH + w],
                              start=True, stop=True).then_inc(m_ps, 1)
                if kind == "top":
                    pe.wait_ge(m_seen, q * len(PIECES) + (len(PIECES) if arg else NT))
                    pe.transpose(psum[0:NT, bank, 0:P], top[:, p % 2, arg * NT:(arg + 1) * NT], ident).then_inc(topT_ps, 1)

            def output(b, t, beside=()):
                if t == 0:
                    pe.wait_ge(oT_ready, b * 2 * NP + 2 * NP)
                if t >= 2:
                    pe.wait_ge(y_ready, b * NT + t - 1)
                elif not isinstance(b, int):
                    pe.wait_ge(v_ready, (b + 1) * NT + NT)
                    pe.wait_ge(scaled, (b + 1) * NT + NT)
                bank = psum[:, 3 + t % 2, :]
                for g in range(NG):
                    pe.matmul(bank, oT[:, g, t * P:(t + 1) * P], w_out[:, g, :], start=(g == 0), stop=False)
                    for u in beside[g:g + 1]:
                        user(b + 1, 0, *u)
                if t == 0:
                    pe.wait_ge(oh_ready, b + 1)
                pe.matmul(bank, ohT[:, t * P:(t + 1) * P], delta[:, bass.ds(b, 1), :].rearrange("p b d -> p (b d)"), start=False, stop=True).then_inc(y_ps, 1)
                for u in beside[NG:]:
                    user(b + 1, 0, *u)

            def score(b, p, n):
                c, j = STEPS[n]
                lo = max(0, j - 4 * c) * P
                k = p * NS + n
                if j == 0:
                    pe.wait_ge(row_in[c], (b * NP + p + 1) * 16)
                for h in range(2):
                    m = 2 * k + h
                    if m >= 3:
                        pe.wait_ge(sc_exp, 2 * b * NP * NS + m - 2)
                    else:
                        pe.wait_ge(scaled, b * NT + NT)
                    pe.matmul(psum[:, m % 3, lo:CH], kS[p % 2][0:RH + 1, h, j * P:(j + 1) * P],
                                     qS[p % 2][0:RH + 1, c, h * CH + lo:(h + 1) * CH], start=True, stop=True).then_inc(sc_ps, 1)

            def value(b, p, n):
                c, j = STEPS[n]
                lo = max(0, j - 4 * c) * P
                k = p * NS + n
                if j >= 4 * c:
                    pe.wait_ge(sc_masked, b * NP * 8 + p * 8 + j + 1)
                else:
                    pe.wait_ge(sc_exp, 2 * (b * NP * NS + k + 1))
                if j == 0:
                    m = b * 2 * NP + 2 * p + c
                    if p == 0:
                        pe.wait_ge(v_ready, b * NT + NT)
                        wait(pe, y_ready, b * NT)
                    else:
                        pe.wait_ge(oT_ready, m - 1)
                bank = 3 + c
                for r in range(4):
                    h = r % 2
                    w = v[:, j, (p * 2 + h) * AD:(p * 2 + h + 1) * AD] if r < 2 else ones[:, 0:AD]
                    last = pe.matmul(psum[AD * r:AD * (r + 1), bank, lo:CH], w, probT[:, k % SLOTS, h, lo:CH],
                                     start=(j == 0), stop=(j == 4 * c + 3))
                last.then_inc(o_ps, 1)

            def batch(b, first):
                for t in range(NT):
                    pe.wait_ge(xn_ready, b * NT + t + 1)
                    if t >= 2:
                        pe.wait_ge(xnT_ready, b * NT + t - 1)
                    else:
                        wait(pe, toprow_ready, b * NP * 2)
                    for k in range(KD):
                        last = pe.transpose(psum[:, 6 + t % 2, k * P:(k + 1) * P], xn[:, t, k * P:(k + 1) * P], ident)
                    last.then_inc(xnT_ps, 1)
                pe.wait_ge(xnT_ready, b * NT + NT)

                def project_v(t):
                    if t >= 2:
                        pe.wait_ge(v_ready, b * NT + t - 1)
                    else:
                        wait(pe, oT_ready, b * 2 * NP)
                    for k in range(KD):
                        last = pe.matmul(psum[:, 4 + t % 2, :], xnT[:, k, t * P:(t + 1) * P], w_qkv[:, k, 2 * D:3 * D], start=(k == 0), stop=(k == KD - 1))
                    last.then_inc(v_ps, 1)

                for t in range(NT):
                    if t >= 2:
                        pe.wait_ge(scaled, b * NT + t - 1)
                    else:
                        wait(pe, sc_exp, 2 * b * NP * NS)
                    if t == 1:
                        wait(pe, oT_ready, b * 2 * NP)
                    for w in range(2):
                        for k in range(KD):
                            last = pe.matmul(psum[:, 2 * (t % 2) + w, :], xnT[:, k, t * P:(t + 1) * P], w_qkv[:, k, w * D:(w + 1) * D], start=(k == 0), stop=(k == KD - 1))
                    last.then_inc(qk_ps, 1)
                    for o in V_AFTER[t]:
                        project_v(o)
                for t in range(NT):
                    if not first:
                        output(b - 1, t, BESIDE_Y[t])
                    else:
                        for u in BESIDE_Y[t]:
                            user(b, 0, *u)
                if first:
                    pe.wait_ge(kones_ready, 2)
                for p in range(NP):
                    for n in range(NS):
                        score(b, p, n)
                        users = beside(p, n)
                        for q, u in users[:len(users) // 2]:
                            user(b, q, *u)
                        if p * NS + n >= 2:
                            value(b, *divmod(p * NS + n - 2, NS))
                        for q, u in users[len(users) // 2:]:
                            user(b, q, *u)
                value(b, NP - 1, NS - 2)
                value(b, NP - 1, NS - 1)

            batch(0, True)
            pe.wait_ge(delta_done, ST)
            with pe.Fori(1, B) as b:
                batch(b, False)
            for t in range(NT):
                output(B - 1, t)

        @block.vector
        def _(dve):
            for started in (rope_done, sg_3, aT_ready, v2_ready, x1_ready,):
                dve.sem_inc(started, 1)
            dve.memset(earlier[:, 0:1], 0.0)

            def tile_x(b, t):
                return x_all[:, bass.ds(b * NT + t, 1), :].rearrange("p b d -> p (b d)")

            def tile_stats(b, tiles, arrived, count):
                dve.wait_ge(arrived, count)
                for t in tiles:
                    dve.bn_stats(stats[:, t, :], tile_x(b, t)).then_inc(p1_stats, 1)

            def joined_stats(b):
                wait_apart(dve, p1_stats, b * 2 * NT + NT)
                wait_apart(dve, p1_mean, b * 2 + 1)
                for t in range(NT):
                    dve.bn_aggr(mv[:, t, :], stats[:, t, :]).then_inc(p1_stats, 1)

            def select(b, last):
                dve.wait_ge(p1_rstd, b + 1)
                for t in range(NT):
                    dve.tensor_scalar(tile_x(b, t), tile_x(b, t), mv[:, t, 0:1], rstd1[:, t:t + 1], ALU.subtract, ALU.mult).then_inc(p1_norm, 1)
                for t in range(NT):
                    wait_apart(dve, p1_norm, b * NT + t + 1)
                    if t >= 2:
                        wait_apart(dve, p1_score, b * NT + t - 1)
                    dve.scalar_tensor_tensor(out=s_row[:, (t % 2) * D:(t % 2 + 1) * D], in0=tile_x(b, t), scalar=1.0, in1=wr_b,
                                             op0=ALU.mult, op1=ALU.mult, accum_out=s_col[:, t:t + 1]).then_inc(p1_score, 1)
                if not last:
                    tile_stats(b + 1, range(NT - 3), x_in, b * 16 + 16)
                dve.wait_ge(p1_row, b + 1)
                for t in range(NT):
                    own = slice(t * P, (t + 1) * P)
                    if t >= 1:
                        dve.wait_ge(p1_cnt, b * NT + t)
                        dve.tensor_scalar(junk1[:, 0, 0:t * P], s_row[:, 0:t * P], s_col[:, t:t + 1], 0.0, ALU.is_ge, ALU.add, accum_out=earlier[:, t:t + 1])
                    dve.tensor_scalar(junk1[:, 0, t * P:T], s_row[:, t * P:T], s_col[:, t:t + 1], 0.0, ALU.is_gt, ALU.add, accum_out=above[:, t:t + 1])
                    dve.scalar_tensor_tensor(out=junk1[:, 1, 0:P], in0=s_row[:, own], scalar=s_col[:, t:t + 1], in1=tie,
                                             op0=ALU.is_equal, op1=ALU.mult, accum_out=tied[:, t:t + 1]).then_inc(p1_cnt, 1)
                dve.wait_ge(p1_cnt, b * NT + NT)
                dve.tensor_tensor(rank, above, tied, ALU.add).then_inc(p1_rank, 1)
                dve.wait_ge(p1_rank, b * 2 + 1)
                dve.tensor_tensor(rank, rank, earlier, ALU.add).then_inc(p1_rank, 1)
                dve.wait_ge(p1_rank, b * 2 + 2)
                dve.tensor_scalar(chosen, rank, float(SEL), None, ALU.is_lt).then_inc(p1_chosen, 1)
                dve.wait_ge(p1_gathered, b * 3 + 1)
                dve.tensor_copy(tab[:, :, FT_W], s_col)
                if not last:
                    tile_stats(b + 1, range(NT - 3, NT), x_in, b * 16 + 16)
                    joined_stats(b + 1)
                dve.wait_ge(p1_pos, b + 1)
                dve.scalar_tensor_tensor(out=slot, in0=psum[:, 2, 0:NT], scalar=1.0, in1=chosen, op0=ALU.add, op1=ALU.mult).then_inc(p1_slot, 1)
                dve.wait_ge(p1_slot, b + 1)
                for t in range(NT):
                    chose = dve.tensor_scalar(onehot[:, t, :], iota1, slot[:, t:t + 1], None, ALU.is_equal)
                chose.then_inc(p1_onehot, 1)

            for half in range(2):
                tile_stats(0, range(half * NT // 2, (half + 1) * NT // 2), x0_in[half], 16)
            joined_stats(0)
            dve.wait_ge(consts1_in, 32)
            dve.wait_ge(p1_tab, 16)
            with dve.Fori(0, B - 1) as b:
                select(b, False)
            select(B - 1, True)

            def norm(src, w_b, n):
                for t in range(ST):
                    dve.tensor_tensor_reduce(hn[:, t, :], src[:, t, :], src[:, t, :], 1.0, 0.0, ALU.mult, ALU.add, ss2[:, t:t + 1]).then_inc(ss2_ready, 1)
                dve.wait_ge(rs2_ready, n + 1)
                for t in range(ST):
                    dve.scalar_tensor_tensor(out=hn[:, t, :], in0=src[:, t, :], scalar=rs2[:, t:t + 1], in1=w_b, op0=ALU.mult, op1=ALU.mult).then_inc(h_ready, 1)

            def low_h(n):
                for t in range(ST):
                    part = slice(t * P, (t + 1) * P)
                    dve.wait_ge(hT_ready, n * ST + t + 1)
                    dve.tensor_tensor(hS[1][:, :, part], psum[:, t, :].rearrange("p (k n) -> p k n", k=KD), hS[0][:, :, part].bitcast(f32), ALU.subtract).then_inc(h_lo, 1)

            dve.wait_ge(p1_gathered, 3 * B - 2 + 1)
            dve.wait_ge(f_const_in, 80)
            norm(xsel, ln1_b, 0)
            low_h(0)
            dve.wait_ge(gate_1, 1)
            dve.tensor_scalar(dgate, egate, 1.0, None, ALU.add).then_inc(gate_2, 1)
            dve.wait_ge(gate_2, 1)
            dve.reciprocal(gate, dgate)
            dve.tensor_copy(x1, xsel).then_inc(delta_a, 1)
            dve.wait_ge(tabT_ready, 2)
            dve.wait_ge(delta_a, 1)

            def rope(n, r, u):
                dst = qT2[u][:, r, :] if r < REP else kT2[u]
                half = FD // 2
                dve.wait_ge(proj_out, n * 3 + r + 1 + 1)
                dve.wait_ge(rope_done, n * 3 + r + 1)
                dve.tensor_tensor(rotd[0:half, :], raw[half:FD, r % 2, :], sinT[half:FD, :], ALU.mult).then_inc(rope_a, 1)
                dve.tensor_tensor(rotd[half:FD, :], raw[0:half, r % 2, :], sinT[0:half, :], ALU.mult).then_inc(rope_a, 1)
                if r == 0:
                    wait(dve, s2_ps, n * 8 - 8 + 1)
                dve.tensor_tensor(dst, raw[:, r % 2, :], cosT, ALU.mult).then_inc(rope_a, 1)
                dve.wait_ge(rope_a, n * 9 + 3 * r + 3)
                dve.tensor_tensor(dst, dst, rotd, ALU.add).then_inc(rope_done, 1)

            def bias_v(n, u):
                dve.wait_ge(proj_ps, n * 4 + 4)
                wait(dve, o2_ps, n * REP - REP + 1)
                dve.tensor_tensor(v2[u], psum[:, 1, :].rearrange("p (t d) -> p t d", d=FD),
                                  bv_b[:, bass.ds(n * FD, FD)].unsqueeze(1).to_broadcast([P, ST, FD]), ALU.add).then_inc(v2_ready, 1)

            def heads(i, final):
                for u in range(2):
                    n = i * 2 + u
                    more = not (final and u)

                    def normalise(m):
                        w = (m % ST + 1) * P
                        dve.wait_ge(s2_exp, n * 8 + m + 1)
                        dve.reciprocal(rden2[:, m:m + 1], den2[:, m:m + 1]).then_inc(s2_den, 1)
                        dve.wait_ge(s2_den, n * 8 + m + 1)
                        dve.tensor_scalar(prob2[:, m, 0:w], prob2[:, m, 0:w], rden2[:, m:m + 1], None, ALU.mult).then_inc(s2_prob, 1)

                    for m in range(REP * ST):
                        w = (m % ST + 1) * P
                        if m == 0:
                            wait_apart(dve, pT2_ps, n * 8 + 1)
                        wait_apart(dve, s2_ps, n * 8 + m + 1 + 1)
                        dve.tensor_tensor_reduce(prob2[:, m, 0:w], psum[:, 2 + m % 2, 0:w], mask[:, CH - w:CH], -(FD ** -0.5), 3e38,
                                                 ALU.add, ALU.min, nmax2[:, m:m + 1]).then_inc(s2_low, 1)
                        if m >= 1:
                            normalise(m - 1)
                        if more and m in ROPE:
                            rope(n + 1, ROPE.index(m), 1 - u)
                    normalise(REP * ST - 1)
                    if more:
                        bias_v(n + 1, 1 - u)
                    for h in range(REP):
                        dve.wait_ge(o2_ps, n * REP + h + 1 + 1)
                        if h == 0:
                            dve.wait_ge(wo_ps, n * ST + 1)
                        dve.tensor_copy(oT2[:, h, :], psum[:, 6 + h, :]).then_inc(o2_ready, 1)
                    for t in range(ST):
                        dve.wait_ge(wo_ps, n * ST + t + 1 + 1)
                        dve.tensor_tensor(x1[:, t, :], psum[:, 7 - t % 2, :], x1[:, t, :], ALU.add).then_inc(x1_ready, 1)

            for r in range(REP + 1):
                rope(0, r, 0)
            bias_v(0, 0)
            with dve.Fori(0, FKV // 2 - 1) as i:
                heads(i, False)
            heads(FKV // 2 - 1, True)
            dve.wait_ge(x1_ready, FKV * ST + 1)
            norm(x1, ln2_b, 1)
            low_h(1)
            dve.memset(zrow, 0.0).then_inc(zero_ready, 1)
            with dve.Fori(0, NC // 2) as i:
                for u in range(2):
                    n = i * 2 + u
                    dve.wait_ge(eg_ready, n + 1)
                    dve.tensor_scalar(sg[:, u, :], eg[:, u, :], 1.0, None, ALU.add).then_inc(sg_1, 1)
                    dve.wait_ge(sg_1, n + 1)
                    dve.reciprocal(eg[:, u, :], sg[:, u, :]).then_inc(sg_2, 1)
                    dve.wait_ge(sg_2, n + 1)
                    dve.tensor_tensor(sg[:, u, :], psum[:, 2 * u, :], eg[:, u, :], ALU.mult).then_inc(sg_3, 1)
                    dve.wait_ge(sg_3, n + 1 + 1)
                    dve.wait_ge(gu_ps, n * 2 + 2)
                    dve.tensor_tensor(aT[:, u, :], psum[:, 2 * u + 1, :], sg[:, u, :], ALU.mult).then_inc(aT_made, 1)
                    dve.wait_ge(aT_made, n + 1)
                    dve.wait_ge(wm_free, n + 1)
                    dve.tensor_copy(aS[:, 0, :], aT[:, u, :]).then_inc(aS_hi, 1)
                    dve.wait_ge(aS_hi, n + 1)
                    dve.tensor_tensor(aS[:, 1, :], aT[:, u, :], aS[:, 0, :].bitcast(f32), ALU.subtract).then_inc(aT_ready, 1)
            dve.wait_ge(mlp_ps, 1)
            for t in range(ST):
                dve.tensor_tensor(x1[:, t, :], psum[:, 4 + t, :], x1[:, t, :], ALU.add).then_inc(delta_a, 1)
            for t in range(ST):
                dve.wait_ge(delta_a, t + 2)
                dve.tensor_tensor(gain[:, t, :], x1[:, t, :], xsel[:, t, :], ALU.subtract).then_inc(delta_b, 1)

            def deltas():
                for t in range(ST):
                    dve.wait_ge(delta_b, t + 1)
                    dve.tensor_scalar(delta[:, t, :], gain[:, t, :], gate[:, t:t + 1], None, ALU.mult).then_inc(delta_done, 1)

            sq = psum[:, 6:8, :].rearrange("p a n -> p (a n)")
            qk3 = qk.rearrange("p (h d) -> p h d", d=AD)
            rot4 = rot.rearrange("p (w h d) -> p w h d", w=2, d=AD)
            qk4 = qk.rearrange("p (w h d) -> p w h d", w=2, d=AD)

            def norm_tile(b, t):
                nb = b % B
                if t == 0:
                    dve.wait_ge(xb_in, b * 16 + 16)
                dve.tensor_scalar(xn[:, t, :], xn[:, t, :], ln_mean[:, bass.ds(nb, 1), t], ln_rstd[:, bass.ds(nb, 1), t],
                                  ALU.subtract, ALU.mult).then_inc(xn_ready, 1)

            def user(b, p, kind, arg):
                if kind != "max":
                    return
                t, c, h = arg
                n = PIECES.index(arg)
                w = min(CH, (t + 1) * P - c * CH)
                q = b * NP + p
                bank = BANK[USERS.index((kind, arg))]
                past = past_top[:, 2 * (t % 2) + h:2 * (t % 2) + h + 1]
                diag = c == t // 4
                place = (t // 4) * NT + h * 4 + t % 4
                wait_apart(dve, m_ps, q * len(PIECES) + n + 1)
                if n == 0:
                    wait_apart(dve, topT_ps, (q - 1) * 2)
                if not diag:
                    dve.tensor_reduce(past, psum[:, bank, :], AX.X, ALU.max).then_inc(m_seen, 1)
                    return
                if c:
                    wait_apart(dve, m_seen, q * len(PIECES) + PIECES.index((t, c - 1, h)) + 1)
                dve.tensor_tensor_reduce(psum[:, bank, 0:w], psum[:, bank, 0:w], mask[:, CH - w:CH], 1.0,
                                         past if c else -3e38, ALU.add, ALU.max, top[:, p % 2, place:place + 1]).then_inc(m_seen, 1)

            def turn_sums(b, p, c):
                m = b * 2 * NP + 2 * p + c
                half = 2 * AD
                dve.wait_ge(o_ps, b * NP * NS + p * NS + (4 if c == 0 else NS))
                wait(dve, oT_ready, m)
                dve.transpose(rden[0:half, :], psum[half:P, 3 + c, :]).then_inc(den_turned, 1)

            def invert_sums(b, p, c):
                m = b * 2 * NP + 2 * p + c
                half = 2 * AD
                dve.wait_ge(den_turned, m + 1)
                dve.reciprocal(rden_t[0:half, :], rden[0:half, :].rearrange("p (g r) -> p g r", r=32)[:, :, 0]).then_inc(rden_ready, 1)
                dve.wait_ge(rden_ready, m + 1)
                dve.transpose(rden[0:half, :], rden_t[0:half, :].unsqueeze(2).to_broadcast([half, CH // 32, 32])).then_inc(rden_turned, 1)

            def divide(b, p, c):
                m = b * 2 * NP + 2 * p + c
                half = 2 * AD
                r = (p % 2) * half
                dve.wait_ge(rden_turned, m + 1)
                dve.tensor_tensor(oT[r:r + half, p // 2, c * CH:(c + 1) * CH], psum[0:half, 3 + c, :], rden[0:half, :], ALU.mult).then_inc(oT_ready, 1)

            def output(b, t):
                dve.wait_ge(y_ps, b * NT + t + 1)
                dve.wait_ge(xr_ready, b * NT + t + 1)
                dve.tensor_tensor(xr[:, t, :], psum[:, 3 + t % 2, :], xr[:, t, :], ALU.add).then_inc(y_ready, 1)

            def batch(b, first):
                def sums(t):
                    k = b * NT + t + 1
                    dve.wait_ge(qk_sq, k)
                    wait(dve, ms3_ready, k - 1)
                    dve.tensor_reduce(ss3, sq.rearrange("p (h d) -> p h d", d=AD), AX.X, ALU.add).then_inc(ss3_ready, 1)

                sums(0)
                for t in range(NT):
                    k = b * NT + t + 1
                    if t + 1 < NT:
                        sums(t + 1)
                    dve.wait_ge(rs3_ready, k)
                    wait(dve, rotated, k - 1)
                    wait(dve, cosed, k - 1)
                    qkp = psum[:, 2 * (t % 2):2 * (t % 2) + 2, :].rearrange("p a n -> p (a n)").rearrange("p (h d) -> p h d", d=AD)
                    dve.tensor_tensor(qk3, qkp, rs3[:, t % 2, :].unsqueeze(2).to_broadcast([P, 2 * AH, AD]), ALU.mult).then_inc(scaled, 1)
                    dve.wait_ge(scaled, k)
                    if t == 0:
                        for w in range(2):
                            wait(dve, lo_ready[w], b * NP)
                    tile = roped[:, t, :].rearrange("p (w h d) -> p w h d", w=2, d=AD)
                    for w in range(2):
                        dve.tensor_tensor(tile[:, w], qk4[:, w], cosG[:, t, w, :].unsqueeze(1).to_broadcast([P, AH, AD]), ALU.mult)
                    for h in range(2):
                        o = h * (AD // 2)
                        sn = sinG[:, t, 1, o:o + AD // 2].unsqueeze(1).to_broadcast([P, AH, AD // 2])
                        last = dve.tensor_tensor(rot4[:, 1, :, o:o + AD // 2], qk4[:, 1, :, AD // 2 - o:AD - o], sn, ALU.mult)
                    last.then_inc(cosed, 1)
                    dve.wait_ge(rotated, k)
                    dve.wait_ge(cosed, k)
                    dve.tensor_tensor(roped[:, t, :], roped[:, t, :], rot, ALU.add).then_inc(roped_ready, 1)
                src = roped[:, :, D:D + 2 * AD].rearrange("p t (h d) -> p t h d", h=2)
                st = stack[:, 1].rearrange("p t (h c) -> p t h c", h=2)
                wait(dve, stackT_ps, b * NP * 8)
                dve.wait_ge(roped_ready, b * NT + NT)
                for h in range(2):
                    dve.tensor_copy(st[:, :, h, 0:AD], src[:, :, h]).then_inc(hi_ready[1], 1)
                dve.wait_ge(hi_ready[1], b * NP * 2 + 2)
                for h in range(2):
                    last = dve.tensor_tensor(st[:, :, h, 2 * AD:3 * AD], src[:, :, h], st[:, :, h, 0:AD].bitcast(f32), ALU.subtract)
                last.then_inc(lo_ready[1], 1)
                for t in range(NT):
                    for u in BESIDE_Y[t]:
                        user(b, 0, *u)
                    if not first:
                        output(b - 1, t)
                for p in range(NP):
                    for n in range(NS):
                        for q, u in beside(p, n):
                            user(b, q, *u)
                        if n == 2 and p > 0:
                            turn_sums(b, p - 1, 1)
                        if n == 3 and p > 0:
                            invert_sums(b, p - 1, 1)
                        if n == 4 and p > 0:
                            divide(b, p - 1, 1)
                        if n == 9:
                            turn_sums(b, p, 0)
                        if n == 10:
                            invert_sums(b, p, 0)
                        if n == 11:
                            divide(b, p, 0)
                        if p == NP - 1 and 2 <= n < 2 + NT:
                            norm_tile(b + 1, n - 2)
                turn_sums(b, NP - 1, 1)
                invert_sums(b, NP - 1, 1)
                divide(b, NP - 1, 1)

            for t in range(NT):
                norm_tile(0, t)
            deltas()
            batch(0, True)
            with dve.Fori(1, B) as b:
                batch(b, False)
            for t in range(NT):
                output(B - 1, t)



STEPS = [(c, j) for c in range(T // CH) for j in range((c + 1) * CH // P)]
NS = len(STEPS)
TURNS = [(w, h, half) for half in range(2) for h in range(2) for w in range(2)]
PIECES = [(t, c, h) for t in range(NT) for c in range(t // 4 + 1) for h in range(2)]
_T, _M = [("turn", a) for a in TURNS], [("max", a) for a in PIECES]
USERS = (_T[:5] + _M[:2] + _T[5:6] + _M[2:4] + _T[6:7] + _M[4:6] + _T[7:] + _M[6:NT + 4] +
         [("top", 0)] + _M[NT + 4:] + [("top", 1)])


BANK = [5 + i % 3 for i in range(len(USERS) - 1)] + [6]


def dealt(counts):
    out, at = [], 0
    for n in counts:
        out.append(USERS[at:at + n])
        at += n
    return out


V_AFTER = [[], [0], [1], [2], [3], [4], [5], [6, 7]]
BESIDE_Y = dealt([0, 3, 5, 5, 5, 5, 5, 5])
BESIDE_STEP = dealt([1, 2, 3, 3, 4, 4, 4, 4, 4, 3, 1, 0])
LEFT_OVER = USERS[33:]


def beside(p, n):
    own = [(p, u) for u in LEFT_OVER] if n == 0 else []
    return own + ([(p + 1, u) for u in BESIDE_STEP[n]] if p + 1 < NP else [])


BUILD_Y = 6
BUILD_STEP = 3
REPEAT_STEP = (6, 8)

PROJECT, PROJECT_OUT, ROPE = (1, 3, 5), (2, 4, 6), (3, 5, 7)

_INS = ["L0_attn_x", "L0_attn_w_qkv", "L0_attn_w_out", "L0_attn_q_gamma", "L0_attn_k_gamma", "L0_ffn_w_router",
        "L0_ffn_wq", "L0_ffn_bq", "L0_ffn_wk", "L0_ffn_bk", "L0_ffn_wv", "L0_ffn_bv", "L0_ffn_wo",
        "L0_ffn_w_gate", "L0_ffn_w_up", "L0_ffn_w_down", "L0_ffn_ln1_w", "L0_ffn_ln2_w"]


def shape_constants():
    import numpy as np
    p = np.arange(P)[:, None]
    const = np.zeros((P, C_W), np.float32)
    const[:, C_ID:C_ID + P] = np.eye(P)
    const[:, C_ONE:C_ONE + P] = 1
    const[:, C_MASK + CH - P:C_MASK + CH] = np.where(np.arange(P)[None] <= p, 0, MASKED)
    const[:, C_TRI:C_TRI + P] = p < np.arange(P)[None]
    const[:, C_IOTA:C_IOTA + P] = np.arange(P)[None] + 1
    const[:, C_TIE:] = np.arange(P)[None] < p

    def angles(width):
        e = np.arange(0, width, 2, dtype=np.float32) / np.float32(width)
        inv = (np.float32(1) / np.power(np.float32(10000.0), e)).astype(np.float32)
        a = np.arange(T, dtype=np.float32)[:, None] * inv[None]
        return np.cos(a).astype(np.float32), np.sin(a).astype(np.float32)

    c, sn = angles(AD)
    rope = np.concatenate([c, c, -sn, sn], 1)
    c, sn = angles(FD)
    frope = np.concatenate([c, c, sn, -sn], 1)
    return {"const": const, "rope": rope, "frope": frope}


def kernel(**inputs):
    import numpy as _np
    import concourse.bacc as _bacc
    from concourse import mybir as _mybir
    from concourse.bass_utils import run_bass_kernel_spmd as _run

    nc = _bacc.Bacc("TRN2", target_bir_lowering=False, num_devices=1)
    arrays, args = {}, []
    given = {n: _np.ascontiguousarray(inputs[n]) for n in _INS}
    given.update(shape_constants())
    for name, a in given.items():
        arrays[f"in_{name}"] = a
        args.append(nc.dram_tensor(f"in_{name}", a.shape, _mybir.dt.from_np(a.dtype), kind="ExternalInput").ap())
    args.append(nc.dram_tensor("out_y", (B, T, D), _mybir.dt.float32, kind="ExternalOutput").ap())
    build(nc, *args)
    r = _run(nc, [arrays], core_ids=[0])
    return r.results[0]["out_y"]
```
